# Optimizing a Trainium2 kernel written in Bass

```python
import numpy as np
import jax
import jax.numpy as jnp

def _softmax(x, axis=-1):
    return jax.nn.softmax(x, axis=axis)

def _gelu(x):
    return jax.nn.gelu(x, approximate=True)

def _silu(x):
    return jax.nn.silu(x)

def _sigmoid(x):
    return jax.nn.sigmoid(x)

def _layernorm(x, axis=-1, eps=1e-05):
    m = jnp.mean(x, axis=axis, keepdims=True)
    v = jnp.var(x, axis=axis, keepdims=True)
    return (x - m) / jnp.sqrt(v + eps)

def _scatter_add(tgt, idx, src, axis=0):
    return tgt.at[idx].add(src)

def _segment_sum(src, seg, n):
    return jax.ops.segment_sum(src, seg, n)
kernel_name = 'mk_recurrent_d2_jaxref_r4_2f8faf'

def setup_inputs(seed: int=0):
    np.random.seed(seed)
    _w = jnp.asarray

    def _L0_attn_setup():
        import jax, jax.numpy as jnp
        import numpy as np
        D_MODEL = 256
        N_HEADS = 16
        HEAD_DIM = D_MODEL // N_HEADS
        WINDOW = 128
        LOCAL_BLOCK = 64
        LATENT_TOKENS = 64
        LATENT_D = 64
        LATENT_HEADS = 4
        LATENT_HD = LATENT_D // LATENT_HEADS
        NEG = -1000000000.0

        def _local_attention(q, k, v):
            B, H, S, hd = q.shape
            bs = min(S, max(WINDOW, LOCAL_BLOCK))
            nb = S // bs
            w = WINDOW
            L = bs + w - 1
            k_pad = jnp.pad(k, ((0, 0), (0, 0), (w - 1, 0), (0, 0)))
            v_pad = jnp.pad(v, ((0, 0), (0, 0), (w - 1, 0), (0, 0)))
            starts = jnp.arange(nb) * bs
            idx = starts[:, None] + jnp.arange(L)[None, :]
            kb = k_pad[:, :, idx]
            vb = v_pad[:, :, idx]
            qb = q.reshape(B, H, nb, bs, hd)
            q_pos = starts[:, None] + jnp.arange(bs)[None, :]
            k_gpos = starts[:, None] + jnp.arange(L)[None, :] - (w - 1)
            dist = q_pos[:, :, None] - k_gpos[:, None, :]
            allowed = (dist > 0) & (dist <= w) & (k_gpos[:, None, :] >= 0)
            scale = 1.0 / np.sqrt(hd)
            scores = jnp.einsum('bhnqd,bhnkd->bhnqk', qb, kb) * scale
            scores = jnp.where(allowed, scores, NEG)
            attn = jax.nn.softmax(scores, axis=-1)
            attn = jnp.where(allowed.any(-1)[None, None, :, :, None], attn, 0.0)
            out = jnp.einsum('bhnqk,bhnkd->bhnqd', attn, vb)
            return out.reshape(B, H, S, hd)
        key = jax.random.key(seed)
        ks = jax.random.split(key, 14)
        B, S = (2, 1024)
        s = 0.02
        f32 = jnp.float32
        return {'x': jax.random.normal(ks[0], (B, S, D_MODEL), f32), 'qkv_w': jax.random.normal(ks[1], (D_MODEL, 3 * D_MODEL), f32) * s, 'qkv_b': jnp.zeros((3 * D_MODEL,), f32), 'rq_w': jax.random.normal(ks[2], (D_MODEL, LATENT_D), f32) * s, 'rq_b': jnp.zeros((LATENT_D,), f32), 'rkv_w': jax.random.normal(ks[3], (D_MODEL, 2 * LATENT_D), f32) * s, 'rkv_b': jnp.zeros((2 * LATENT_D,), f32), 'rout_w': jax.random.normal(ks[4], (LATENT_D, D_MODEL), f32) * s, 'rout_b': jnp.zeros((D_MODEL,), f32), 'out_w': jax.random.normal(ks[5], (D_MODEL, D_MODEL), f32) * s, 'out_b': jnp.zeros((D_MODEL,), f32), 'gl_w': jax.random.normal(ks[6], (HEAD_DIM, 1), f32) * s, 'gr_w': jax.random.normal(ks[7], (HEAD_DIM, 1), f32) * s}
    _L0_attn_in = _L0_attn_setup()

    def _L0_ffn_setup():
        import jax, jax.numpy as jnp
        import numpy as np
        LN_EPS = 1e-12
        key = jax.random.key(seed)
        ks = jax.random.split(key, 8)
        B, S, H, I, E = (4, 512, 256, 1024, 8)
        sH = 1.0 / np.sqrt(H)
        sI = 1.0 / np.sqrt(I)
        return {'hidden_states': jax.random.normal(ks[0], (B, S, H), dtype=jnp.float32), 'Wr': jax.random.uniform(ks[1], (E, H), jnp.float32, -sH, sH), 'W1': jax.random.uniform(ks[2], (E, H, I), jnp.float32, -sH, sH), 'b1': jax.random.uniform(ks[3], (E, I), jnp.float32, -sH, sH), 'Wo': jax.random.uniform(ks[4], (I, H), jnp.float32, -sI, sI), 'bo': jax.random.uniform(ks[5], (H,), jnp.float32, -sI, sI), 'gamma': jnp.ones((H,), jnp.float32), 'beta': jnp.zeros((H,), jnp.float32)}
    _L0_ffn_in = _L0_ffn_setup()

    def _L1_attn_setup():
        import jax, jax.numpy as jnp
        import numpy as np
        N_HEAD = 16
        BUCKET = 64
        HIDDEN = 256
        EPS = 1e-05

        def _ln(x, g, b):
            m = x.mean(-1, keepdims=True)
            v = x.var(-1, keepdims=True)
            return (x - m) * jax.lax.rsqrt(v + EPS) * g + b
        key = jax.random.key(seed)
        ks = jax.random.split(key, 6)

        def w(k, shape, s=0.02):
            return jax.random.normal(k, shape, jnp.float32) * s
        C = HIDDEN
        return {'x': jax.random.normal(ks[0], (4, 2048, C), jnp.float32), 'ln1_g': jnp.ones((C,), jnp.float32), 'ln1_b': jnp.zeros((C,), jnp.float32), 'w_qkv': w(ks[1], (C, 3 * C)), 'b_qkv': jnp.zeros((3 * C,), jnp.float32), 'w_out': w(ks[2], (C, C)), 'b_out': jnp.zeros((C,), jnp.float32), 'ln2_g': jnp.ones((C,), jnp.float32), 'ln2_b': jnp.zeros((C,), jnp.float32), 'w1': w(ks[3], (C, 4 * C)), 'b1': jnp.zeros((4 * C,), jnp.float32), 'w2': w(ks[4], (4 * C, C)), 'b2': jnp.zeros((C,), jnp.float32)}
    _L1_attn_in = _L1_attn_setup()

    def _L1_ffn_setup():
        import jax, jax.numpy as jnp
        import numpy as np
        DIM = 256
        DEPTH = 2
        HEADS = 8
        DIM_HEAD = 64
        WINDOW = 128
        INNER = HEADS * DIM_HEAD
        HID = int(DIM * 4 * 2 / 3)
        B, N = (2, 2048)
        QK_SCALE = 8.0

        def shift_token(t):
            t1, t2 = jnp.split(t, 2, axis=-1)
            t2 = jnp.pad(t2, ((0, 0), (1, 0), (0, 0)))[:, :-1]
            return jnp.concatenate([t1, t2], axis=-1)

        def l2norm(t):
            return t / jnp.clip(jnp.linalg.norm(t, axis=-1, keepdims=True), 1e-12)

        def rotate_half(x):
            x1, x2 = jnp.split(x, 2, axis=-1)
            return jnp.concatenate([-x2, x1], axis=-1)

        def rotary_xpos(q, k):
            n = q.shape[-2]
            half_idx = jnp.arange(0, DIM_HEAD, 2, dtype=jnp.float32)
            inv_freq = 1.0 / 10000.0 ** (half_idx / DIM_HEAD)
            t = jnp.arange(n, dtype=jnp.float32)
            freqs = t[:, None] * inv_freq[None, :]
            freqs = jnp.concatenate([freqs, freqs], axis=-1)
            base = (half_idx + 0.4 * DIM_HEAD) / (1.4 * DIM_HEAD)
            power = (t - n // 2) / float(WINDOW // 2)
            scale = base[None, :] ** power[:, None]
            scale = jnp.concatenate([scale, scale], axis=-1)
            cos, sin = (jnp.cos(freqs), jnp.sin(freqs))
            q = q * cos * scale + rotate_half(q) * sin * scale
            k = k * cos / scale + rotate_half(k) * sin / scale
            return (q, k)

        def local_attention(q, k, v):
            b, h, n, d = q.shape
            w = n // WINDOW
            bq = q.reshape(b, h, w, WINDOW, d) * QK_SCALE
            bk = k.reshape(b, h, w, WINDOW, d)
            bv = v.reshape(b, h, w, WINDOW, d)

            def look_around(t):
                p = jnp.pad(t, ((0, 0), (0, 0), (1, 0), (0, 0), (0, 0)))
                return jnp.concatenate([p[:, :, :w], p[:, :, 1:]], axis=3)
            bk, bv = (look_around(bk), look_around(bv))
            bt = jnp.arange(n).reshape(w, WINDOW)
            btp = jnp.pad(bt, ((1, 0), (0, 0)), constant_values=-1)
            btk = jnp.concatenate([btp[:w], btp[1:]], axis=1)
            sim = jnp.einsum('bhwid,bhwjd->bhwij', bq, bk)
            i = bt[:, :, None]
            j = btk[:, None, :]
            mask = (i < j) | (i > j + WINDOW) | (j == -1)
            sim = jnp.where(mask, -jnp.finfo(sim.dtype).max, sim)
            attn = jax.nn.softmax(sim, axis=-1)
            out = jnp.einsum('bhwij,bhwjd->bhwid', attn, bv)
            return out.reshape(b, h, n, d)

        def _layer(x, wqkv, qs, ksc, wo, lg, lb, w1, b1, w2, b2):
            b, n, _ = x.shape
            h = shift_token(x)
            qkv = h @ wqkv
            q, k, v = jnp.split(qkv, 3, axis=-1)
            to_heads = lambda t: t.reshape(b, n, HEADS, DIM_HEAD).transpose(0, 2, 1, 3)
            q, k, v = (to_heads(q), to_heads(k), to_heads(v))
            q = l2norm(q) * qs
            k = l2norm(k) * ksc
            q, k = rotary_xpos(q, k)
            o = local_attention(q, k, v)
            o = o.transpose(0, 2, 1, 3).reshape(b, n, INNER)
            x = x + o @ wo
            h = shift_token(x)
            mu = h.mean(-1, keepdims=True)
            var = h.var(-1, keepdims=True)
            h = (h - mu) / jnp.sqrt(var + 1e-05) * lg + lb
            h = h @ w1 + b1
            a, g = jnp.split(h, 2, axis=-1)
            h = a * jax.nn.gelu(g, approximate=False)
            x = x + h @ w2 + b2
            return x
        key = jax.random.key(seed)
        ks = jax.random.split(key, 6)
        return {'x': jax.random.normal(ks[0], (B, N, DIM), jnp.float32), 'wqkv': jax.random.normal(ks[1], (DEPTH, DIM, 3 * INNER), jnp.float32) * 0.02, 'q_scale': jnp.ones((DEPTH, DIM_HEAD), jnp.float32), 'k_scale': jnp.ones((DEPTH, DIM_HEAD), jnp.float32), 'wo': jax.random.normal(ks[2], (DEPTH, INNER, DIM), jnp.float32) * 0.02, 'ln_g': jnp.ones((DEPTH, DIM), jnp.float32), 'ln_b': jnp.zeros((DEPTH, DIM), jnp.float32), 'w1': jax.random.normal(ks[3], (DEPTH, DIM, 2 * HID), jnp.float32) * 0.02, 'b1': jnp.zeros((DEPTH, 2 * HID), jnp.float32), 'w2': jax.random.normal(ks[4], (DEPTH, HID, DIM), jnp.float32) * 0.02, 'b2': jnp.zeros((DEPTH, DIM), jnp.float32)}
    _L1_ffn_in = _L1_ffn_setup()
    _d = {'L0_attn_x': _L0_attn_in['x'], 'L0_attn_qkv_w': _L0_attn_in['qkv_w'], 'L0_attn_qkv_b': _L0_attn_in['qkv_b'], 'L0_attn_rq_w': _L0_attn_in['rq_w'], 'L0_attn_rq_b': _L0_attn_in['rq_b'], 'L0_attn_rkv_w': _L0_attn_in['rkv_w'], 'L0_attn_rkv_b': _L0_attn_in['rkv_b'], 'L0_attn_rout_w': _L0_attn_in['rout_w'], 'L0_attn_rout_b': _L0_attn_in['rout_b'], 'L0_attn_out_w': _L0_attn_in['out_w'], 'L0_attn_out_b': _L0_attn_in['out_b'], 'L0_attn_gl_w': _L0_attn_in['gl_w'], 'L0_attn_gr_w': _L0_attn_in['gr_w'], 'L0_ffn_Wr': _L0_ffn_in['Wr'], 'L0_ffn_W1': _L0_ffn_in['W1'], 'L0_ffn_b1': _L0_ffn_in['b1'], 'L0_ffn_Wo': _L0_ffn_in['Wo'], 'L0_ffn_bo': _L0_ffn_in['bo'], 'L0_ffn_gamma': _L0_ffn_in['gamma'], 'L0_ffn_beta': _L0_ffn_in['beta'], 'L1_attn_ln1_g': _L1_attn_in['ln1_g'], 'L1_attn_ln1_b': _L1_attn_in['ln1_b'], 'L1_attn_w_qkv': _L1_attn_in['w_qkv'], 'L1_attn_b_qkv': _L1_attn_in['b_qkv'], 'L1_attn_w_out': _L1_attn_in['w_out'], 'L1_attn_b_out': _L1_attn_in['b_out'], 'L1_attn_ln2_g': _L1_attn_in['ln2_g'], 'L1_attn_ln2_b': _L1_attn_in['ln2_b'], 'L1_attn_w1': _L1_attn_in['w1'], 'L1_attn_b1': _L1_attn_in['b1'], 'L1_attn_w2': _L1_attn_in['w2'], 'L1_attn_b2': _L1_attn_in['b2'], 'L1_ffn_wqkv': _L1_ffn_in['wqkv'], 'L1_ffn_q_scale': _L1_ffn_in['q_scale'], 'L1_ffn_k_scale': _L1_ffn_in['k_scale'], 'L1_ffn_wo': _L1_ffn_in['wo'], 'L1_ffn_ln_g': _L1_ffn_in['ln_g'], 'L1_ffn_ln_b': _L1_ffn_in['ln_b'], 'L1_ffn_w1': _L1_ffn_in['w1'], 'L1_ffn_b1': _L1_ffn_in['b1'], 'L1_ffn_w2': _L1_ffn_in['w2'], 'L1_ffn_b2': _L1_ffn_in['b2']}
    _x0 = _d['L0_attn_x']
    _d['L0_attn_x'] = jax.random.normal(jax.random.fold_in(jax.random.key(seed), 1), (2, 2048, 256), dtype=_x0.dtype)
    del _x0
    return _d

def reference(L0_attn_x, L0_attn_qkv_w, L0_attn_qkv_b, L0_attn_rq_w, L0_attn_rq_b, L0_attn_rkv_w, L0_attn_rkv_b, L0_attn_rout_w, L0_attn_rout_b, L0_attn_out_w, L0_attn_out_b, L0_attn_gl_w, L0_attn_gr_w, L0_ffn_Wr, L0_ffn_W1, L0_ffn_b1, L0_ffn_Wo, L0_ffn_bo, L0_ffn_gamma, L0_ffn_beta, L1_attn_ln1_g, L1_attn_ln1_b, L1_attn_w_qkv, L1_attn_b_qkv, L1_attn_w_out, L1_attn_b_out, L1_attn_ln2_g, L1_attn_ln2_b, L1_attn_w1, L1_attn_b1, L1_attn_w2, L1_attn_b2, L1_ffn_wqkv, L1_ffn_q_scale, L1_ffn_k_scale, L1_ffn_wo, L1_ffn_ln_g, L1_ffn_ln_b, L1_ffn_w1, L1_ffn_b1, L1_ffn_w2, L1_ffn_b2):

    def _L0_attn_ref(x, qkv_w, qkv_b, rq_w, rq_b, rkv_w, rkv_b, rout_w, rout_b, out_w, out_b, gl_w, gr_w):
        import jax, jax.numpy as jnp
        import numpy as np
        D_MODEL = 256
        N_HEADS = 16
        HEAD_DIM = D_MODEL // N_HEADS
        WINDOW = 128
        LOCAL_BLOCK = 64
        LATENT_TOKENS = 64
        LATENT_D = 64
        LATENT_HEADS = 4
        LATENT_HD = LATENT_D // LATENT_HEADS
        NEG = -1000000000.0

        def _local_attention(q, k, v):
            B, H, S, hd = q.shape
            bs = min(S, max(WINDOW, LOCAL_BLOCK))
            nb = S // bs
            w = WINDOW
            L = bs + w - 1
            k_pad = jnp.pad(k, ((0, 0), (0, 0), (w - 1, 0), (0, 0)))
            v_pad = jnp.pad(v, ((0, 0), (0, 0), (w - 1, 0), (0, 0)))
            starts = jnp.arange(nb) * bs
            idx = starts[:, None] + jnp.arange(L)[None, :]
            kb = k_pad[:, :, idx]
            vb = v_pad[:, :, idx]
            qb = q.reshape(B, H, nb, bs, hd)
            q_pos = starts[:, None] + jnp.arange(bs)[None, :]
            k_gpos = starts[:, None] + jnp.arange(L)[None, :] - (w - 1)
            dist = q_pos[:, :, None] - k_gpos[:, None, :]
            allowed = (dist > 0) & (dist <= w) & (k_gpos[:, None, :] >= 0)
            scale = 1.0 / np.sqrt(hd)
            scores = jnp.einsum('bhnqd,bhnkd->bhnqk', qb, kb) * scale
            scores = jnp.where(allowed, scores, NEG)
            attn = jax.nn.softmax(scores, axis=-1)
            attn = jnp.where(allowed.any(-1)[None, None, :, :, None], attn, 0.0)
            out = jnp.einsum('bhnqk,bhnkd->bhnqd', attn, vb)
            return out.reshape(B, H, S, hd)
        B, S, D = x.shape
        qkv = x @ qkv_w + qkv_b
        q, k, v = jnp.split(qkv, 3, axis=-1)

        def heads(t):
            return t.reshape(B, S, N_HEADS, HEAD_DIM).transpose(0, 2, 1, 3)
        local = _local_attention(heads(q), heads(k), heads(v))
        chunk = -(-S // min(LATENT_TOKENS, S))
        nlat = S // chunk
        pooled = x.reshape(B, nlat, chunk, D).mean(axis=2)
        chunk_ids = jnp.arange(S) // chunk
        rq = (x @ rq_w + rq_b).reshape(B, S, LATENT_HEADS, LATENT_HD).transpose(0, 2, 1, 3)
        rkv = pooled @ rkv_w + rkv_b
        rk, rv = jnp.split(rkv, 2, axis=-1)
        rk = rk.reshape(B, nlat, LATENT_HEADS, LATENT_HD).transpose(0, 2, 1, 3)
        rv = rv.reshape(B, nlat, LATENT_HEADS, LATENT_HD).transpose(0, 2, 1, 3)
        lscale = 1.0 / np.sqrt(LATENT_HD)
        lscores = jnp.einsum('bhsd,bhld->bhsl', rq, rk) * lscale
        lat_allowed = jnp.arange(nlat)[None, :] < chunk_ids[:, None]
        lscores = jnp.where(lat_allowed[None, None], lscores, NEG)
        lattn = jax.nn.softmax(lscores, axis=-1)
        lattn = jnp.where(lat_allowed.any(-1)[None, None, :, None], lattn, 0.0)
        lat_out = jnp.einsum('bhsl,bhld->bhsd', lattn, rv)
        lat_out = lat_out.transpose(0, 2, 1, 3).reshape(B, S, LATENT_D)
        remote = lat_out @ rout_w + rout_b
        remote_h = remote.reshape(B, S, N_HEADS, HEAD_DIM).transpose(0, 2, 1, 3)
        gate = jax.nn.sigmoid(local @ gl_w + remote_h @ gr_w)
        mixed = gate * local + (1.0 - gate) * remote_h
        mixed = mixed.transpose(0, 2, 1, 3).reshape(B, S, D)
        return mixed @ out_w + out_b

    def _L0_ffn_ref(hidden_states, Wr, W1, b1, Wo, bo, gamma, beta):
        import jax, jax.numpy as jnp
        import numpy as np
        LN_EPS = 1e-12
        B, S, H = hidden_states.shape
        E = Wr.shape[0]
        x = hidden_states.reshape(-1, H)
        router_logits = x @ Wr.T
        expert_idx = jnp.argmax(jax.nn.softmax(router_logits, axis=-1), axis=-1)
        inter = jnp.zeros((x.shape[0], W1.shape[2]), dtype=x.dtype)
        for e in range(E):
            mask = (expert_idx == e)[:, None].astype(x.dtype)
            inter = inter + mask * jax.nn.gelu(x @ W1[e] + b1[e], approximate=False)
        y = inter @ Wo + bo + x
        mu = jnp.mean(y, axis=-1, keepdims=True)
        var = jnp.mean(jnp.square(y - mu), axis=-1, keepdims=True)
        out = (y - mu) * jax.lax.rsqrt(var + LN_EPS) * gamma + beta
        return out.reshape(B, S, H)

    def _L1_attn_ref(x, ln1_g, ln1_b, w_qkv, b_qkv, w_out, b_out, ln2_g, ln2_b, w1, b1, w2, b2):
        import jax, jax.numpy as jnp
        import numpy as np
        N_HEAD = 16
        BUCKET = 64
        HIDDEN = 256
        EPS = 1e-05

        def _ln(x, g, b):
            m = x.mean(-1, keepdims=True)
            v = x.var(-1, keepdims=True)
            return (x - m) * jax.lax.rsqrt(v + EPS) * g + b
        B, T, C = x.shape
        nb = T // BUCKET
        hd = C // N_HEAD
        scale = 1.0 / np.sqrt(hd)
        h = _ln(x, ln1_g, ln1_b)
        qkv = h @ w_qkv + b_qkv
        q, k, v = jnp.split(qkv, 3, axis=-1)

        def buck(t):
            return t.reshape(B, nb, BUCKET, N_HEAD, hd)
        qb, kb, vb = (buck(q), buck(k), buck(v))
        kp = jnp.concatenate([jnp.zeros_like(kb[:, :1]), kb[:, :-1]], axis=1)
        vp = jnp.concatenate([jnp.zeros_like(vb[:, :1]), vb[:, :-1]], axis=1)
        kc = jnp.concatenate([kp, kb], axis=2)
        vc = jnp.concatenate([vp, vb], axis=2)
        scores = jnp.einsum('bnihd,bnjhd->bnhij', qb, kc) * scale
        i = jnp.arange(BUCKET)[:, None]
        j = jnp.arange(2 * BUCKET)[None, :]
        mask = (j < BUCKET) | (j - BUCKET <= i)
        scores = jnp.where(mask, scores, -jnp.inf)
        attn = jax.nn.softmax(scores, axis=-1)
        ob = jnp.einsum('bnhij,bnjhd->bnihd', attn, vc).reshape(B, T, C)
        x = x + ob @ w_out + b_out
        h2 = _ln(x, ln2_g, ln2_b)
        m = jax.nn.gelu(h2 @ w1 + b1, approximate=False) @ w2 + b2
        return x + m

    def _L1_ffn_ref(x, wqkv, q_scale, k_scale, wo, ln_g, ln_b, w1, b1, w2, b2):
        import jax, jax.numpy as jnp
        import numpy as np
        DIM = 256
        DEPTH = 2
        HEADS = 8
        DIM_HEAD = 64
        WINDOW = 128
        INNER = HEADS * DIM_HEAD
        HID = int(DIM * 4 * 2 / 3)
        B, N = (2, 2048)
        QK_SCALE = 8.0

        def shift_token(t):
            t1, t2 = jnp.split(t, 2, axis=-1)
            t2 = jnp.pad(t2, ((0, 0), (1, 0), (0, 0)))[:, :-1]
            return jnp.concatenate([t1, t2], axis=-1)

        def l2norm(t):
            return t / jnp.clip(jnp.linalg.norm(t, axis=-1, keepdims=True), 1e-12)

        def rotate_half(x):
            x1, x2 = jnp.split(x, 2, axis=-1)
            return jnp.concatenate([-x2, x1], axis=-1)

        def rotary_xpos(q, k):
            n = q.shape[-2]
            half_idx = jnp.arange(0, DIM_HEAD, 2, dtype=jnp.float32)
            inv_freq = 1.0 / 10000.0 ** (half_idx / DIM_HEAD)
            t = jnp.arange(n, dtype=jnp.float32)
            freqs = t[:, None] * inv_freq[None, :]
            freqs = jnp.concatenate([freqs, freqs], axis=-1)
            base = (half_idx + 0.4 * DIM_HEAD) / (1.4 * DIM_HEAD)
            power = (t - n // 2) / float(WINDOW // 2)
            scale = base[None, :] ** power[:, None]
            scale = jnp.concatenate([scale, scale], axis=-1)
            cos, sin = (jnp.cos(freqs), jnp.sin(freqs))
            q = q * cos * scale + rotate_half(q) * sin * scale
            k = k * cos / scale + rotate_half(k) * sin / scale
            return (q, k)

        def local_attention(q, k, v):
            b, h, n, d = q.shape
            w = n // WINDOW
            bq = q.reshape(b, h, w, WINDOW, d) * QK_SCALE
            bk = k.reshape(b, h, w, WINDOW, d)
            bv = v.reshape(b, h, w, WINDOW, d)

            def look_around(t):
                p = jnp.pad(t, ((0, 0), (0, 0), (1, 0), (0, 0), (0, 0)))
                return jnp.concatenate([p[:, :, :w], p[:, :, 1:]], axis=3)
            bk, bv = (look_around(bk), look_around(bv))
            bt = jnp.arange(n).reshape(w, WINDOW)
            btp = jnp.pad(bt, ((1, 0), (0, 0)), constant_values=-1)
            btk = jnp.concatenate([btp[:w], btp[1:]], axis=1)
            sim = jnp.einsum('bhwid,bhwjd->bhwij', bq, bk)
            i = bt[:, :, None]
            j = btk[:, None, :]
            mask = (i < j) | (i > j + WINDOW) | (j == -1)
            sim = jnp.where(mask, -jnp.finfo(sim.dtype).max, sim)
            attn = jax.nn.softmax(sim, axis=-1)
            out = jnp.einsum('bhwij,bhwjd->bhwid', attn, bv)
            return out.reshape(b, h, n, d)

        def _layer(x, wqkv, qs, ksc, wo, lg, lb, w1, b1, w2, b2):
            b, n, _ = x.shape
            h = shift_token(x)
            qkv = h @ wqkv
            q, k, v = jnp.split(qkv, 3, axis=-1)
            to_heads = lambda t: t.reshape(b, n, HEADS, DIM_HEAD).transpose(0, 2, 1, 3)
            q, k, v = (to_heads(q), to_heads(k), to_heads(v))
            q = l2norm(q) * qs
            k = l2norm(k) * ksc
            q, k = rotary_xpos(q, k)
            o = local_attention(q, k, v)
            o = o.transpose(0, 2, 1, 3).reshape(b, n, INNER)
            x = x + o @ wo
            h = shift_token(x)
            mu = h.mean(-1, keepdims=True)
            var = h.var(-1, keepdims=True)
            h = (h - mu) / jnp.sqrt(var + 1e-05) * lg + lb
            h = h @ w1 + b1
            a, g = jnp.split(h, 2, axis=-1)
            h = a * jax.nn.gelu(g, approximate=False)
            x = x + h @ w2 + b2
            return x
        for l in range(DEPTH):
            x = _layer(x, wqkv[l], q_scale[l], k_scale[l], wo[l], ln_g[l], ln_b[l], w1[l], b1[l], w2[l], b2[l])
        return x
    x = L0_attn_x
    xn = _layernorm(x, axis=-1)
    s = _L0_attn_ref(xn, L0_attn_qkv_w, L0_attn_qkv_b, L0_attn_rq_w, L0_attn_rq_b, L0_attn_rkv_w, L0_attn_rkv_b, L0_attn_rout_w, L0_attn_rout_b, L0_attn_out_w, L0_attn_out_b, L0_attn_gl_w, L0_attn_gr_w)
    g = _silu(_L0_ffn_ref(xn, L0_ffn_Wr, L0_ffn_W1, L0_ffn_b1, L0_ffn_Wo, L0_ffn_bo, L0_ffn_gamma, L0_ffn_beta))
    x = x + s * g
    xn = _layernorm(x, axis=-1)
    s = _L1_attn_ref(xn, L1_attn_ln1_g, L1_attn_ln1_b, L1_attn_w_qkv, L1_attn_b_qkv, L1_attn_w_out, L1_attn_b_out, L1_attn_ln2_g, L1_attn_ln2_b, L1_attn_w1, L1_attn_b1, L1_attn_w2, L1_attn_b2)
    g = _silu(_L1_ffn_ref(xn, L1_ffn_wqkv, L1_ffn_q_scale, L1_ffn_k_scale, L1_ffn_wo, L1_ffn_ln_g, L1_ffn_ln_b, L1_ffn_w1, L1_ffn_b1, L1_ffn_w2, L1_ffn_b2))
    x = x + s * g
    return x

_drawn_inputs = setup_inputs


def setup_inputs(seed=0):
    import zlib

    import numpy as np

    out = dict(_drawn_inputs(seed))
    spreads = {'L0_attn_qkv_b': (0.0, 0.344),
     'L0_attn_rq_b': (0.0, 2.0),
     'L0_attn_rkv_b': (0.0, 0.8),
     'L0_attn_rout_b': (0.0, 0.369),
     'L0_attn_out_b': (0.0, 0.1),
     'L0_ffn_gamma': (1.0, 0.2),
     'L0_ffn_beta': (0.0, 0.8),
     'L1_attn_ln1_g': (1.0, 0.6),
     'L1_attn_ln1_b': (0.0, 0.8),
     'L1_attn_b_qkv': (0.0, 0.766),
     'L1_attn_b_out': (0.0, 0.568),
     'L1_attn_ln2_g': (1.0, 0.6),
     'L1_attn_ln2_b': (0.0, 2.0),
     'L1_attn_b1': (0.0, 0.692),
     'L1_attn_b2': (0.0, 0.511),
     'L1_ffn_q_scale': (1.0, 0.6),
     'L1_ffn_k_scale': (1.0, 0.6),
     'L1_ffn_ln_g': (1.0, 0.6),
     'L1_ffn_ln_b': (0.0, 0.8),
     'L1_ffn_b1': (0.0, 0.8),
     'L1_ffn_b2': (0.0, 0.1)}
    factors = {'L0_attn_qkv_w': 7.377,
     'L0_attn_rq_w': 8.0,
     'L0_attn_rkv_w': 8.0,
     'L0_attn_rout_w': 8.0,
     'L0_attn_gl_w': 8.0,
     'L0_attn_gr_w': 8.0,
     'L0_ffn_Wr': 3.553,
     'L0_ffn_W1': 3.311,
     'L0_ffn_b1': 8.0,
     'L0_ffn_Wo': 3.137,
     'L0_ffn_bo': 8.0,
     'L1_attn_w_qkv': 8.0,
     'L1_attn_w_out': 5.124,
     'L1_ffn_wqkv': 4.383,
     'L1_ffn_wo': 4.438,
     'L1_ffn_w1': 2.926,
     'L1_ffn_w2': 2.891}
    for name, (base, spread) in spreads.items():
        noise = np.random.default_rng([zlib.crc32(name.encode()), seed]).standard_normal(out[name].shape)
        drawn = base * np.exp(spread * noise) if base else spread * noise
        out[name] = jnp.asarray(drawn.astype(out[name].dtype))
    for name, factor in factors.items():
        out[name] = (out[name] * factor).astype(out[name].dtype)
    return out
```

```python
from contextlib import ExitStack

import numpy as np
import concourse.bass as bass
from concourse import mybir

F32 = mybir.dt.float32
BF16 = mybir.dt.bfloat16
U32 = mybir.dt.uint32
ALU = mybir.AluOpType
ACT = mybir.ActivationFunctionType
AX = mybir.AxisListType

P = 128
D = 256
KC = D // P
BATCH, SEQ = 2, 2048
NT = BATCH * SEQ // P
TPG = 4
NG = NT // TPG
GPB = SEQ // P // TPG
BANK = 512
NEG = -1.0e30
EXPERTS, INNER = 8, 1024
SLOT_TILES = NT + EXPERTS


class Count:

    def __init__(self, sem, per, credit=0):
        self.sem, self.per, self.credit = sem, per, credit

    def at(self, it, k):
        return it * self.per + (k + self.credit)


class Space:

    def __init__(self, nc, ctx, stage):
        self.nc, self.ctx, self.stage = nc, ctx, stage
        self.sems = []

    def sb(self, name, shape, dt=F32):
        return self.ctx.enter_context(self.nc.sbuf_tensor(f"{self.stage}_{name}", shape, dt))

    def ps(self, name, shape=(P, BANK), dt=F32):
        return self.ctx.enter_context(self.nc.psum_tensor(f"{self.stage}_{name}", list(shape), dt))

    def sem(self, name):
        self.sems.append(self.ctx.enter_context(self.nc.semaphore(f"{self.stage}_{name}")))
        return self.sems[-1]

    def clear_semaphores(self):
        with self.nc.Block() as block:
            @block.gpsimd
            def _(pool):
                for sem in self.sems:
                    pool.sem_clear(sem)

    def count(self, name, per, credit=0):
        return Count(self.sem(name), per, credit)


def bcast(row, shape):
    return row.unsqueeze(2).to_broadcast(shape)


def load_bias_rows(sp, done, pairs):
    for dst, src in pairs:
        sp.dma_start(dst, src.partition_broadcast(P)).then_inc(done, 16)
    return 16 * len(pairs)


def normalise_input(nc, io, keep):
    with ExitStack() as ctx:
        s = Space(nc, ctx, "norm")
        stats = s.sb("stats", [P, TPG, 6])
        mv, mv4 = s.sb("mv", [P, NT, 2]), s.sb("mv4", [P, TPG, 2])
        ve = s.sb("ve", [P, NT])
        x_loaded = [s.sem(f"x_loaded{b}") for b in range(BATCH)]
        consts_loaded = s.sem("consts_loaded")
        var_ready, rstd_ready = s.sem("var_ready"), s.sem("rstd_ready")
        XN = keep.XN
        tiles = io["L0_attn_x"].rearrange("b (n p) d -> b p n d", p=P)
        npb = SEQ // P
        with nc.Block() as block:
            @block.sync
            def _(sp):
                for b in range(BATCH):
                    sp.dma_start(XN[:, 1 + b * npb:1 + (b + 1) * npb, :], tiles[b]).then_inc(x_loaded[b], 16)
                sp.dma_start(keep.ident[:], io["const_ident"]).then_inc(consts_loaded, 16)
                sp.dma_start(keep.identb[:], io["const_identb"]).then_inc(consts_loaded, 16)
                sp.dma_start(keep.going[:], io["const_going"]).then_inc(consts_loaded, 16)
                sp.dma_start(keep.w_router[:], io["w_router"]).then_inc(consts_loaded, 16)
                sp.wait_ge(consts_loaded, 64)

            @block.gpsimd
            def _(pool):
                pool.memset(keep.minus_half[:], -0.5)
                pool.memset(XN[:, 0, :], 0.0)
                pool.drain()
                for b in range(BATCH):
                    pool.wait_ge(var_ready, b + 1)
                    pool.tensor_tensor(keep.rstd[:, b * npb:(b + 1) * npb], ve[:, b * npb:(b + 1) * npb],
                                       keep.minus_half[:, 0:npb], ALU.pow).then_inc(rstd_ready, 1)

            @block.vector
            def _(dve):
                for b in range(BATCH):
                    dve.wait_ge(x_loaded[b], 16)
                    with dve.Fori(b * NG // BATCH, (b + 1) * NG // BATCH) as g:
                        for n in range(TPG):
                            dve.bn_stats(stats[:, n, :], XN[:, g * TPG + (n + 1), :])
                        dve.drain()
                        for n in range(TPG):
                            dve.bn_aggr(mv4[:, n, :], stats[:, n, :])
                        dve.drain()
                        dve.tensor_copy(mv[:, bass.ds(g * TPG, TPG), :], mv4[:])
                        dve.drain()
                    dve.tensor_scalar(ve[:, b * npb:(b + 1) * npb], mv[:, b * npb:(b + 1) * npb, 1], 1e-5, None,
                                      ALU.add).then_inc(var_ready, 1)
                for b in range(BATCH):
                    dve.wait_ge(rstd_ready, b + 1)
                    with dve.Fori(b * NG // BATCH, (b + 1) * NG // BATCH) as g:
                        for n in range(TPG):
                            t = g * TPG + n
                            dve.tensor_scalar(XN[:, g * TPG + (n + 1), :], XN[:, g * TPG + (n + 1), :],
                                              mv[:, t, 0:1], keep.rstd[:, bass.ds(g * TPG + n, 1)],
                                              ALU.subtract, ALU.mult)
        s.clear_semaphores()


class Keep:

    def __init__(self, nc, ctx):
        s = Space(nc, ctx, "keep")
        self.XN = s.sb("xn", [P, NT + 1, D])
        self.X2 = s.sb("x2", [P, NT + 1, D])
        self.ident = s.sb("ident", [P, P])
        self.identb = s.sb("identb", [P, P], BF16)
        self.going = s.sb("going", [P, NG])
        self.minus_half = s.sb("minus_half", [P, NT])
        self.rstd = s.sb("rstd", [P, NT])
        self.mean = s.sb("mean", [P, NT])
        self.w_router = s.sb("w_router", [P, KC, EXPERTS])
        self.logits = s.sb("logits", [P, NT, EXPERTS])
        self.slot = s.sb("slot", [P, NT], U32)
        self.expert = s.sb("expert", [1, SLOT_TILES], U32)


HEADS, HD = 16, 16
LAT, LAT_HEADS = 64, 4
CHUNK = SEQ // LAT
LPT = P // CHUNK


def window_attention(nc, io, keep, layer):
    latents = layer == 0
    pre = "L0_attn_" if latents else "L1_attn_"
    WU = HEADS // 2
    ST = WU + latents
    U = ST * TPG
    if latents:
        before = ["hT", "Q", "K", "V", "R"]
        plan = {0: ("hT", 1), 1: ("Q", 1), 2: ("latT", -1), 3: ("K", 1), 4: ("rem", -1), 5: ("V", 1), 6: ("R", 1),
                7: ("oT", -1), 8: ("out", -1)}
        by_act = ("hT", "latT", "oT")
    else:
        before = ["hT", "Q", "K", "V"]
        plan = {0: ("hT", 1), 1: ("Q", 1), 2: ("oT", -1), 3: ("K", 1), 4: ("out", -1), 5: ("V", 1)}
        by_act = ("hT", "oT")
    linear = [(-1, name, 0) for name in before]
    for step in range(U + ST):
        name, ahead = plan.get(step % ST, (None, 0))
        if name and 0 <= step // ST + ahead < TPG and (step < U or ahead < 0):
            linear.append((step, name, step // ST + ahead))
    order = [(name, n) for _, name, n in linear]
    NACT = sum(name in by_act for name, _ in order)
    NDVE = len(order) - NACT

    with ExitStack() as ctx:
        s = Space(nc, ctx, f"win{layer}")
        XN, X2 = keep.XN, keep.X2
        w_qk = s.sb("w_qk", [P, KC, 2 * HEADS, 32])
        w_v = s.sb("w_v", [P, KC, D])
        w_out = s.sb("w_out", [P, KC, D])
        b_qk = s.sb("b_qk", [P, 8])
        b_v, b_out = s.sb("b_v", [P, D]), s.sb("b_out", [P, D])
        h = s.sb("h", [P, TPG, D])
        hT = s.sb("hT", [P, KC, P])
        QT = s.sb("QT", [P, 2, 4, P])
        KT = s.sb("KT", [P, 4, (TPG + 1) * P])
        V = s.sb("V", [P, TPG + 1, D])
        probs = s.sb("probs", [P, 2, BANK])
        probsT = s.sb("probsT", [P, 2, BANK])
        negmax = s.sb("negmax", [P, 4, 4])
        sums = s.sb("sums", [P, 2, HEADS + LAT_HEADS])
        rsum = s.sb("rsum", [P, HEADS + LAT_HEADS])
        attn = s.sb("attn", [P, D])
        oT = s.sb("oT", [P, KC, P])
        tmp = s.sb("tmp", [P, D])
        mask = s.sb("mask", [P, NG, 2 * P], BF16)
        if latents:
            w_rq = s.sb("w_rq", [P, KC, LAT_HEADS, 32])
            w_rk = s.sb("w_rk", [P, KC, LAT_HEADS, 32])
            w_rv = s.sb("w_rv", [P, KC, LAT])
            w_rout = s.sb("w_rout", [LAT, D])
            b_rq, b_rk = s.sb("b_rq", [P, 1]), s.sb("b_rk", [P, 1])
            b_rv, b_rout = s.sb("b_rv", [P, LAT]), s.sb("b_rout", [P, D])
            gl, gr = s.sb("gl", [P, HD]), s.sb("gr", [P, HD])
            pooledT = s.sb("pooledT", [P, KC, 2 * LAT])
            RQT = s.sb("RQT", [P, 2, P])
            RKT = s.sb("RKT", [P, 2, LAT_HEADS * LAT])
            RV = s.sb("RV", [P, 2, LAT])
            lat_mask = s.sb("lat_mask", [P, NT, LAT], BF16)
            valid = s.sb("valid", [P, NG, 2])
            lat, latT = s.sb("lat", [P, P]), s.sb("latT", [LAT, P])
            rem = s.sb("rem", [P, D])
            tmp2 = s.sb("tmp2", [P, D])
            z, ez, gate = s.sb("z", [P, HEADS]), s.sb("ez", [P, HEADS]), s.sb("gate", [P, HEADS])
        else:
            g1, b1 = s.sb("g1", [P, KC]), s.sb("b1", [P, KC])
            stats, mv, mv1 = s.sb("stats", [P, 6]), s.sb("mv", [P, NT, 2]), s.sb("mv1", [P, 2])
            ve = s.sb("ve", [P, NT])

        score = [s.ps(f"score{i}") for i in range(4)]
        turned = [s.ps(f"turned{i}") for i in range(2)]
        po, lin = s.ps("po"), s.ps("lin")

        loaded, zeroed, biases = s.sem("loaded"), s.sem("zeroed"), s.sem("biases")
        h_ready = s.count("h_ready", 1)
        lin_ready = s.count("lin_ready", len(order))
        act_took = s.count("act_took", NACT)
        dve_took = s.count("dve_took", NDVE, credit=1)
        scores_ready = s.count("scores_ready", U)
        max_ready = s.count("max_ready", U)
        probs_ready = s.count("probs_ready", U, credit=4)
        turned_ready = s.count("turned_ready", U, credit=2)
        probsT_ready = s.count("probsT_ready", U, credit=2)
        pv_done = s.count("pv_done", U, credit=2)
        attn_ready = s.count("attn_ready", TPG, credit=1)
        pooled_ready = s.count("pooled_ready", TPG)
        z_ready, ez_ready = s.count("z_ready", TPG), s.count("ez_ready", TPG)
        mixed_ready = s.count("mixed_ready", TPG)
        var_ready, rstd_done = s.sem("var_ready"), s.sem("rstd_done")
        rows_zeroed = s.sem("rows_zeroed")

        def taken(name, n):
            upto = order[:order.index((name, n)) + 1]
            acts = sum(x in by_act for x, _ in upto)
            return (act_took, acts) if name in by_act else (dve_took, len(upto) - acts)

        def heads_of(u):
            n, i = divmod(u, ST)
            return n, ([8 * (i // 4) + i % 4, 8 * (i // 4) + i % 4 + 4] if i < WU else None)

        with nc.Block() as block:
            @block.sync
            def _(sp):
                sp.wait_ge(zeroed, 1)
                qkv = io[pre + ("qkv_w" if latents else "w_qkv")].rearrange("(c p) (w n) -> p c w n", p=P, w=3)
                bqkv = io[pre + ("qkv_b" if latents else "b_qkv")]
                n = 0
                pairs = [(w_qk[:], io[f"win{layer}_w_qk"]), (b_qk[:], io[f"win{layer}_b_qk"]), (w_v[:], qkv[:, :, 2, :]),
                         (w_out[:], io[pre + ("out_w" if latents else "w_out")].rearrange("(c p) n -> p c n", p=P)),
                         (mask[:], io["const_mask0" if latents else "const_mask1"])]
                if latents:
                    rkv = io[pre + "rkv_w"].rearrange("(c p) n -> p c n", p=P)
                    pairs += [(w_rq[:], io["win0_w_rq"]), (w_rk[:], io["win0_w_rk"]),
                              (b_rq[:], io["win0_b_rq"]), (b_rk[:], io["win0_b_rk"])]
                    pairs += [(w_rv[:], rkv[:, :, LAT:]), (w_rout[:], io[pre + "rout_w"]),
                              (lat_mask[:], io["const_lat_mask"]), (valid[:], io["const_valid"])]
                else:
                    pairs += [(g1[:], io["win1_gain"]), (b1[:], io["win1_offset"])]
                for dst, src in pairs:
                    sp.dma_start(dst, src).then_inc(loaded, 16)
                    n += 16
                rows = [(b_v[:], bqkv[2 * D:3 * D]), (b_out[:], io[pre + ("out_b" if latents else "b_out")])]
                if latents:
                    rows += [(b_rv[:], io[pre + "rkv_b"][LAT:]), (b_rout[:], io[pre + "rout_b"]),
                             (gl[:], io[pre + "gl_w"].rearrange("d o -> (d o)")),
                             (gr[:], io[pre + "gr_w"].rearrange("d o -> (d o)"))]
                n += load_bias_rows(sp, loaded, rows)
                sp.wait_ge(loaded, n)
                sp.sem_inc(biases, 1)
                if latents:
                    sp.dma_start(io["rows_in"].rearrange("(t p) d -> p t d", p=P),
                                 XN[:, 0:1, :].to_broadcast([P, SLOT_TILES, D])).then_inc(rows_zeroed, 16)
                    sp.wait_ge(rows_zeroed, 16)

            @block.gpsimd
            def _(pool):
                pool.memset(KT[:, :, TPG * P:], 0.0)
                pool.memset(V[:, TPG, :], 0.0)
                if latents:
                    pool.memset(pooledT[:], 0.0)
                    pool.memset(lat[:], 0.0)
                    pool.memset(RKT[:], 0.0)
                    pool.memset(RV[:], 0.0)
                pool.drain()
                pool.sem_inc(zeroed, 1)
                if not latents:
                    pool.wait_ge(var_ready, 1)
                    pool.tensor_tensor(keep.rstd[:], ve[:], keep.minus_half[:], ALU.pow).then_inc(rstd_done, 1)

            @block.tensor
            def _(pe):
                pe.sem_inc(turned_ready.sem, turned_ready.credit)
                pe.sem_inc(pv_done.sem, pv_done.credit)
                pe.wait_ge(biases, 1)

                def linear_step(it, name, n):
                    i = order.index((name, n))
                    if i == 0:
                        pe.wait_ge(dve_took.sem, dve_took.at(it, 0))
                    else:
                        c, k = taken(*order[i - 1])
                        pe.wait_ge(c.sem, c.at(it, k))
                    if name in ("Q", "K", "V"):
                        c, k = taken("hT", n)
                        pe.wait_ge(c.sem, c.at(it, k))
                    if name == "hT":
                        if n == 0:
                            pe.wait_ge(h_ready.sem, h_ready.at(it, 1))
                        for c in range(KC):
                            last = pe.transpose(lin[:, c * P:(c + 1) * P], h[:, n, c * P:(c + 1) * P], keep.ident[:])
                    elif name in ("Q", "K"):
                        for quad in range(4):
                            first = (name == "K") * HEADS + 4 * quad
                            for c in range(KC):
                                last = pe.matmul(lin[:, quad * P:(quad + 1) * P],
                                                 w_qk[:, c, first:first + 4, :].rearrange("p h d -> p (h d)"),
                                                 hT[:, c, :], start=(c == 0), stop=(c == KC - 1))
                    elif name == "V":
                        for c in range(KC):
                            last = pe.matmul(lin[:, 0:D], hT[:, c, :], w_v[:, c, :], start=(c == 0), stop=(c == KC - 1))
                        if latents:
                            for c in range(KC):
                                last = pe.matmul(lin[:, D:D + P], w_rq[:, c, :, :].rearrange("p h d -> p (h d)"),
                                                 hT[:, c, :], start=(c == 0), stop=(c == KC - 1))
                            for c in range(KC):
                                last = pe.matmul(lin[:, D + P:D + P + EXPERTS], hT[:, c, :], keep.w_router[:, c, :],
                                                 start=(c == 0), stop=(c == KC - 1))
                    elif name == "R":
                        pe.wait_ge(pooled_ready.sem, pooled_ready.at(it, n + 1))
                        for c in range(KC):
                            pe.matmul(lin[:, 0:LAT], w_rk[:, c, :, :].rearrange("p h d -> p (h d)"), pooledT[:, c, 0:LAT],
                                      start=(c == 0), stop=(c == KC - 1))
                        for c in range(KC):
                            last = pe.matmul(lin[:, LAT:2 * LAT], pooledT[:, c, :], w_rv[:, c, :],
                                             start=(c == 0), stop=(c == KC - 1))
                    elif name == "latT":
                        pe.wait_ge(attn_ready.sem, attn_ready.at(it, n + 1))
                        last = pe.transpose(lin[:, 0:P], lat[:], keep.ident[:])
                    elif name == "rem":
                        c, k = taken("latT", n)
                        pe.wait_ge(c.sem, c.at(it, k))
                        last = pe.matmul(lin[:, 0:D], latT[:], w_rout[:], start=True, stop=True)
                    elif name == "oT":
                        ready = mixed_ready if latents else attn_ready
                        pe.wait_ge(ready.sem, ready.at(it, n + 1))
                        for c in range(KC):
                            last = pe.transpose(lin[:, c * P:(c + 1) * P], attn[:, c * P:(c + 1) * P], keep.ident[:])
                    elif name == "out":
                        c, k = taken("oT", n)
                        pe.wait_ge(c.sem, c.at(it, k))
                        for c in range(KC):
                            last = pe.matmul(lin[:, 0:D], oT[:, c, :], w_out[:, c, :], start=(c == 0), stop=(c == KC - 1))
                    last.then_inc(lin_ready.sem, 1)

                def scores(it, g, u):
                    n, heads = heads_of(u)
                    bank = score[u % 4]
                    pe.wait_ge(probs_ready.sem, probs_ready.at(it, u - 3))
                    if u % ST == 0:
                        c, k = taken("R" if latents else "V", n)
                        pe.wait_ge(c.sem, c.at(it, k))
                    if heads is None:
                        pe.matmul(bank[:, 0:LAT_HEADS * LAT], keep.identb[:],
                                  lat_mask[:, bass.ds(g * TPG + n, 1), :].to_broadcast([P, LAT_HEADS, LAT]),
                                  start=True, stop=False)
                        last = pe.matmul(bank[:, 0:LAT_HEADS * LAT], RQT[:, n % 2, :], RKT[:, n % 2, :],
                                         start=False, stop=True)
                    else:
                        m = mask[:, bass.ds(g, 1), :] if n == 0 else mask[:, 1:2, :]
                        pe.matmul(bank[:], keep.identb[:], m.to_broadcast([P, 2, 2 * P]), start=True, stop=False)
                        for i in range(2):
                            c, j = divmod(heads[i], 4)
                            last = pe.matmul(bank[:, i * 2 * P:(i + 1) * 2 * P], QT[32 * j:32 * j + HD, n % 2, c, :],
                                             KT[32 * j:32 * j + HD, c, n * P:(n + 2) * P], start=False, stop=(i == 1))
                    last.then_inc(scores_ready.sem, 1)

                def turn(it, u):
                    n, heads = heads_of(u)
                    pe.wait_ge(probs_ready.sem, probs_ready.at(it, u + 1))
                    pe.wait_ge(probsT_ready.sem, probsT_ready.at(it, u - 1))
                    for i in range(LAT_HEADS // 2 if heads is None else 4):
                        last = pe.transpose(turned[u % 2][:, i * P:(i + 1) * P],
                                            probs[:, u % 2, i * P:(i + 1) * P], keep.ident[:])
                    last.then_inc(turned_ready.sem, 1)

                def weigh(it, u):
                    n, heads = heads_of(u)
                    pe.wait_ge(probsT_ready.sem, probsT_ready.at(it, u + 1))
                    if u % ST == 0:
                        pe.wait_ge(attn_ready.sem, attn_ready.at(it, n))
                    if heads is None:
                        for j in range(LAT_HEADS // 2):
                            last = pe.matmul(po[:, D + j * 2 * HD:D + (j + 1) * 2 * HD], probsT[:, u % 2, j * P:(j + 1) * P],
                                             RV[:, n % 2, j * 2 * HD:(j + 1) * 2 * HD], start=True, stop=True)
                    else:
                        for i in range(2):
                            a = heads[i] * HD
                            for kb in range(2):
                                last = pe.matmul(po[:, a:a + HD], probsT[:, u % 2, (2 * i + kb) * P:(2 * i + kb + 1) * P],
                                                 V[:, n + kb, a:a + HD], start=(kb == 0), stop=(kb == 1))
                    last.then_inc(pv_done.sem, 1)

                with pe.Fori(0, NG) as g:
                    for _, name, n in linear[:len(before)]:
                        linear_step(g, name, n)
                    scores(g, g, 0)
                    scores(g, g, 1)
                    for step in range(U + ST):
                        for at, name, n in linear:
                            if at == step:
                                linear_step(g, name, n)
                        if step + 2 < U:
                            scores(g, g, step + 2)
                        if step < U:
                            turn(g, step)
                        if 1 <= step <= U:
                            weigh(g, step - 1)

            @block.scalar
            def _(act):
                act.sem_inc(probs_ready.sem, probs_ready.credit)
                act.wait_ge(biases, 1)

                def take(it, name, n):
                    act.wait_ge(lin_ready.sem, lin_ready.at(it, order.index((name, n)) + 1))
                    if name == "hT" and not latents:
                        act.activation(hT[:, 0, :], lin[:, 0:P], ACT.Identity, bias=b1[:, 0:1], scale=g1[:, 0:1])
                        last = act.activation(hT[:, 1, :], lin[:, P:2 * P], ACT.Identity, bias=b1[:, 1:2], scale=g1[:, 1:2])
                    elif name in ("hT", "oT"):
                        dst = hT if name == "hT" else oT
                        last = act.activation(dst[:].rearrange("p c n -> p (c n)"), lin[:, 0:D], ACT.Copy)
                    else:
                        last = act.activation(latT[:], lin[0:LAT, 0:P], ACT.Copy)
                    last.then_inc(act_took.sem, 1)

                def softmax(it, u):
                    n, heads = heads_of(u)
                    act.wait_ge(max_ready.sem, max_ready.at(it, u + 1))
                    act.wait_ge(turned_ready.sem, turned_ready.at(it, u - 1))
                    width = LAT if heads is None else 2 * P
                    cols = range(HEADS, HEADS + LAT_HEADS) if heads is None else heads
                    for i, col in enumerate(cols):
                        last = act.activation(probs[:, u % 2, i * width:(i + 1) * width],
                                              score[u % 4][:, i * width:(i + 1) * width], ACT.Exp,
                                              bias=negmax[:, u % 4, i:i + 1],
                                              accum_out=sums[:, n % 2, col:col + 1])
                    last.then_inc(probs_ready.sem, 1)

                with act.Fori(0, NG) as g:
                    for _, name, n in linear[:len(before)]:
                        if name in by_act:
                            take(g, name, n)
                    softmax(g, 0)
                    softmax(g, 1)
                    for step in range(U + ST):
                        for at, name, n in linear:
                            if at == step and name in by_act:
                                take(g, name, n)
                        if step + 2 < U:
                            softmax(g, step + 2)
                        if latents and step % ST == 5 and step >= ST:
                            act.wait_ge(z_ready.sem, z_ready.at(g, step // ST))
                            act.activation(ez[:], z[:], ACT.Exp, scale=-1.0).then_inc(ez_ready.sem, 1)

            @block.vector
            def _(dve):
                dve.sem_inc(dve_took.sem, dve_took.credit)
                dve.sem_inc(probsT_ready.sem, probsT_ready.credit)
                dve.sem_inc(attn_ready.sem, attn_ready.credit)
                dve.wait_ge(biases, 1)
                dve.tensor_scalar(b_qk[:, 0:4], b_qk[:, 0:4], HD ** -0.5, None, ALU.mult)
                dve.drain()

                def take(it, g, name, n):
                    dve.wait_ge(lin_ready.sem, lin_ready.at(it, order.index((name, n)) + 1))
                    if name == "Q":
                        last = dve.scalar_tensor_tensor(QT[:, n % 2, :, :], lin[:].rearrange("p (c n) -> p c n", c=4),
                                                        HD ** -0.5, bcast(b_qk[:, 0:4], [P, 4, P]), ALU.mult, ALU.add)
                    elif name == "K":
                        last = dve.tensor_tensor(KT[:, :, (n + 1) * P:(n + 2) * P],
                                                 lin[:].rearrange("p (c n) -> p c n", c=4),
                                                 bcast(b_qk[:, 4:8], [P, 4, P]), ALU.add)
                    elif name == "V":
                        last = dve.tensor_tensor(V[:, n + 1, :], lin[:, 0:D], b_v[:], ALU.add)
                        if latents:
                            dve.tensor_scalar(RQT[:, n % 2, :], lin[:, D:D + P], b_rq[:, 0:1], HD ** -0.5,
                                              ALU.add, ALU.mult)
                            last = dve.tensor_copy(keep.logits[:, g * TPG + n, :], lin[:, D + P:D + P + EXPERTS])
                    elif name == "R":
                        for j in range(LAT_HEADS):
                            quad = slice(32 * j, 32 * j + 32)
                            dve.tensor_scalar(RKT[quad, n % 2, j * LAT:(j + 1) * LAT], lin[quad, 0:LAT], 1.0 / CHUNK,
                                              b_rk[quad, 0:1], ALU.mult, ALU.add)
                        for odd in range(2):
                            rows = slice(odd * LAT, (odd + 1) * LAT)
                            pairs = lambda t: t.rearrange("p (j two d) -> p j two d", two=2, d=HD)[:, :, odd, :]
                            last = dve.scalar_tensor_tensor(pairs(RV[rows, n % 2, :]), pairs(lin[rows, LAT:2 * LAT]),
                                                            1.0 / CHUNK, pairs(b_rv[rows, :]), ALU.mult, ALU.add)
                    elif name == "rem":
                        last = dve.tensor_tensor(rem[:], lin[:, 0:D], b_rout[:], ALU.add)
                    elif latents:
                        last = dve.tensor_tensor(X2[:, g * TPG + (n + 1), :], lin[:, 0:D], b_out[:], ALU.add)
                    else:
                        last = dve.tensor_tensor(tmp[:], lin[:, 0:D], b_out[:], ALU.add)
                    last.then_inc(dve_took.sem, 1)
                    if name == "out" and not latents:
                        dve.drain()
                        dve.tensor_tensor(X2[:, g * TPG + (n + 1), :], tmp[:], XN[:, g * TPG + (n + 1), :], ALU.add)
                        dve.drain()
                        dve.bn_stats(stats[:], X2[:, g * TPG + (n + 1), :])
                        dve.drain()
                        dve.bn_aggr(mv1[:], stats[:])
                        dve.drain()
                        dve.tensor_copy(mv[:, g * TPG + n, :], mv1[:])

                def pool_latents(it, gi, n):
                    c, k = taken("hT", n)
                    dve.wait_ge(c.sem, c.at(it, k))
                    for c in range(KC):
                        for twice in range(2):
                            first = gi * (TPG * LPT) + (n * LPT + twice * LAT)
                            last = dve.tensor_reduce(pooledT[:, c, bass.ds(first, LPT)],
                                                     hT[:, c, :].rearrange("p (l n) -> p l n", n=CHUNK), AX.X, ALU.add)
                    last.then_inc(pooled_ready.sem, 1)

                def maxima(it, u):
                    _, heads = heads_of(u)
                    dve.wait_ge(scores_ready.sem, scores_ready.at(it, u + 1))
                    k = LAT_HEADS if heads is None else 2
                    w = LAT if heads is None else 2 * P
                    dve.tensor_reduce(negmax[:, u % 4, 0:k], score[u % 4][:, 0:k * w].rearrange("p (h k) -> p h k", h=k),
                                      AX.X, ALU.max, negate=True).then_inc(max_ready.sem, 1)

                def take_turned(it, u):
                    _, heads = heads_of(u)
                    dve.wait_ge(turned_ready.sem, turned_ready.at(it, u + 1))
                    dve.wait_ge(pv_done.sem, pv_done.at(it, u - 1))
                    k = LAT_HEADS // 2 * P if heads is None else BANK
                    dve.tensor_copy(probsT[:, u % 2, 0:k], turned[u % 2][:, 0:k]).then_inc(probsT_ready.sem, 1)

                def normalise(it, g, n):
                    dve.wait_ge(pv_done.sem, pv_done.at(it, (n + 1) * ST))
                    if latents:
                        pass
                    heads = HEADS + (LAT_HEADS if latents else 0)
                    dve.reciprocal(rsum[:, 0:heads], sums[:, n % 2, 0:heads])
                    dve.drain()
                    if latents and n == 0:
                        dve.tensor_scalar(rsum[:, 0:HEADS], rsum[:, 0:HEADS], valid[:, g, 0:1], None, ALU.mult)
                        dve.tensor_scalar(rsum[:, HEADS:], rsum[:, HEADS:], valid[:, g, 1:2], None, ALU.mult)
                        dve.drain()
                    last = dve.tensor_tensor(attn[:].rearrange("p (h d) -> p h d", d=HD),
                                             po[:, 0:D].rearrange("p (h d) -> p h d", d=HD),
                                             bcast(rsum[:, 0:HEADS], [P, HEADS, HD]), ALU.mult)
                    if latents:
                        last = dve.tensor_tensor(lat[:, 0:LAT].rearrange("p (h d) -> p h d", d=HD),
                                                 po[:, D:D + LAT].rearrange("p (h d) -> p h d", d=HD),
                                                 bcast(rsum[:, HEADS:], [P, LAT_HEADS, HD]), ALU.mult)
                    last.then_inc(attn_ready.sem, 1)

                by_head = lambda t: t[:].rearrange("p (h d) -> p h d", d=HD)
                gate_row = lambda t: t[:].unsqueeze(1).to_broadcast([P, HEADS, HD])

                def gate_logits(it):
                    dve.drain()
                    dve.tensor_tensor(by_head(tmp), by_head(attn), gate_row(gl), ALU.mult)
                    dve.tensor_tensor(by_head(tmp2), by_head(rem), gate_row(gr), ALU.mult)
                    dve.drain()
                    dve.tensor_tensor(tmp[:], tmp[:], tmp2[:], ALU.add)
                    dve.drain()
                    dve.tensor_reduce(z[:], by_head(tmp), AX.X, ALU.add).then_inc(z_ready.sem, 1)

                def mix(it, n):
                    dve.tensor_tensor(attn[:], attn[:], rem[:], ALU.subtract)
                    dve.wait_ge(ez_ready.sem, ez_ready.at(it, n + 1))
                    dve.tensor_scalar(gate[:], ez[:], 1.0, None, ALU.add)
                    dve.drain()
                    dve.reciprocal(gate[:], gate[:])
                    dve.drain()
                    dve.tensor_tensor(by_head(attn), by_head(attn), bcast(gate[:], [P, HEADS, HD]), ALU.mult)
                    dve.drain()
                    dve.tensor_tensor(attn[:], attn[:], rem[:], ALU.add).then_inc(mixed_ready.sem, 1)

                def group(it, gi):
                    g = it
                    if latents:
                        dve.tensor_copy(h[:], XN[:, bass.ds(g * TPG + 1, TPG), :])
                    else:
                        for n in range(TPG):
                            dve.tensor_scalar(h[:, n, :], XN[:, g * TPG + (n + 1), :],
                                              keep.mean[:, bass.ds(g * TPG + n, 1)],
                                              keep.rstd[:, bass.ds(g * TPG + n, 1)], ALU.subtract, ALU.mult)
                    dve.drain()
                    dve.sem_inc(h_ready.sem, 1)
                    dve.tensor_scalar(KT[:, :, 0:P], KT[:, :, TPG * P:], keep.going[:, bass.ds(g, 1)], None, ALU.mult)
                    dve.tensor_scalar(V[:, 0, :], V[:, TPG, :], keep.going[:, bass.ds(g, 1)], None, ALU.mult)
                    dve.drain()
                    for _, name, n in linear[:len(before)]:
                        if latents and name == "Q":
                            pool_latents(it, gi, n)
                        if name not in by_act:
                            take(it, g, name, n)
                    maxima(it, 0)
                    maxima(it, 1)
                    for step in range(U + ST):
                        for at, name, n in linear:
                            if at == step and name not in by_act:
                                if latents and name == "Q":
                                    pool_latents(it, gi, n)
                                take(it, g, name, n)
                        if step + 2 < U:
                            maxima(it, step + 2)
                        if step < U:
                            take_turned(it, step)
                        if step % ST == 0 and step > 0:
                            normalise(it, g, step // ST - 1)
                        if latents and step % ST == 4 and step > ST:
                            gate_logits(it)
                        if latents and step % ST == 5 and step > ST:
                            mix(it, step // ST - 1)

                if latents:
                    with dve.Fori(0, BATCH) as b:
                        with dve.Fori(0, GPB) as gi:
                            group(b * GPB + gi, gi)
                else:
                    with dve.Fori(0, NG) as g:
                        group(g, None)
                    dve.drain()
                    dve.tensor_copy(keep.mean[:], mv[:, :, 0])
                    dve.tensor_scalar(ve[:], mv[:, :, 1], 1e-5, None, ALU.add).then_inc(var_ready, 1)
                    dve.wait_ge(rstd_done, 1)
        s.clear_semaphores()


def route(nc, io, keep):
    with ExitStack() as ctx:
        s = Space(nc, ctx, "route")
        top, number = s.sb("top", [P, NT]), s.sb("number", [P, EXPERTS])
        chosen = s.sb("chosen", [P, NT])
        mask = s.sb("mask", [P, NT, EXPERTS])
        mask16 = s.sb("mask16", [P, NT, EXPERTS], BF16)
        before = s.sb("before", [P, NT + 1, EXPERTS])
        before16 = s.sb("before16", [P, NT + 1, EXPERTS], BF16)
        earlier = s.sb("earlier", [P, P], BF16)
        ones16 = s.sb("ones16", [P, P], BF16)
        iota = s.sb("iota", [P, SLOT_TILES])
        counts = s.sb("counts", [P, EXPERTS])
        over = s.sb("over", [P, EXPERTS, NT])
        tiles, ends, first = s.sb("tiles", [P, EXPERTS]), s.sb("ends", [P, EXPERTS]), s.sb("first", [P, EXPERTS])
        ones = s.sb("ones", [P, EXPERTS])
        place = s.sb("place", [P, NT, EXPERTS])
        slotf = s.sb("slotf", [P, NT])
        past = s.sb("past", [P, SLOT_TILES, EXPERTS])
        expertf = s.sb("expertf", [P, SLOT_TILES])
        copied = s.sb("copied", [P, 2, D])
        index_now = s.sb("index_now", [P, 2, 1], U32)
        rank, total = s.ps("rank", [P, NT * EXPERTS]), s.ps("total", [P, EXPERTS])
        loaded, masks_ready, ranks_ready = s.sem("loaded"), s.sem("masks_ready"), s.sem("ranks_ready")
        slots_ready, staged, started = s.sem("slots_ready"), s.sem("staged"), s.sem("started")
        scattered = [s.sem(f"scattered{i}") for i in range(2)]
        with nc.Block() as block:
            @block.sync
            def _(sp):
                sp.dma_start(earlier[:], io["const_earlier"]).then_inc(loaded, 16)
                sp.dma_start(iota[:], io["const_iota"]).then_inc(loaded, 16)

            @block.tensor
            def _(pe):
                pe.wait_ge(loaded, 32)
                pe.wait_ge(masks_ready, 1)
                pe.matmul(rank[:], earlier[:], mask16[:].rearrange("p t e -> p (t e)"), start=True, stop=False)
                pe.matmul(rank[:], ones16[:], before16[:, 0:NT, :].rearrange("p t e -> p (t e)"), start=False, stop=True)
                pe.matmul(total[:], ones16[:], before16[:, NT, :], start=True, stop=True).then_inc(ranks_ready, 1)

            @block.gpsimd
            def _(pool):
                pool.wait_ge(slots_ready, 1)
                with pool.Fori(0, NT // 2) as t2:
                    for i in range(2):
                        pool.wait_ge(staged, t2 * 2 + (i + 1))
                        pool.sem_inc(started, 1)
                        pool.indirect_dma_start(io["rows_in"], bass.IndirectOffsetOnAxis(ap=index_now[:, i, :], axis=0),
                                                copied[:, i, :], None).then_inc(scattered[i], 16)
                for i in range(2):
                    pool.wait_ge(scattered[i], 16 * NT // 2)

            @block.vector
            def _(dve):
                dve.memset(ones16[:], 1.0)
                dve.memset(ones[:], 1.0)
                dve.memset(before[:, 0, :], 0.0)
                dve.wait_ge(loaded, 32)
                dve.tensor_reduce(top[:], keep.logits[:], AX.X, ALU.max)
                dve.tensor_scalar(number[:], iota[:, 0:EXPERTS], float(EXPERTS), None, ALU.subtract)
                dve.drain()
                dve.tensor_tensor(mask[:], keep.logits[:], bcast(top[:], [P, NT, EXPERTS]), ALU.is_equal)
                dve.drain()
                numbers = number[:].unsqueeze(1).to_broadcast([P, NT, EXPERTS])
                dve.tensor_tensor(mask[:], mask[:], numbers, ALU.mult)
                dve.drain()
                dve.tensor_reduce(chosen[:], mask[:], AX.X, ALU.min)
                dve.drain()
                dve.tensor_tensor(mask[:], bcast(chosen[:], [P, NT, EXPERTS]), numbers, ALU.is_equal)
                dve.drain()
                dve.tensor_copy(mask16[:], mask[:])
                for t in range(NT):
                    dve.tensor_tensor(before[:, t + 1, :], before[:, t, :], mask[:, t, :], ALU.add)
                    dve.drain()
                dve.tensor_copy(before16[:], before[:]).then_inc(masks_ready, 1)
                dve.wait_ge(ranks_ready, 1)
                dve.tensor_copy(counts[:], total[:])
                dve.drain()
                dve.tensor_scalar(slotf[:], iota[:, 0:NT], float(P), None, ALU.mult)
                dve.drain()
                dve.tensor_tensor(over[:], bcast(counts[:], [P, EXPERTS, NT]),
                                  slotf[:].unsqueeze(1).to_broadcast([P, EXPERTS, NT]), ALU.is_gt)
                dve.drain()
                dve.tensor_reduce(tiles[:], over[:], AX.X, ALU.add)
                dve.drain()
                dve.tensor_tensor_scan(ends[:], ones[:], tiles[:], 0.0, ALU.mult, ALU.add)
                dve.drain()
                dve.tensor_tensor(first[:], ends[:], tiles[:], ALU.subtract)
                dve.drain()
                dve.tensor_scalar(first[:], first[:], float(P), None, ALU.mult)
                dve.drain()
                dve.tensor_tensor(place[:], rank[:].rearrange("p (t e) -> p t e", e=EXPERTS),
                                  first[:].unsqueeze(1).to_broadcast([P, NT, EXPERTS]), ALU.add)
                dve.drain()
                dve.tensor_tensor(place[:], place[:], mask[:], ALU.mult)
                dve.drain()
                dve.tensor_reduce(slotf[:], place[:], AX.X, ALU.add)
                dve.drain()
                dve.tensor_copy(keep.slot[:], slotf[:])
                dve.tensor_tensor(past[:], bcast(iota[:], [P, SLOT_TILES, EXPERTS]),
                                  ends[:].unsqueeze(1).to_broadcast([P, SLOT_TILES, EXPERTS]), ALU.is_ge)
                dve.drain()
                dve.tensor_reduce(expertf[:], past[:], AX.X, ALU.add)
                dve.drain()
                dve.tensor_scalar(expertf[:], expertf[:], float(EXPERTS - 1), None, ALU.min)
                dve.drain()
                dve.tensor_copy(keep.expert[:], expertf[0:1, :])
                dve.drain()
                dve.sem_inc(slots_ready, 1)

                def stage(t2, i):
                    dve.tensor_copy(copied[:, i, :], keep.XN[:, t2 * 2 + (i + 1), :])
                    dve.tensor_copy(index_now[:, i, :], keep.slot[:, bass.ds(t2 * 2 + i, 1)])
                    dve.drain()
                    dve.sem_inc(staged, 1)

                for i in range(2):
                    stage(0, i)
                with dve.Fori(1, NT // 2) as t2:
                    for i in range(2):
                        dve.wait_ge(scattered[i], t2 * 16)
                        stage(t2, i)
        s.clear_semaphores()


def experts(nc, io, keep):
    HB = INNER // BANK
    IC = INNER // P
    N = SLOT_TILES
    with ExitStack() as ctx:
        s = Space(nc, ctx, "experts")
        w1 = s.sb("w1", [P, KC, EXPERTS * INNER])
        b1 = s.sb("b1", [P, EXPERTS * INNER])
        wo = s.sb("wo", [P, IC, D])
        rows = s.sb("rows", [P, 2, D])
        rowsT = s.sb("rowsT", [P, KC, P])
        inner = s.sb("inner", [P, 1, INNER])
        innerT = s.sb("innerT", [P, IC, P])
        y = s.sb("y", [P, 2, D])
        turned = s.ps("turned")
        hidden = [[s.ps(f"hidden{i}{b}") for b in range(HB)] for i in range(2)]
        innerT_ps = [s.ps(f"innerT{b}") for b in range(HB)]
        out = s.ps("out")
        loaded = s.sem("loaded")
        rows_loaded = [s.sem(f"rows_loaded{i}") for i in range(2)]
        stored = [s.sem(f"stored{i}") for i in range(2)]
        turned_ready, rowsT_ready = s.sem("turned_ready"), s.sem("rowsT_ready")
        hidden_ready, biased, gelu_done = s.sem("hidden_ready"), s.sem("biased"), s.sem("gelu_done")
        innerT_turned, innerT_ready = s.sem("innerT_turned"), s.sem("innerT_ready")
        out_ready, y_ready = s.sem("out_ready"), s.sem("y_ready")
        rows_in = io["rows_in"].rearrange("(t p) d -> t p d", p=P)
        rows_out = io["rows_out"].rearrange("(t p) d -> t p d", p=P)
        with nc.Block() as block:
            @block.sync
            def _(sp):
                n = 0
                for dst, src in [(wo[:], io["L0_ffn_Wo"].rearrange("(c p) n -> p c n", p=P))] + \
                        [(w1[:, c, e * INNER:(e + 1) * INNER], io["L0_ffn_W1"][e, c * P:(c + 1) * P, :])
                         for e in range(EXPERTS) for c in range(KC)] + \
                        [(b1[:, e * INNER:(e + 1) * INNER], io["L0_ffn_b1"][e].partition_broadcast(P))
                         for e in range(EXPERTS)]:
                    sp.dma_start(dst, src).then_inc(loaded, 16)
                    n += 16
                for i in range(2):
                    sp.dma_start(rows[:, i, :], rows_in[i]).then_inc(rows_loaded[i], 16)
                with sp.Fori(1, N // 2) as j2:
                    for i in range(2):
                        sp.wait_ge(turned_ready, j2 * 2 + (i - 1))
                        sp.dma_start(rows[:, i, :], rows_in[j2 * 2 + i]).then_inc(rows_loaded[i], 16)

            @block.tensor
            def _(pe):
                def turn_rows(j, i, count):
                    pe.wait_ge(rows_loaded[i], 16 * count)
                    for c in range(KC):
                        last = pe.transpose(turned[:, c * P:(c + 1) * P], rows[:, i, c * P:(c + 1) * P], keep.ident[:])
                    last.then_inc(turned_ready, 1)

                def hide(j, i, later):
                    e = pe.value_load(keep.expert[0:1, bass.ds(j, 1)], min_val=0, max_val=EXPERTS - 1)
                    pe.wait_ge(rowsT_ready, j + 1)
                    if later:
                        pe.wait_ge(biased, (j - 1) * HB)
                    for b in range(HB):
                        for c in range(KC):
                            last = pe.matmul(hidden[i][b][:], rowsT[:, c, :],
                                             w1[:, c, bass.ds(e * INNER + b * BANK, BANK)],
                                             start=(c == 0), stop=(c == KC - 1))
                        last.then_inc(hidden_ready, 1)

                def project(j):
                    pe.wait_ge(gelu_done, j * HB + HB)
                    for b in range(HB):
                        for c in range(4):
                            a = b * BANK + c * P
                            last = pe.transpose(innerT_ps[b][:, c * P:(c + 1) * P], inner[:, 0, a:a + P], keep.ident[:])
                        last.then_inc(innerT_turned, 1)
                    for b in range(HB):
                        pe.wait_ge(innerT_ready, j * HB + (b + 1))
                        for c in range(4 * b, 4 * b + 4):
                            last = pe.matmul(out[:, 0:D], innerT[:, c, :], wo[:, c, :], start=(c == 0), stop=(c == IC - 1))
                    last.then_inc(out_ready, 1)

                pe.wait_ge(loaded, 16 * (1 + EXPERTS * (KC + 1)))
                turn_rows(0, 0, 1)
                hide(0, 0, False)
                turn_rows(1, 1, 1)
                pe.wait_ge(y_ready, 1)
                hide(1, 1, False)
                pe.wait_ge(rowsT_ready, 2)
                turn_rows(2, 0, 2)
                project(0)
                with pe.Fori(1, N // 2 - 1) as j2:
                    for i in range(2):
                        j = j2 * 2 + i
                        hide(j, i, True)
                        turn_rows(j2 * 2 + (i + 1), 1 - i, j2 + (i + 1))
                        pe.wait_ge(y_ready, j2 * 2 + i)
                        project(j2 * 2 + (i - 1))
                hide(N - 2, 0, True)
                turn_rows(N - 1, 1, N // 2)
                pe.wait_ge(y_ready, N - 2)
                project(N - 3)
                hide(N - 1, 1, True)
                pe.wait_ge(y_ready, N - 1)
                project(N - 2)
                pe.wait_ge(y_ready, N)
                project(N - 1)

            @block.vector
            def _(dve):
                dve.wait_ge(loaded, 16 * (1 + EXPERTS * (KC + 1)))
                def bias(j, i, first):
                    e = dve.value_load(keep.expert[0:1, bass.ds(j, 1)], min_val=0, max_val=EXPERTS - 1)
                    for b in range(HB):
                        dve.wait_ge(hidden_ready, j * HB + (b + 1))
                        if not first and b == 0:
                            dve.wait_ge(innerT_turned, j * HB)
                        dve.tensor_tensor(inner[:, 0, b * BANK:(b + 1) * BANK], hidden[i][b][:],
                                          b1[:, bass.ds(e * INNER + b * BANK, BANK)], ALU.add).then_inc(biased, 1)

                def take_inner(j, first):
                    for b in range(HB):
                        dve.wait_ge(innerT_turned, j * HB + (b + 1))
                        if not first and b == 0:
                            dve.wait_ge(out_ready, j)
                        dve.tensor_copy(innerT[:, 4 * b:4 * b + 4, :].rearrange("p c n -> p (c n)"), innerT_ps[b][:])\
                           .then_inc(innerT_ready, 1)

                bias(0, 0, True)
                take_inner(0, True)
                bias(1, 1, False)
                take_inner(1, False)
                with dve.Fori(1, N // 2) as j2:
                    for i in range(2):
                        bias(j2 * 2 + i, i, False)
                        take_inner(j2 * 2 + i, False)

            @block.scalar
            def _(act):
                act.sem_inc(y_ready, 1)
                def take_rows(j):
                    act.wait_ge(turned_ready, j + 1)
                    act.activation(rowsT[:].rearrange("p c n -> p (c n)"), turned[:, 0:D], ACT.Copy).then_inc(rowsT_ready, 1)

                def gelu(j):
                    for b in range(HB):
                        act.wait_ge(biased, j * HB + (b + 1))
                        act.activation(inner[:, 0, b * BANK:(b + 1) * BANK], inner[:, 0, b * BANK:(b + 1) * BANK],
                                       ACT.Gelu).then_inc(gelu_done, 1)

                def take_out(j, i, count):
                    act.wait_ge(out_ready, j + 1)
                    if count is not None:
                        act.wait_ge(stored[i], 16 * count)
                    act.activation(y[:, i, :], out[:, 0:D], ACT.Copy).then_inc(y_ready, 1)

                take_rows(0)
                take_rows(1)
                gelu(0)
                take_rows(2)
                take_out(0, 0, None)
                gelu(1)
                take_rows(3)
                take_out(1, 1, None)
                with act.Fori(1, N // 2 - 1) as j2:
                    for i in range(2):
                        gelu(j2 * 2 + i)
                        take_rows(j2 * 2 + (i + 2))
                        take_out(j2 * 2 + i, i, j2)
                for i in range(2):
                    gelu(N - 2 + i)
                    take_out(N - 2 + i, i, N // 2 - 1)

            @block.gpsimd
            def _(pool):
                with pool.Fori(0, N // 2) as j2:
                    for i in range(2):
                        pool.wait_ge(y_ready, j2 * 2 + (i + 2))
                        pool.dma_start(rows_out[j2 * 2 + i], y[:, i, :]).then_inc(stored[i], 16)
                for i in range(2):
                    pool.wait_ge(stored[i], 16 * N // 2)
        s.clear_semaphores()


def finish_layer0(nc, io, keep):
    with ExitStack() as ctx:
        s = Space(nc, ctx, "fin0")
        XN, X2 = keep.XN, keep.X2
        bo, gamma, beta = (s.sb(n, [P, D]) for n in ("bo", "gamma", "beta"))
        got = s.sb("got", [P, 2, TPG, D])
        xin = s.sb("xin", [P, 2, TPG, D])
        y = s.sb("y", [P, TPG, D])
        gate = s.sb("gate", [P, TPG, D])
        x1 = s.sb("x1", [P, 2, TPG, D])
        index_now = s.sb("index_now", [P, 2, TPG, 1], U32)
        stats, mv, ve, rs = s.sb("stats", [P, TPG, 6]), s.sb("mv", [P, TPG, 2]), s.sb("ve", [P, TPG]), s.sb("rs", [P, TPG])
        mv_all, ve_all = s.sb("mv_all", [P, NT, 2]), s.sb("ve_all", [P, NT])
        loaded = s.sem("loaded")
        x_loaded = [s.sem(f"x_loaded{i}") for i in range(2)]
        gathered = [s.sem(f"gathered{i}") for i in range(2)]
        x1_ready, biases, all_var_ready = s.sem("x1_ready"), s.sem("biases"), s.sem("all_var_ready")
        stored = [s.sem(f"stored{i}") for i in range(2)]
        var_ready, rstd_ready = s.sem("var_ready"), s.sem("rstd_ready")
        normed, gate_ready = s.sem("normed"), s.sem("gate_ready")
        groups = io["L0_attn_x"].rearrange("b (g n p) d -> (b g) p n d", p=P, n=TPG)
        x1_groups = io["x1"].rearrange("(g n p) d -> g p n d", p=P, n=TPG)
        rows4 = lambda row: row[:].unsqueeze(1).to_broadcast([P, TPG, D])
        with nc.Block() as block:
            @block.sync
            def _(sp):
                n = load_bias_rows(sp, loaded, [(bo[:], io["L0_ffn_bo"]), (gamma[:], io["L0_ffn_gamma"]),
                                                (beta[:], io["L0_ffn_beta"])])
                for i in range(2):
                    sp.dma_start(xin[:, i, :, :], groups[i]).then_inc(x_loaded[i], 16)
                sp.wait_ge(loaded, n)
                sp.sem_inc(biases, 1)
                with sp.Fori(0, NG // 2 - 1) as g2:
                    for i in range(2):
                        sp.wait_ge(x1_ready, g2 * 2 + (i + 1))
                        sp.dma_start(x1_groups[g2 * 2 + i], x1[:, i, :, :]).then_inc(stored[i], 16)
                        sp.dma_start(xin[:, i, :, :], groups[g2 * 2 + (i + 2)]).then_inc(x_loaded[i], 16)
                for i in range(2):
                    sp.wait_ge(x1_ready, NG - 1 + i)
                    sp.dma_start(x1_groups[NG - 2 + i], x1[:, i, :, :]).then_inc(stored[i], 16)
                for i in range(2):
                    sp.wait_ge(stored[i], 16 * (NG // 2 + 1))

            @block.gpsimd
            def _(pool):
                def gather(g, i):
                    for n in range(TPG):
                        pool.tensor_copy(index_now[:, i, n, :], keep.slot[:, bass.ds(g * TPG + n, 1)])
                    pool.drain()
                    for n in range(TPG):
                        pool.indirect_dma_start(got[:, i, n, :], None, io["rows_out"],
                                                bass.IndirectOffsetOnAxis(ap=index_now[:, i, n, :], axis=0))\
                            .then_inc(gathered[i], 16)

                def rstds(k):
                    pool.wait_ge(var_ready, k)
                    pool.tensor_tensor(rs[:], ve[:], keep.minus_half[:, 0:TPG], ALU.pow).then_inc(rstd_ready, 1)

                for i in range(2):
                    gather(i, i)
                with pool.Fori(0, NG // 2 - 1) as g2:
                    for i in range(2):
                        rstds(g2 * 4 + (2 * i + 1))
                        rstds(g2 * 4 + (2 * i + 2))
                        pool.wait_ge(x1_ready, g2 * 2 + (i + 1))
                        gather(g2 * 2 + (i + 2), i)
                for i in range(2):
                    rstds(2 * NG - 4 + 2 * i + 1)
                    rstds(2 * NG - 4 + 2 * i + 2)
                pool.wait_ge(all_var_ready, 1)
                pool.tensor_tensor(keep.rstd[:], ve_all[:], keep.minus_half[:], ALU.pow).then_inc(rstd_ready, 1)

            @block.scalar
            def _(act):
                with act.Fori(0, NG) as g:
                    act.wait_ge(normed, g + 1)
                    act.activation(gate[:], y[:], ACT.Silu).then_inc(gate_ready, 1)

            @block.vector
            def _(dve):
                for i in range(2):
                    dve.sem_inc(stored[i], 16)
                dve.wait_ge(biases, 1)

                def statistics(src, k, eps):
                    for n in range(TPG):
                        dve.bn_stats(stats[:, n, :], src(n))
                    dve.drain()
                    for n in range(TPG):
                        dve.bn_aggr(mv[:, n, :], stats[:, n, :])
                    dve.drain()
                    dve.tensor_scalar(ve[:], mv[:, :, 1], eps, None, ALU.add).then_inc(var_ready, 1)
                    dve.wait_ge(rstd_ready, k)

                def group(g2, i):
                    g = g2 * 2 + i
                    dve.tensor_tensor(y[:], XN[:, bass.ds(g * TPG + 1, TPG), :], rows4(bo), ALU.add)
                    dve.drain()
                    dve.wait_ge(gathered[i], g2 * (16 * TPG) + 16 * TPG)
                    dve.tensor_tensor(y[:], y[:], got[:, i, :, :], ALU.add)
                    dve.drain()
                    statistics(lambda n: y[:, n, :], g2 * 4 + (2 * i + 1), 1e-12)
                    for n in range(TPG):
                        dve.tensor_scalar(y[:, n, :], y[:, n, :], mv[:, n, 0:1], rs[:, n:n + 1], ALU.subtract, ALU.mult)
                    dve.drain()
                    dve.tensor_tensor(y[:], y[:], rows4(gamma), ALU.mult)
                    dve.drain()
                    dve.tensor_tensor(y[:], y[:], rows4(beta), ALU.add).then_inc(normed, 1)
                    dve.wait_ge(gate_ready, g + 1)
                    dve.tensor_tensor(gate[:], gate[:], X2[:, bass.ds(g * TPG + 1, TPG), :], ALU.mult)
                    dve.drain()
                    dve.wait_ge(x_loaded[i], g2 * 16 + 16)
                    dve.wait_ge(stored[i], g2 * 16 + 16)
                    dve.tensor_tensor(x1[:, i, :, :], xin[:, i, :, :], gate[:], ALU.add).then_inc(x1_ready, 1)
                    dve.drain()
                    statistics(lambda n: x1[:, i, n, :], g2 * 4 + (2 * i + 2), 1e-5)
                    for n in range(TPG):
                        dve.tensor_scalar(XN[:, g * TPG + (n + 1), :], x1[:, i, n, :], mv[:, n, 0:1], rs[:, n:n + 1],
                                          ALU.subtract, ALU.mult)
                    dve.drain()
                    for n in range(TPG):
                        dve.bn_stats(stats[:, n, :], XN[:, g * TPG + (n + 1), :])
                    dve.drain()
                    for n in range(TPG):
                        dve.bn_aggr(mv[:, n, :], stats[:, n, :])
                    dve.drain()
                    dve.tensor_copy(mv_all[:, bass.ds(g * TPG, TPG), :], mv[:])
                    dve.drain()

                with dve.Fori(0, NG // 2) as g2:
                    for i in range(2):
                        group(g2, i)
                dve.tensor_copy(keep.mean[:], mv_all[:, :, 0])
                dve.tensor_scalar(ve_all[:], mv_all[:, :, 1], 1e-5, None, ALU.add).then_inc(all_var_ready, 1)
                dve.wait_ge(rstd_ready, 2 * NG + 1)
        s.clear_semaphores()


def feed_forward(nc, io, keep, gated, layer=0):
    HID = int(D * 4 * 2 / 3) if gated else 4 * D
    IC = -(-HID // P)
    rows = [min(P, HID - m * P) for m in range(IC)]
    TOK = TPG * P
    RING = 2 if gated else 4
    with ExitStack() as ctx:
        s = Space(nc, ctx, "ffn" if gated else "mlp")
        XN, X2 = keep.XN, keep.X2
        W = 2 * HID if gated else HID
        w1 = s.sb("w1", [P, KC, W])
        w2 = s.sb("w2", [P, IC, D])
        b1 = s.sb("b1", [P, 1 + gated, IC])
        b2 = s.sb("b2", [P, D])
        gain, offset = s.sb("gain", [P, KC]), s.sb("offset", [P, KC])
        h = s.sb("h", [P, TPG, D])
        hT = s.sb("hT", [P, KC, TOK])
        inner = s.sb("inner", [P, IC, TOK])
        gel = s.sb("gel", [P, 2, TOK])
        result = s.sb("result", [P, TPG, D])
        stats, mv = s.sb("stats", [P, TPG, 6]), s.sb("mv", [P, TPG, 2])
        ve, rs = s.sb("ve", [P, TPG]), s.sb("rs", [P, TPG])
        turned = [s.ps(f"turned{c}") for c in range(KC)]
        hidden = [[s.ps(f"hidden{i}{k}") for k in range(1 + gated)] for i in range(RING)]
        out = [s.ps(f"out{i}") for i in range(2)]
        loaded, biases, h_loaded = s.sem("loaded"), s.sem("biases"), s.sem("h_loaded")
        var_ready, rstd_ready = s.sem("var_ready"), s.sem("rstd_ready")
        h_ready = s.count("h_ready", 1)
        turned_ready, hT_ready = s.count("turned_ready", KC), s.count("hT_ready", KC)
        hidden_ready, gel_ready = s.count("hidden_ready", IC), s.count("gel_ready", IC)
        inner_ready = s.count("inner_ready", IC, credit=RING)
        out_ready, out_taken = s.count("out_ready", TPG), s.count("out_taken", TPG, credit=2)
        stored = s.sem("stored")
        result_ready = s.sem("result_ready")
        with nc.Block() as block:
            @block.sync
            def _(sp):
                pre = "L1_ffn_" if gated else "L1_attn_"
                of = (lambda name: io[pre + name][layer]) if gated else (lambda name: io[pre + name])
                mine = (lambda name: io["ffn_" + name][layer]) if gated else (lambda name: io["mlp_" + name])
                whole = HID // P
                n = 0
                pairs = [(w1[:], of("w1").rearrange("(c p) n -> p c n", p=P)),
                         (w2[:, 0:whole, :], of("w2")[0:whole * P, :].rearrange("(c p) n -> p c n", p=P)),
                         (gain[:], mine("gain")), (offset[:], mine("offset")), (b1[:], mine("b1"))]
                if whole < IC:
                    pairs.append((w2[0:rows[-1], whole, :], of("w2")[whole * P:, :]))
                for dst, src in pairs:
                    sp.dma_start(dst, src).then_inc(loaded, 16)
                    n += 16
                n += load_bias_rows(sp, loaded, [(b2[:], of("b2"))])

                def load_h(g):
                    half = D // 2
                    sp.dma_start(h[:, :, 0:half], X2[:, bass.ds(g * TPG + 1, TPG), 0:half]).then_inc(h_loaded, 16)
                    sp.dma_start(h[1:P, :, half:], X2[0:P - 1, bass.ds(g * TPG + 1, TPG), half:]).then_inc(h_loaded, 16)
                    sp.dma_start(h[0:1, :, half:], X2[P - 1:P, bass.ds(g * TPG, TPG), half:]).then_inc(h_loaded, 16)

                if gated:
                    load_h(0)
                sp.wait_ge(loaded, n)
                sp.sem_inc(biases, 1)
                if gated:
                    with sp.Fori(1, NG) as g:
                        sp.wait_ge(turned_ready.sem, turned_ready.at(g, 0))
                        load_h(g)
                else:
                    groups = io["s1"].rearrange("(g n p) d -> g p n d", p=P, n=TPG)
                    with sp.Fori(0, NG) as g:
                        sp.wait_ge(result_ready, g + 1)
                        sp.dma_start(groups[g], result[:]).then_inc(stored, 16)
                    sp.wait_ge(stored, 16 * NG + 16)

            if gated:
                @block.gpsimd
                def _(pool):
                    with pool.Fori(0, NG) as g:
                        pool.wait_ge(var_ready, g + 1)
                        pool.tensor_tensor(rs[:], ve[:], keep.minus_half[:, 0:TPG], ALU.pow).then_inc(rstd_ready, 1)

            @block.tensor
            def _(pe):
                pe.wait_ge(biases, 1)

                def turn(g):
                    pe.wait_ge(h_ready.sem, h_ready.at(g, 1))
                    for c in range(KC):
                        for n in range(TPG):
                            last = pe.transpose(turned[c][:, n * P:(n + 1) * P], h[:, n, c * P:(c + 1) * P], keep.ident[:])
                        last.then_inc(turned_ready.sem, 1)

                def hide(g):
                    pe.wait_ge(hT_ready.sem, hT_ready.at(g, KC))
                    for m in range(IC):
                        pe.wait_ge(inner_ready.sem, inner_ready.at(g, m + 1 - RING))
                        for k in range(1 + gated):
                            for c in range(KC):
                                a = k * HID + m * P
                                last = pe.matmul(hidden[m % RING][k][0:rows[m], :], w1[:, c, a:a + rows[m]], hT[:, c, :],
                                                 start=(c == 0), stop=(c == KC - 1))
                        last.then_inc(hidden_ready.sem, 1)

                def project(g):
                    pe.wait_ge(inner_ready.sem, inner_ready.at(g, IC))
                    for n in range(TPG):
                        pe.wait_ge(out_taken.sem, out_taken.at(g, n - 1))
                        for m in range(IC):
                            last = pe.matmul(out[n % 2][:, 0:D],
                                             inner[0:rows[m], m, n * P:(n + 1) * P], w2[0:rows[m], m, :],
                                             start=(m == 0), stop=(m == IC - 1))
                        last.then_inc(out_ready.sem, 1)

                turn(0)
                with pe.Fori(0, NG - 1) as g:
                    hide(g)
                    turn(g + 1)
                    project(g)
                hide(NG - 1)
                project(NG - 1)

            @block.scalar
            def _(act):
                if not gated:
                    act.sem_inc(inner_ready.sem, RING)
                act.wait_ge(biases, 1)

                def take_turned(g):
                    for c in range(KC):
                        act.wait_ge(turned_ready.sem, turned_ready.at(g, c + 1))
                        act.activation(hT[:, c, :], turned[c][:], ACT.Identity, bias=offset[:, c:c + 1],
                                       scale=gain[:, c:c + 1]).then_inc(hT_ready.sem, 1)

                def gelus(g):
                    for m in range(IC):
                        act.wait_ge(hidden_ready.sem, hidden_ready.at(g, m + 1))
                        if gated:
                            act.wait_ge(inner_ready.sem, inner_ready.at(g, m + 1 - RING))
                            act.activation(gel[0:rows[m], m % 2, :], hidden[m % RING][1][0:rows[m], :], ACT.Gelu,
                                           bias=b1[0:rows[m], 1, m:m + 1]).then_inc(gel_ready.sem, 1)
                        else:
                            act.activation(inner[:, m, :], hidden[m % RING][0][:], ACT.Gelu,
                                           bias=b1[:, 0, m:m + 1]).then_inc(inner_ready.sem, 1)

                take_turned(0)
                with act.Fori(0, NG - 1) as g:
                    gelus(g)
                    take_turned(g + 1)
                gelus(NG - 1)

            @block.vector
            def _(dve):
                dve.sem_inc(out_taken.sem, out_taken.credit)
                if gated:
                    dve.sem_inc(inner_ready.sem, RING)
                else:
                    dve.sem_inc(stored, 16)
                dve.wait_ge(biases, 1)

                def make_h(g, first):
                    if gated:
                        dve.wait_ge(h_loaded, g * 48 + 48)
                        dve.tensor_scalar(h[0:1, 0, D // 2:], h[0:1, 0, D // 2:], keep.going[0:1, bass.ds(g, 1)], None, ALU.mult)
                        dve.drain()
                        for n in range(TPG):
                            dve.bn_stats(stats[:, n, :], h[:, n, :])
                        dve.drain()
                        for n in range(TPG):
                            dve.bn_aggr(mv[:, n, :], stats[:, n, :])
                        dve.drain()
                        dve.tensor_scalar(ve[:], mv[:, :, 1], 1e-5, None, ALU.add).then_inc(var_ready, 1)
                        dve.wait_ge(rstd_ready, g + 1)
                        for n in range(TPG):
                            dve.tensor_scalar(h[:, n, :], h[:, n, :], mv[:, n, 0:1], rs[:, n:n + 1], ALU.subtract, ALU.mult)
                    else:
                        if not first:
                            dve.wait_ge(turned_ready.sem, turned_ready.at(g, 0))
                        for n in range(TPG):
                            t = g * TPG + n
                            dve.tensor_scalar(h[:, n, :], X2[:, g * TPG + (n + 1), :], keep.mean[:, bass.ds(t, 1)],
                                              keep.rstd[:, bass.ds(t, 1)], ALU.subtract, ALU.mult)
                    dve.drain()
                    dve.sem_inc(h_ready.sem, 1)

                def multiply(g):
                    for m in range(IC):
                        dve.wait_ge(gel_ready.sem, gel_ready.at(g, m + 1))
                        dve.scalar_tensor_tensor(inner[0:rows[m], m, :], hidden[m % RING][0][0:rows[m], :],
                                                 b1[0:rows[m], 0, m:m + 1], gel[0:rows[m], m % 2, :],
                                                 ALU.add, ALU.mult).then_inc(inner_ready.sem, 1)

                def take_out(g):
                    if not gated:
                        dve.wait_ge(stored, g * 16 + 16)
                    for n in range(TPG):
                        dve.wait_ge(out_ready.sem, out_ready.at(g, n + 1))
                        dve.tensor_tensor(result[:, n, :], out[n % 2][:, 0:D], b2[:], ALU.add)\
                           .then_inc(out_taken.sem, 1)
                    dve.drain()
                    slots = bass.ds(g * TPG + 1, TPG)
                    if gated:
                        dve.tensor_tensor(XN[:, slots, :], result[:], X2[:, slots, :], ALU.add)
                        dve.drain()
                    else:
                        dve.tensor_tensor(result[:], result[:], X2[:, slots, :], ALU.add).then_inc(result_ready, 1)

                make_h(0, True)
                with dve.Fori(0, NG - 1) as g:
                    make_h(g + 1, False)
                    if gated:
                        multiply(g)
                    take_out(g)
                if gated:
                    multiply(NG - 1)
                take_out(NG - 1)
        s.clear_semaphores()


RH, RD = 8, 64
RI = RH * RD


def rotary_attention(nc, io, keep, layer):
    ST = RH // 2
    U = ST * TPG
    before = [("hT", 0), ("q", 0), ("k", 0), ("v", 0), ("QT", 0), ("KT", 0), ("hT", 1), ("q", 1), ("k", 1), ("v", 1)]
    plan = {0: (("hT", 2), ("QT", 1)), 1: (("KT", 1), ("q", 2)), 2: (("oT", -1), ("k", 2)), 3: (("out", -1), ("v", 2))}
    linear = [(-1, 0, name, n) for name, n in before]
    for step in range(U + ST):
        for half, (name, ahead) in enumerate(plan[step % ST]):
            if 0 <= step // ST + ahead < TPG and (step < U or ahead < 0):
                linear.append((step, half, name, step // ST + ahead))
    order = [(name, n) for _, _, name, n in linear]
    NACT = sum(name != "out" for name, _ in order)
    NDVE = len(order) - NACT

    with ExitStack() as ctx:
        s = Space(nc, ctx, "rot")
        XN, X2 = keep.XN, keep.X2
        w_qkv = s.sb("w_qkv", [P, KC, 3 * RI])
        w_out = s.sb("w_out", [P, RI // P, D])
        scales = s.sb("scales", [P, 2, RD])
        NTAB = SEQ // P + 2
        cos, sin = s.sb("cos", [P, 2, NTAB, RD]), s.sb("sin", [P, 2, NTAB, RD])
        mask = s.sb("mask", [P, NG, 2 * P], BF16)
        h = s.sb("h", [P, TPG, D])
        hT = s.sb("hT", [P, KC, P])
        qk = s.sb("qk", [P, 2, RI])
        square, turn_a = s.sb("square", [P, 2, RI]), s.sb("turn_a", [P, 2, RI])
        rot = s.sb("rot", [P, 2, RI])
        ss, rnorm = s.sb("ss", [P, 2 * RH]), s.sb("rnorm", [P, 2 * RH])
        QT, KT = s.sb("QT", [P, 2, 4, P]), s.sb("KT", [P, 4, (TPG + 1) * P])
        V = s.sb("V", [P, TPG + 1, RI])
        probs, probsT = s.sb("probs", [P, 2, BANK]), s.sb("probsT", [P, 2, BANK])
        negmax = s.sb("negmax", [P, 4, 2])
        sums, rsum = s.sb("sums", [P, 2, RH]), s.sb("rsum", [P, RH])
        attn, oT = s.sb("attn", [P, RI]), s.sb("oT", [P, RI // P, P])
        score = [s.ps(f"score{i}") for i in range(4)]
        turned = [s.ps(f"turned{i}") for i in range(2)]
        po, lin = s.ps("po"), s.ps("lin")

        loaded, biases, h_loaded, zeroed = s.sem("loaded"), s.sem("biases"), s.sem("h_loaded"), s.sem("zeroed")
        h_ready = s.count("h_ready", 1)
        lin_ready = s.count("lin_ready", len(order))
        act_took, dve_took = s.count("act_took", NACT), s.count("dve_took", NDVE, credit=1)
        scores_ready, max_ready = s.count("scores_ready", U), s.count("max_ready", U)
        probs_ready = s.count("probs_ready", U, credit=4)
        turned_ready, probsT_ready = s.count("turned_ready", U, credit=2), s.count("probsT_ready", U, credit=2)
        pv_done = s.count("pv_done", U, credit=2)
        attn_ready = s.count("attn_ready", TPG, credit=1)
        squared, ss_ready, rn_ready = s.count("squared", TPG), s.count("ss_ready", TPG), s.count("rn_ready", TPG)
        normed, turned_a, rot_ready = s.count("normed", TPG), s.count("turned_a", TPG), s.count("rot_ready", TPG)

        def taken(name, n):
            upto = order[:order.index((name, n)) + 1]
            acts = sum(x != "out" for x, _ in upto)
            return (act_took, acts) if name != "out" else (dve_took, len(upto) - acts)

        def heads_of(u):
            n, i = divmod(u, ST)
            return n, [4 * (i // 2) + i % 2, 4 * (i // 2) + i % 2 + 2]

        with nc.Block() as block:
            @block.sync
            def _(sp):
                n = 0
                pairs = [(w_qkv[:], io["L1_ffn_wqkv"][layer].rearrange("(c p) n -> p c n", p=P)),
                         (w_out[:], io["L1_ffn_wo"][layer].rearrange("(c p) n -> p c n", p=P)),
                         (cos[:], io["const_cos"]), (sin[:], io["const_sin"]), (mask[:], io["const_mask2"])]
                for dst, src in pairs:
                    sp.dma_start(dst, src).then_inc(loaded, 16)
                    n += 16
                n += load_bias_rows(sp, loaded, [(scales[:, 0, :], io["L1_ffn_q_scale"][layer]),
                                                 (scales[:, 1, :], io["L1_ffn_k_scale"][layer])])

                def load_h(g):
                    half = D // 2
                    sp.dma_start(h[:, :, 0:half], XN[:, bass.ds(g * TPG + 1, TPG), 0:half]).then_inc(h_loaded, 16)
                    sp.dma_start(h[1:P, :, half:], XN[0:P - 1, bass.ds(g * TPG + 1, TPG), half:]).then_inc(h_loaded, 16)
                    sp.dma_start(h[0:1, :, half:], XN[P - 1:P, bass.ds(g * TPG, TPG), half:]).then_inc(h_loaded, 16)

                load_h(0)
                sp.wait_ge(loaded, n)
                sp.sem_inc(biases, 1)
                with sp.Fori(1, NG) as g:
                    sp.wait_ge(lin_ready.sem, lin_ready.at(g - 1, order.index(("hT", TPG - 1)) + 1))
                    load_h(g)

            @block.gpsimd
            def _(pool):
                pool.memset(KT[:, :, TPG * P:], 0.0)
                pool.memset(V[:, TPG, :], 0.0)
                pool.memset(X2[:, 0, :], 0.0)
                pool.drain()
                pool.sem_inc(zeroed, 1)
                pool.wait_ge(biases, 1)
                by_head = lambda t, i: t[:, i, :].rearrange("p (h d) -> p h d", d=RD)

                def rotate(it, gi, n):
                    c, k = taken("k", n)
                    pool.wait_ge(c.sem, c.at(it, k))
                    pool.tensor_tensor(square[:], qk[:], qk[:], ALU.mult).then_inc(squared.sem, 1)
                    pool.wait_ge(ss_ready.sem, ss_ready.at(it, n + 1))
                    pool.tensor_tensor(rnorm[:], ss[:], keep.minus_half[:, 0:2 * RH], ALU.pow).then_inc(rn_ready.sem, 1)
                    pool.wait_ge(normed.sem, normed.at(it, n + 1))
                    for i in range(2):
                        last = pool.tensor_tensor(by_head(turn_a, i), by_head(qk, i),
                                                  cos[:, i, bass.ds(gi * TPG + n, 1), :].to_broadcast([P, RH, RD]),
                                                  ALU.mult)
                    last.then_inc(turned_a.sem, 1)

                with pool.Fori(0, BATCH) as b:
                    with pool.Fori(0, GPB) as gi:
                        for n in range(TPG):
                            rotate(b * GPB + gi, gi, n)

            @block.tensor
            def _(pe):
                pe.sem_inc(turned_ready.sem, turned_ready.credit)
                pe.sem_inc(pv_done.sem, pv_done.credit)
                pe.wait_ge(biases, 1)

                def linear_step(it, name, n):
                    i = order.index((name, n))
                    if i == 0:
                        pe.wait_ge(dve_took.sem, dve_took.at(it, 0))
                    else:
                        c, k = taken(*order[i - 1])
                        pe.wait_ge(c.sem, c.at(it, k))
                    if name == "hT":
                        if n == 0:
                            pe.wait_ge(h_ready.sem, h_ready.at(it, 1))
                        for c in range(KC):
                            last = pe.transpose(lin[:, c * P:(c + 1) * P], h[:, n, c * P:(c + 1) * P], keep.ident[:])
                    elif name in ("q", "k", "v"):
                        c, k = taken("hT", n)
                        pe.wait_ge(c.sem, c.at(it, k))
                        a = "qkv".index(name) * RI
                        for c in range(KC):
                            last = pe.matmul(lin[:], hT[:, c, :], w_qkv[:, c, a:a + RI], start=(c == 0), stop=(c == KC - 1))
                    elif name in ("QT", "KT"):
                        pe.wait_ge(rot_ready.sem, rot_ready.at(it, n + 1))
                        for c in range(4):
                            last = pe.transpose(lin[:, c * P:(c + 1) * P], rot[:, "QK".index(name[0]), c * P:(c + 1) * P],
                                                keep.ident[:])
                    elif name == "oT":
                        pe.wait_ge(attn_ready.sem, attn_ready.at(it, n + 1))
                        for c in range(RI // P):
                            last = pe.transpose(lin[:, c * P:(c + 1) * P], attn[:, c * P:(c + 1) * P], keep.ident[:])
                    else:
                        c, k = taken("oT", n)
                        pe.wait_ge(c.sem, c.at(it, k))
                        for c in range(RI // P):
                            last = pe.matmul(lin[:, 0:D], oT[:, c, :], w_out[:, c, :], start=(c == 0), stop=(c == RI // P - 1))
                    last.then_inc(lin_ready.sem, 1)

                def scores(it, g, u):
                    n, heads = heads_of(u)
                    bank = score[u % 4]
                    pe.wait_ge(probs_ready.sem, probs_ready.at(it, u - 3))
                    if u % ST == 0:
                        c, k = taken("KT", n)
                        pe.wait_ge(c.sem, c.at(it, k))
                    m = mask[:, bass.ds(g, 1), :] if n == 0 else mask[:, 1:2, :]
                    pe.matmul(bank[:], keep.identb[:], m.to_broadcast([P, 2, 2 * P]), start=True, stop=False)
                    for j in range(2):
                        c, half = divmod(heads[j], 2)
                        rows = slice(RD * half, RD * (half + 1))
                        last = pe.matmul(bank[:, j * 2 * P:(j + 1) * 2 * P], QT[rows, n % 2, c, :],
                                         KT[rows, c, n * P:(n + 2) * P], start=False, stop=(j == 1))
                    last.then_inc(scores_ready.sem, 1)

                def turn(it, u):
                    pe.wait_ge(probs_ready.sem, probs_ready.at(it, u + 1))
                    pe.wait_ge(probsT_ready.sem, probsT_ready.at(it, u - 1))
                    for i in range(4):
                        last = pe.transpose(turned[u % 2][:, i * P:(i + 1) * P], probs[:, u % 2, i * P:(i + 1) * P], keep.ident[:])
                    last.then_inc(turned_ready.sem, 1)

                def weigh(it, u):
                    n, heads = heads_of(u)
                    pe.wait_ge(probsT_ready.sem, probsT_ready.at(it, u + 1))
                    if u % ST == 0:
                        pe.wait_ge(attn_ready.sem, attn_ready.at(it, n))
                        c, k = taken("v", n)
                        pe.wait_ge(c.sem, c.at(it, k))
                    for j in range(2):
                        a = heads[j] * RD
                        for kb in range(2):
                            last = pe.matmul(po[:, a:a + RD], probsT[:, u % 2, (2 * j + kb) * P:(2 * j + kb + 1) * P],
                                             V[:, n + kb, a:a + RD], start=(kb == 0), stop=(kb == 1))
                    last.then_inc(pv_done.sem, 1)

                with pe.Fori(0, NG) as g:
                    for name, n in before:
                        linear_step(g, name, n)
                    scores(g, g, 0)
                    scores(g, g, 1)
                    for step in range(U + ST):
                        for half in range(2):
                            for at, hf, name, n in linear:
                                if at == step and hf == half:
                                    linear_step(g, name, n)
                            if half == 0 and step + 2 < U:
                                scores(g, g, step + 2)
                        if step < U:
                            turn(g, step)
                        if 1 <= step <= U:
                            weigh(g, step - 1)

            @block.scalar
            def _(act):
                act.sem_inc(probs_ready.sem, probs_ready.credit)
                act.wait_ge(biases, 1)

                def take(it, name, n):
                    act.wait_ge(lin_ready.sem, lin_ready.at(it, order.index((name, n)) + 1))
                    if name == "hT":
                        last = act.activation(hT[:].rearrange("p c n -> p (c n)"), lin[:, 0:D], ACT.Copy)
                    elif name in ("q", "k"):
                        last = act.activation(qk[:, "qk".index(name), :], lin[:], ACT.Copy)
                    elif name == "v":
                        last = act.activation(V[:, n + 1, :], lin[:], ACT.Copy)
                    elif name == "QT":
                        last = act.activation(QT[:, n % 2, :, :].rearrange("p c n -> p (c n)"), lin[:], ACT.Copy)
                    elif name == "KT":
                        last = act.activation(KT[:, :, (n + 1) * P:(n + 2) * P], lin[:].rearrange("p (c n) -> p c n", c=4),
                                              ACT.Copy)
                    else:
                        last = act.activation(oT[:].rearrange("p c n -> p (c n)"), lin[:], ACT.Copy)
                    last.then_inc(act_took.sem, 1)

                def softmax(it, u):
                    n, heads = heads_of(u)
                    act.wait_ge(max_ready.sem, max_ready.at(it, u + 1))
                    act.wait_ge(turned_ready.sem, turned_ready.at(it, u - 1))
                    for j in range(2):
                        a = heads[j]
                        last = act.activation(probs[:, u % 2, j * 2 * P:(j + 1) * 2 * P],
                                              score[u % 4][:, j * 2 * P:(j + 1) * 2 * P], ACT.Exp,
                                              bias=negmax[:, u % 4, j:j + 1], accum_out=sums[:, n % 2, a:a + 1])
                    last.then_inc(probs_ready.sem, 1)

                with act.Fori(0, NG) as g:
                    act.wait_ge(h_ready.sem, h_ready.at(g, 1))
                    for name, n in before:
                        take(g, name, n)
                    softmax(g, 0)
                    softmax(g, 1)
                    for step in range(U + ST):
                        for half in range(2):
                            for at, hf, name, n in linear:
                                if at == step and hf == half and name != "out":
                                    take(g, name, n)
                            if half == 0 and step + 2 < U:
                                softmax(g, step + 2)

            @block.vector
            def _(dve):
                dve.sem_inc(dve_took.sem, dve_took.credit)
                dve.sem_inc(probsT_ready.sem, probsT_ready.credit)
                dve.sem_inc(attn_ready.sem, attn_ready.credit)
                dve.wait_ge(biases, 1)
                dve.wait_ge(zeroed, 1)
                half = RD // 2
                for i in range(2):
                    sc = lambda a, b: scales[:, i:i + 1, a:b].to_broadcast([P, NTAB, b - a])
                    dve.tensor_tensor(cos[:, i, :, :], cos[:, i, :, :], sc(0, RD), ALU.mult)
                    dve.tensor_tensor(sin[:, i, :, 0:half], sin[:, i, :, 0:half], sc(half, RD), ALU.mult)
                    dve.tensor_tensor(sin[:, i, :, half:], sin[:, i, :, half:], sc(0, half), ALU.mult)
                dve.drain()
                dve.sem_inc(biases, 1)

                def rotate(it, gi, n):
                    by = lambda t, i, a, b: t[:, i, :].rearrange("p (h d) -> p h d", d=RD)[:, :, a:b]
                    every = lambda t: t[:].rearrange("p i (h d) -> p (i h) d", d=RD)
                    dve.wait_ge(squared.sem, squared.at(it, n + 1))
                    dve.tensor_reduce(ss[:], every(square), AX.X, ALU.add)
                    dve.drain()
                    dve.tensor_scalar(ss[:], ss[:], 1e-24, None, ALU.max).then_inc(ss_ready.sem, 1)
                    dve.wait_ge(rn_ready.sem, rn_ready.at(it, n + 1))
                    dve.tensor_tensor(every(qk), every(qk), bcast(rnorm[:], [P, 2 * RH, RD]), ALU.mult).then_inc(normed.sem, 1)
                    dve.drain()
                    table = lambda i, a, b: sin[:, i, bass.ds(gi * TPG + n, 1), a:b].to_broadcast([P, RH, b - a])
                    for i in range(2):
                        dve.tensor_tensor(by(rot, i, 0, half), by(qk, i, half, RD), table(i, 0, half), ALU.mult)
                        dve.tensor_tensor(by(rot, i, half, RD), by(qk, i, 0, half), table(i, half, RD), ALU.mult)
                    dve.drain()
                    dve.wait_ge(turned_a.sem, turned_a.at(it, n + 1))
                    dve.tensor_tensor(rot[:], rot[:], turn_a[:], ALU.add).then_inc(rot_ready.sem, 1)

                def maxima(it, u):
                    dve.wait_ge(scores_ready.sem, scores_ready.at(it, u + 1))
                    dve.tensor_reduce(negmax[:, u % 4, :], score[u % 4][:].rearrange("p (h k) -> p h k", h=2),
                                      AX.X, ALU.max, negate=True).then_inc(max_ready.sem, 1)

                def take_turned(it, u):
                    dve.wait_ge(turned_ready.sem, turned_ready.at(it, u + 1))
                    dve.wait_ge(pv_done.sem, pv_done.at(it, u - 1))
                    dve.tensor_copy(probsT[:, u % 2, :], turned[u % 2][:]).then_inc(probsT_ready.sem, 1)

                def normalise(it, n):
                    dve.wait_ge(pv_done.sem, pv_done.at(it, (n + 1) * ST))
                    dve.reciprocal(rsum[:], sums[:, n % 2, :])
                    dve.drain()
                    dve.tensor_tensor(attn[:].rearrange("p (h d) -> p h d", d=RD), po[:].rearrange("p (h d) -> p h d", d=RD),
                                      bcast(rsum[:], [P, RH, RD]), ALU.mult).then_inc(attn_ready.sem, 1)

                def take_out(it, g, n):
                    dve.wait_ge(lin_ready.sem, lin_ready.at(it, order.index(("out", n)) + 1))
                    dve.tensor_tensor(X2[:, g * TPG + (n + 1), :], lin[:, 0:D], XN[:, g * TPG + (n + 1), :], ALU.add)\
                       .then_inc(dve_took.sem, 1)

                def group(it, gi):
                    dve.wait_ge(h_loaded, it * 48 + 48)
                    dve.tensor_scalar(h[0:1, 0, D // 2:], h[0:1, 0, D // 2:], keep.going[0:1, bass.ds(it, 1)], None, ALU.mult)
                    dve.tensor_copy(KT[:, :, 0:P], KT[:, :, TPG * P:])
                    dve.tensor_copy(V[:, 0, :], V[:, TPG, :])
                    dve.drain()
                    dve.sem_inc(h_ready.sem, 1)
                    rotate(it, gi, 0)
                    rotate(it, gi, 1)
                    maxima(it, 0)
                    maxima(it, 1)
                    for step in range(U + ST):
                        for at, _, name, n in linear:
                            if at == step and name == "out":
                                take_out(it, it, n)
                        if step + 2 < U:
                            maxima(it, step + 2)
                        if step < U:
                            take_turned(it, step)
                        if step % ST == 0 and step > 0:
                            normalise(it, step // ST - 1)
                        for at, _, name, n in linear:
                            if at == step and name == "k":
                                rotate(it, gi, n)

                with dve.Fori(0, BATCH) as b:
                    with dve.Fori(0, GPB) as gi:
                        group(b * GPB + gi, gi)
        s.clear_semaphores()


def combine(nc, io, keep):
    with ExitStack() as ctx:
        s = Space(nc, ctx, "comb")
        x1, s1 = s.sb("x1", [P, 2, TPG, D]), s.sb("s1", [P, 2, TPG, D])
        gate = s.sb("gate", [P, 2, TPG, D])
        x_loaded = [s.sem(f"x_loaded{i}") for i in range(2)]
        stored = [s.sem(f"stored{i}") for i in range(2)]
        gate_ready, result_ready = s.sem("gate_ready"), s.sem("result_ready")
        by_group = lambda name: io[name].rearrange("(g n p) d -> g p n d", p=P, n=TPG)
        with nc.Block() as block:
            @block.sync
            def _(sp):
                def load(g, i):
                    sp.dma_start(x1[:, i, :, :], by_group("x1")[g]).then_inc(x_loaded[i], 16)
                    sp.dma_start(s1[:, i, :, :], by_group("s1")[g]).then_inc(x_loaded[i], 16)

                for i in range(2):
                    load(i, i)
                def store(g2, i):
                    sp.wait_ge(result_ready, g2 * 2 + (i + 1))
                    sp.dma_start(by_group("out")[g2 * 2 + i], gate[:, i, :, :]).then_inc(stored[i], 16)

                with sp.Fori(0, NG // 2 - 1) as g2:
                    for i in range(2):
                        store(g2, i)
                        load(g2 * 2 + (i + 2), i)
                for i in range(2):
                    store(NG // 2 - 1, i)
                for i in range(2):
                    sp.wait_ge(stored[i], 16 * (NG // 2 + 1))

            @block.scalar
            def _(act):
                for i in range(2):
                    act.sem_inc(stored[i], 16)
                with act.Fori(0, NG // 2) as g2:
                    for i in range(2):
                        act.wait_ge(stored[i], g2 * 16 + 16)
                        act.activation(gate[:, i, :, :], keep.XN[:, bass.ds(g2 * (2 * TPG) + (i * TPG + 1), TPG), :],
                                       ACT.Silu).then_inc(gate_ready, 1)

            @block.vector
            def _(dve):
                with dve.Fori(0, NG // 2) as g2:
                    for i in range(2):
                        dve.wait_ge(gate_ready, g2 * 2 + (i + 1))
                        dve.wait_ge(x_loaded[i], g2 * 32 + 32)
                        dve.tensor_tensor(gate[:, i, :, :], gate[:, i, :, :], s1[:, i, :, :], ALU.mult)
                        dve.drain()
                        dve.tensor_tensor(gate[:, i, :, :], gate[:, i, :, :], x1[:, i, :, :], ALU.add)\
                           .then_inc(result_ready, 1)


def build(nc, io):
    rows = [SLOT_TILES * P, D]
    for name, shape in (("rows_in", rows), ("rows_out", rows), ("x1", [NT * P, D]), ("s1", [NT * P, D])):
        io[name] = nc.dram_tensor("scratch_" + name, shape, F32).ap()
    with ExitStack() as ctx:
        keep = Keep(nc, ctx)
        normalise_input(nc, io, keep)
        window_attention(nc, io, keep, 0)
        route(nc, io, keep)
        experts(nc, io, keep)
        finish_layer0(nc, io, keep)
        window_attention(nc, io, keep, 1)
        feed_forward(nc, io, keep, False)
        with nc.Fori(0, 2) as layer:
            rotary_attention(nc, io, keep, layer)
            feed_forward(nc, io, keep, True, layer)
        combine(nc, io, keep)


def layouts(inputs):
    def columns(v):
        c = -(-v.shape[0] // P)
        out = np.zeros((c * P,), v.dtype)
        out[:v.shape[0]] = v
        return out.reshape(c, P).T

    def heads_down(v):
        out = np.zeros((4, 32, v.shape[0] // 64), v.dtype)
        out[:, 0:HD, :] = v.reshape(-1, 4, HD).transpose(1, 2, 0)
        return out.reshape(P, -1)

    def heads_apart(w):
        out = np.zeros((P, KC, w.shape[1] // HD, 32), w.dtype)
        out[:, :, :, 0:HD] = w.reshape(KC, P, -1, HD).transpose(1, 0, 2, 3)
        return out

    x = {name: np.asarray(a) for name, a in inputs.items()}
    a = {"w_router": x["L0_ffn_Wr"].T.reshape(KC, P, EXPERTS).transpose(1, 0, 2),
         "win0_w_rq": heads_apart(x["L0_attn_rq_w"]), "win0_w_rk": heads_apart(x["L0_attn_rkv_w"][:, 0:LAT]),
         "win0_b_rq": heads_down(x["L0_attn_rq_b"]), "win0_b_rk": heads_down(x["L0_attn_rkv_b"][0:LAT]),
         "win1_gain": columns(x["L1_attn_ln1_g"]), "win1_offset": columns(x["L1_attn_ln1_b"]),
         "mlp_gain": columns(x["L1_attn_ln2_g"]), "mlp_offset": columns(x["L1_attn_ln2_b"]),
         "mlp_b1": columns(x["L1_attn_b1"])[:, None, :]}
    for layer, (w, b) in enumerate((("L0_attn_qkv_w", "L0_attn_qkv_b"), ("L1_attn_w_qkv", "L1_attn_b_qkv"))):
        a[f"win{layer}_w_qk"] = heads_apart(x[w][:, 0:2 * D])
        a[f"win{layer}_b_qk"] = heads_down(x[b][0:2 * D])
    a["ffn_gain"] = np.stack([columns(v) for v in x["L1_ffn_ln_g"]])
    a["ffn_offset"] = np.stack([columns(v) for v in x["L1_ffn_ln_b"]])
    a["ffn_b1"] = np.stack([np.stack([columns(half) for half in np.split(v, 2)], axis=1) for v in x["L1_ffn_b1"]])
    return {name: np.ascontiguousarray(v) for name, v in a.items()}


def constants():
    bf16 = mybir.dt.np(BF16)
    c = {}
    q, k = np.arange(P)[:, None], np.arange(P)[None, :]
    c["ident"] = np.eye(P, dtype=np.float32)
    c["identb"] = np.eye(P).astype(bf16)
    c["earlier"] = (q < k).astype(bf16)
    first = np.arange(NG) % GPB == 0
    c["going"] = np.broadcast_to(np.where(first, 0.0, 1.0), (P, NG)).astype(np.float32)
    c["iota"] = np.broadcast_to(np.arange(SLOT_TILES), (P, SLOT_TILES)).astype(np.float32)

    def window(prev, cur, closed_at_start):
        m = np.zeros((P, NG, 2 * P))
        for g in range(NG):
            m[:, g, 0:P] = np.where(prev & ~(closed_at_start & first[g]), 0.0, NEG)
            m[:, g, P:] = np.where(cur, 0.0, NEG)
        return m.astype(bf16)

    c["mask0"] = window((k >= q) & (k >= 1), k < q, True)
    c["mask1"] = window((k >= P // 2) & (q < P // 2), k <= q, False)
    c["mask2"] = window(k >= q, k <= q, True)
    tile = np.arange(NT) % (SEQ // P)
    chunk = tile[None, :, None] * LPT + (np.arange(P) // CHUNK)[:, None, None]
    c["lat_mask"] = np.where(np.arange(LAT)[None, None, :] < chunk, 0.0, NEG).astype(bf16)
    valid = np.ones((P, NG, 2), np.float32)
    valid[0, first, 0] = 0.0
    valid[0:CHUNK, first, 1] = 0.0
    c["valid"] = valid

    f = np.float32
    half = np.arange(0, RD, 2, dtype=f)
    inv_freq = f(1.0) / np.power(f(10000.0), half / f(RD))
    t = np.arange(SEQ, dtype=f)
    freqs = t[:, None] * inv_freq[None, :]
    base = (half + f(0.4 * RD)) / f(1.4 * RD)
    power = (t - f(SEQ // 2)) / f(P // 2)
    scale = np.power(base[None, :], power[:, None])
    cos, sin = np.cos(freqs), np.sin(freqs)
    two = lambda a, b: np.concatenate([a, b], axis=-1)
    tables = {"cos": (two(cos * scale, cos * scale) * f(8.0), two(cos / scale, cos / scale)),
              "sin": (two(-sin * scale, sin * scale) * f(8.0), two(-sin / scale, sin / scale))}
    for name, pair in tables.items():
        a = np.stack([x.reshape(SEQ // P, P, RD) for x in pair]).transpose(2, 0, 1, 3)
        c[name] = np.ascontiguousarray(np.concatenate([a, a[:, :, 0:2]], axis=2)).astype(f)
    return {f"const_{k}": np.ascontiguousarray(v) for k, v in c.items()}


_INS = ["L0_attn_x", "L0_attn_qkv_w", "L0_attn_qkv_b", "L0_attn_rq_w", "L0_attn_rq_b", "L0_attn_rkv_w", "L0_attn_rkv_b",
        "L0_attn_rout_w", "L0_attn_rout_b", "L0_attn_out_w", "L0_attn_out_b", "L0_attn_gl_w", "L0_attn_gr_w", "L0_ffn_Wr",
        "L0_ffn_W1", "L0_ffn_b1", "L0_ffn_Wo", "L0_ffn_bo", "L0_ffn_gamma", "L0_ffn_beta", "L1_attn_ln1_g",
        "L1_attn_ln1_b", "L1_attn_w_qkv", "L1_attn_b_qkv", "L1_attn_w_out", "L1_attn_b_out", "L1_attn_ln2_g",
        "L1_attn_ln2_b", "L1_attn_w1", "L1_attn_b1", "L1_attn_w2", "L1_attn_b2", "L1_ffn_wqkv", "L1_ffn_q_scale",
        "L1_ffn_k_scale", "L1_ffn_wo", "L1_ffn_ln_g", "L1_ffn_ln_b", "L1_ffn_w1", "L1_ffn_b1", "L1_ffn_w2", "L1_ffn_b2"]


def kernel(**inputs):
    import concourse.bacc as bacc
    from concourse.bass_utils import run_bass_kernel_spmd

    nc = bacc.Bacc("TRN2", target_bir_lowering=False, num_devices=1)
    arrays = {name: np.ascontiguousarray(inputs[name]) for name in _INS}
    arrays.update(layouts(inputs))
    arrays.update(constants())
    io = {name: nc.dram_tensor("in_" + name, a.shape, mybir.dt.from_np(a.dtype), kind="ExternalInput").ap()
          for name, a in arrays.items()}
    out = nc.dram_tensor("out", (BATCH, SEQ, D), F32, kind="ExternalOutput").ap()
    io["out"] = out.rearrange("b n d -> (b n) d")
    build(nc, io)
    r = run_bass_kernel_spmd(nc, [{"in_" + name: a for name, a in arrays.items()}], core_ids=[0])
    return r.results[0]["out"]
```

```python
from contextlib import ExitStack

import numpy as np
import concourse.bass as bass
from concourse import mybir

F32 = mybir.dt.float32
BF16 = mybir.dt.bfloat16
U32 = mybir.dt.uint32
ALU = mybir.AluOpType
ACT = mybir.ActivationFunctionType
AX = mybir.AxisListType

P = 128
D = 256
KC = D // P
BATCH, SEQ = 2, 2048
NT = BATCH * SEQ // P
TPG = 4
NG = NT // TPG
GPB = SEQ // P // TPG
BANK = 512
NEG = -1.0e30
EXPERTS, INNER = 8, 1024
SLOT_TILES = NT + EXPERTS


class Count:

    def __init__(self, sem, per, credit=0):
        self.sem, self.per, self.credit = sem, per, credit

    def at(self, it, k):
        return it * self.per + (k + self.credit)


class Space:

    def __init__(self, nc, ctx, stage):
        self.nc, self.ctx, self.stage = nc, ctx, stage
        self.sems = []

    def sb(self, name, shape, dt=F32):
        return self.ctx.enter_context(self.nc.sbuf_tensor(f"{self.stage}_{name}", shape, dt))

    def ps(self, name, shape=(P, BANK), dt=F32):
        return self.ctx.enter_context(self.nc.psum_tensor(f"{self.stage}_{name}", list(shape), dt))

    def sem(self, name):
        self.sems.append(self.ctx.enter_context(self.nc.semaphore(f"{self.stage}_{name}")))
        return self.sems[-1]

    def clear_semaphores(self):
        with self.nc.Block() as block:
            @block.gpsimd
            def _(pool):
                for sem in self.sems:
                    pool.sem_clear(sem)

    def count(self, name, per, credit=0):
        return Count(self.sem(name), per, credit)


def bcast(row, shape):
    return row.unsqueeze(2).to_broadcast(shape)


def load_bias_rows(sp, done, pairs):
    for dst, src in pairs:
        sp.dma_start(dst, src.partition_broadcast(P)).then_inc(done, 16)
    return 16 * len(pairs)


def normalise_input(nc, io, keep):
    with ExitStack() as ctx:
        s = Space(nc, ctx, "norm")
        stats = s.sb("stats", [P, TPG, 6])
        mv, mv4 = s.sb("mv", [P, NT, 2]), s.sb("mv4", [P, TPG, 2])
        ve = s.sb("ve", [P, NT])
        x_loaded = [s.sem(f"x_loaded{b}") for b in range(BATCH)]
        consts_loaded = s.sem("consts_loaded")
        var_ready, rstd_ready = s.sem("var_ready"), s.sem("rstd_ready")
        XN = keep.XN
        tiles = io["L0_attn_x"].rearrange("b (n p) d -> b p n d", p=P)
        npb = SEQ // P
        with nc.Block() as block:
            @block.sync
            def _(sp):
                for b in range(BATCH):
                    sp.dma_start(XN[:, 1 + b * npb:1 + (b + 1) * npb, :], tiles[b]).then_inc(x_loaded[b], 16)
                sp.dma_start(keep.ident[:], io["const_ident"]).then_inc(consts_loaded, 16)
                sp.dma_start(keep.identb[:], io["const_identb"]).then_inc(consts_loaded, 16)
                sp.dma_start(keep.going[:], io["const_going"]).then_inc(consts_loaded, 16)
                sp.dma_start(keep.w_router[:], io["w_router"]).then_inc(consts_loaded, 16)
                sp.wait_ge(consts_loaded, 64)

            @block.gpsimd
            def _(pool):
                pool.memset(keep.minus_half[:], -0.5)
                pool.memset(XN[:, 0, :], 0.0)
                pool.memset(XN[:, NT + 1:, :], 0.0)
                pool.memset(keep.mean[:, NT:], 0.0)
                pool.memset(keep.rstd[:, NT:], 0.0)
                pool.drain()
                for b in range(BATCH):
                    pool.wait_ge(var_ready, b + 1)
                    pool.tensor_tensor(keep.rstd[:, b * npb:(b + 1) * npb], ve[:, b * npb:(b + 1) * npb],
                                       keep.minus_half[:, 0:npb], ALU.pow).then_inc(rstd_ready, 1)

            @block.vector
            def _(dve):
                for b in range(BATCH):
                    dve.wait_ge(x_loaded[b], 16)
                    with dve.Fori(b * NG // BATCH, (b + 1) * NG // BATCH) as g:
                        for n in range(TPG):
                            dve.bn_stats(stats[:, n, :], XN[:, g * TPG + (n + 1), :])
                        dve.drain()
                        for n in range(TPG):
                            dve.bn_aggr(mv4[:, n, :], stats[:, n, :])
                        dve.drain()
                        dve.tensor_copy(mv[:, bass.ds(g * TPG, TPG), :], mv4[:])
                        dve.drain()
                    dve.tensor_scalar(ve[:, b * npb:(b + 1) * npb], mv[:, b * npb:(b + 1) * npb, 1], 1e-5, None,
                                      ALU.add).then_inc(var_ready, 1)
                for b in range(BATCH):
                    dve.wait_ge(rstd_ready, b + 1)
                    with dve.Fori(b * NG // BATCH, (b + 1) * NG // BATCH) as g:
                        for n in range(TPG):
                            t = g * TPG + n
                            dve.tensor_scalar(XN[:, g * TPG + (n + 1), :], XN[:, g * TPG + (n + 1), :],
                                              mv[:, t, 0:1], keep.rstd[:, bass.ds(g * TPG + n, 1)],
                                              ALU.subtract, ALU.mult)
        s.clear_semaphores()


class Keep:

    def __init__(self, nc, ctx):
        s = Space(nc, ctx, "keep")
        self.XN = s.sb("xn", [P, NT + 4, D])
        self.X2 = s.sb("x2", [P, NT + 1, D])
        self.ident = s.sb("ident", [P, P])
        self.identb = s.sb("identb", [P, P], BF16)
        self.going = s.sb("going", [P, NG + 1])
        self.minus_half = s.sb("minus_half", [P, NT])
        self.rstd = s.sb("rstd", [P, NT + 3])
        self.mean = s.sb("mean", [P, NT + 3])
        self.w_router = s.sb("w_router", [P, KC, EXPERTS])
        self.logits = s.sb("logits", [P, NT + 1, EXPERTS])
        self.slot = s.sb("slot", [P, NT], U32)
        self.expert = s.sb("expert", [1, SLOT_TILES], U32)


HEADS, HD = 16, 16
LAT, LAT_HEADS = 64, 4
CHUNK = SEQ // LAT
LPT = P // CHUNK


def window_attention(nc, io, keep, layer):
    latents = layer == 0
    pre = "L0_attn_" if latents else "L1_attn_"
    HU = 2 if latents else 4
    KEYS = 2 * P if latents else P
    WU = HEADS // HU
    ST = WU + latents
    U = ST * TPG
    HALF = P // 2
    LEAD = 3
    none = (None, 0)
    if latents:
        plan = [(("QK", 1), none), (("V", 1), none), (("latT", -1), none), (("rem", -1), none), (("R", 1), none),
                (none, none), (none, none), (("oT", -1), ("hT", 2)), (("out", -1), none)]
        ends_short = 1
        prologue = [("hT", 0), ("QK", 0), ("V", 0), ("R", 0), ("hT", 1)]
        epilogue = ["latT", "rem", "oT", "out"]
    else:
        plan = [(none, none), (("hT", 2), ("out", -1)), (("QK", 2), none), (("V", 2), none)]
        ends_short = 0
        prologue = [("hT", 0), ("QK", 0), ("V", 0), ("hT", 1), ("QK", 1), ("V", 1)]
        epilogue = ["out"]
    by_act = ("hT", "latT", "oT")
    order = [(name, n + ahead) for n in range(TPG) for pair in plan for name, ahead in pair if name]
    NACT = sum(name in by_act for name, _ in order)
    NDVE = len(order) - NACT
    acts_before = sum(name in by_act for name, _ in prologue)
    where = lambda m: 1 + m % TPG
    first_bank = lambda i: (i - len(prologue) - ends_short) % 2

    with ExitStack() as ctx:
        s = Space(nc, ctx, f"win{layer}")
        XN, X2 = keep.XN, keep.X2
        w_qkv = s.sb("w_qkv", [P, KC, 3 * D])
        w_out = s.sb("w_out", [P, KC, D])
        b_qk = s.sb("b_qk", [P, 2, KC])
        b_k = s.sb("b_k", [P, 2, KC])
        parity = s.sb("parity", [P, 2])
        b_v, b_out = s.sb("b_v", [P, D]), s.sb("b_out", [P, D])
        h = s.sb("h", [P, TPG, D])
        hT = s.sb("hT", [P, KC, P])
        QT = s.sb("QT", [P, 2, KC, P])
        KT = s.sb("KT", [P, 2, KC, (TPG + 1) * P])
        probs = s.sb("probs", [P, 4, BANK])
        probsT = s.sb("probsT", [P, 2, BANK])
        negmax = s.sb("negmax", [P, 4, 4])
        sums = s.sb("sums", [P, 2, HEADS + LAT_HEADS])
        oT = s.sb("oT", [P, KC, P])
        if latents:
            mask = s.sb("mask", [P, NG + 1, KEYS], BF16)
            w_rq = s.sb("w_rq", [P, KC, LAT_HEADS, 32])
            w_rk = s.sb("w_rk", [P, KC, LAT_HEADS, 32])
            w_rv = s.sb("w_rv", [P, KC, LAT])
            w_rout = s.sb("w_rout", [LAT, D])
            b_rq, b_rk = s.sb("b_rq", [P, 1]), s.sb("b_rk", [P, 1])
            b_rv, b_rout = s.sb("b_rv", [P, LAT]), s.sb("b_rout", [P, D])
            gl, gr = s.sb("gl", [P, HD]), s.sb("gr", [P, HD])
            pooledT = s.sb("pooledT", [P, KC, 2 * LAT])
            RQT = s.sb("RQT", [P, 2, P])
            RKT = s.sb("RKT", [P, 2, LAT_HEADS * LAT])
            RV = s.sb("RV", [P, 2, LAT])
            lat_mask = s.sb("lat_mask", [P, NT + 1, LAT], BF16)
            valid = s.sb("valid", [P, NG + 1, 2])
            lat, latT = s.sb("lat", [P, P]), s.sb("latT", [LAT, P])
            rem = s.sb("rem", [P, D])
            V = s.sb("V", [P, TPG + 1, D])
            rsum = s.sb("rsum", [P, HEADS + LAT_HEADS])
            attn = s.sb("attn", [P, D])
            local_part, remote_part = s.sb("local_part", [P, D]), s.sb("remote_part", [P, D])
            apart = s.sb("apart", [P, D])
            z, ez, gate = s.sb("z", [P, HEADS]), s.sb("ez", [P, HEADS]), s.sb("gate", [P, HEADS])
        else:
            mask = s.sb("mask", [P, KEYS], BF16)
            V, V_first = s.sb("V", [P, TPG + 1, 2, D]), s.sb("V_first", [P, TPG + 1, 2, D])
            rsum = s.sb("rsum", [P, 4, HU])
            tmp = s.sb("tmp", [P, D])
            g1, b1 = s.sb("g1", [P, KC]), s.sb("b1", [P, KC])
            stats, mv, mv1 = s.sb("stats", [P, 6]), s.sb("mv", [P, NT + 1, 2]), s.sb("mv1", [P, 2])
            ve = s.sb("ve", [P, NT])

        score = [s.ps(f"score{i}") for i in range(4)]
        turned, po = s.ps("turned"), s.ps("po")
        lin_banks = [s.ps(f"lin{i}") for i in range(2)]

        loaded, zeroed, biases = s.sem("loaded"), s.sem("zeroed"), s.sem("biases")
        h_ready = s.count("h_ready", TPG, credit=3)
        lin_ready = s.count("lin_ready", len(order), credit=len(prologue))
        act_took = s.count("act_took", NACT, credit=acts_before)
        dve_took = s.count("dve_took", NDVE, credit=len(prologue) - acts_before + ends_short)
        scores_ready = s.count("scores_ready", U)
        max_ready = s.count("max_ready", U)
        exp_done = s.count("exp_done", U, credit=4)
        probs_ready = exp_done if latents else s.count("probs_ready", U)
        inverse_ready = s.count("inverse_ready", U)
        turned_ready = s.count("turned_ready", U, credit=4)
        probsT_ready = s.count("probsT_ready", U, credit=1)
        pv_done = s.count("pv_done", U, credit=2)
        attn_ready = s.count("attn_ready", TPG, credit=1)
        pooled_ready = s.count("pooled_ready", TPG)
        parts_ready, z_ready = s.count("parts_ready", TPG, credit=1), s.count("z_ready", TPG, credit=1)
        ez_ready, gate_ready = s.count("ez_ready", TPG, credit=1), s.count("gate_ready", TPG, credit=1)
        mixed_ready = s.count("mixed_ready", TPG, credit=1)
        var_ready, rstd_done = s.sem("var_ready"), s.sem("rstd_done")
        rows_zeroed = s.sem("rows_zeroed")

        def taken(it, i):
            upto = [name in by_act for name, _ in order[:max(i + 1, 0)]]
            if order[i][0] in by_act:
                return act_took.sem, act_took.at(it, sum(upto))
            return dve_took.sem, dve_took.at(it, len(upto) - sum(upto))

        def heads_of(u):
            n, i = divmod(u, ST)
            if i == WU:
                return n, None
            return n, [2 * i, 2 * i + 1] if latents else [2 * i, 2 * i + 1, 8 + 2 * i, 8 + 2 * i + 1]

        with nc.Block() as block:
            @block.sync
            def _(sp):
                qkv = io[pre + ("qkv_w" if latents else "w_qkv")].rearrange("(c p) n -> p c n", p=P)
                bqkv = io[pre + ("qkv_b" if latents else "b_qkv")]
                pairs = [(w_qkv[:], qkv), (b_qk[:], io[f"win{layer}_b_qk"]), (parity[:], io["const_parity"]),
                         (w_out[:], io[pre + ("out_w" if latents else "w_out")].rearrange("(c p) n -> p c n", p=P)),
                         (mask[:], io["const_mask0" if latents else "const_mask1"])]
                if latents:
                    rkv = io[pre + "rkv_w"].rearrange("(c p) n -> p c n", p=P)
                    pairs += [(w_rq[:], io["win0_w_rq"]), (w_rk[:], io["win0_w_rk"]),
                              (b_rq[:], io["win0_b_rq"]), (b_rk[:], io["win0_b_rk"])]
                    pairs += [(w_rv[:], rkv[:, :, LAT:]), (w_rout[:], io[pre + "rout_w"]),
                              (lat_mask[:], io["const_lat_mask"]), (valid[:], io["const_valid"])]
                else:
                    pairs += [(g1[:], io["win1_gain"]), (b1[:], io["win1_offset"])]
                n = 0
                for dst, src in pairs:
                    sp.dma_start(dst, src).then_inc(loaded, 16)
                    n += 16
                rows = [(b_v[:], bqkv[2 * D:3 * D]), (b_out[:], io[pre + ("out_b" if latents else "b_out")])]
                if latents:
                    rows += [(b_rv[:], io[pre + "rkv_b"][LAT:]), (b_rout[:], io[pre + "rout_b"]),
                             (gl[:], io[pre + "gl_w"].rearrange("d o -> (d o)")),
                             (gr[:], io[pre + "gr_w"].rearrange("d o -> (d o)"))]
                n += load_bias_rows(sp, loaded, rows)
                sp.wait_ge(loaded, n)
                sp.sem_inc(biases, 1)
                if latents:
                    sp.dma_start(io["rows_in"].rearrange("(t p) d -> p t d", p=P),
                                 XN[:, 0:1, :].to_broadcast([P, SLOT_TILES, D])).then_inc(rows_zeroed, 16)
                    sp.wait_ge(rows_zeroed, 16)

            @block.gpsimd
            def _(pool):
                pool.memset(KT[:, :, :, 0:P], 0.0)
                pool.memset(V[:], 0.0)
                pool.memset(probsT[:], 0.0)
                if latents:
                    pool.memset(pooledT[:], 0.0)
                    pool.memset(lat[:], 0.0)
                    pool.memset(RKT[:], 0.0)
                    pool.memset(RV[:], 0.0)
                else:
                    pool.memset(V_first[:], 0.0)
                    pool.wait_ge(biases, 1)
                pool.drain()
                pool.sem_inc(zeroed, 1)

                def prepare(g, m):
                    if m > 2:
                        before = order.index(("hT", m - 2)) + 1 if m > 3 else 0
                        pool.wait_ge(lin_ready.sem, lin_ready.at(g, before))
                    if latents:
                        last = pool.tensor_copy(h[:, m % TPG, :], XN[:, g * TPG + (m + 1), :])
                    else:
                        pool.tensor_tensor(h[:, m % TPG, :], XN[:, g * TPG + (m + 1), :],
                                           keep.mean[:, bass.ds(g * TPG + m, 1)].to_broadcast([P, D]), ALU.subtract)
                        pool.drain()
                        last = pool.tensor_tensor(h[:, m % TPG, :], h[:, m % TPG, :],
                                                  keep.rstd[:, bass.ds(g * TPG + m, 1)].to_broadcast([P, D]), ALU.mult)
                    last.then_inc(h_ready.sem, 1)

                by_head = lambda t: t[:].rearrange("p (h d) -> p h d", d=HD)
                gate_row = lambda t: t[:].unsqueeze(1).to_broadcast([P, HEADS, HD])

                def mix(it, n, rem_taken):
                    pool.wait_ge(*rem_taken)
                    pool.tensor_tensor(by_head(local_part), by_head(attn), gate_row(gl), ALU.mult)
                    pool.tensor_tensor(by_head(remote_part), by_head(rem), gate_row(gr), ALU.mult)
                    pool.drain()
                    pool.tensor_tensor(local_part[:], local_part[:], remote_part[:], ALU.add).then_inc(parts_ready.sem, 1)
                    pool.tensor_tensor(apart[:], attn[:], rem[:], ALU.subtract)
                    pool.drain()
                    pool.wait_ge(gate_ready.sem, gate_ready.at(it, n + 1))
                    pool.tensor_tensor(by_head(apart), by_head(apart), bcast(gate[:], [P, HEADS, HD]), ALU.mult)
                    pool.drain()
                    pool.tensor_tensor(attn[:], apart[:], rem[:], ALU.add).then_inc(mixed_ready.sem, 1)

                def divide(it, u):
                    pool.wait_ge(inverse_ready.sem, inverse_ready.at(it, u + 1))
                    mine = probs[:, u % 4, :].rearrange("p (h k) -> p h k", h=HU)
                    pool.tensor_tensor(mine, mine, bcast(rsum[:, u % 4, :], [P, HU, KEYS]), ALU.mult)\
                        .then_inc(probs_ready.sem, 1)

                for m in range(3):
                    prepare(0, m)
                if not latents:
                    for u in range(LEAD - 1):
                        divide(0, u)
                with pool.Fori(0, NG) as g:
                    for n in range(TPG):
                        if latents:
                            prepare(g, n + 3)
                            mix(g, n - 1, taken(g, order.index(("rem", n - 1))))
                        else:
                            divide(g, n * ST + LEAD - 1)
                            prepare(g, n + 3)
                            for u in range(n * ST + 1, (n + 1) * ST):
                                divide(g, u + LEAD - 1)
                if latents:
                    mix(NG - 1, TPG - 1, (dve_took.sem, dve_took.at(NG, 1)))
                if not latents:
                    pool.wait_ge(var_ready, 1)
                    pool.tensor_tensor(keep.rstd[:, 0:NT], ve[:], keep.minus_half[:], ALU.pow).then_inc(rstd_done, 1)

            @block.tensor
            def _(pe):
                pe.sem_inc(turned_ready.sem, turned_ready.credit)
                pe.sem_inc(pv_done.sem, 1)
                pe.wait_ge(zeroed, 1)
                pe.wait_ge(biases, 1)
                pe.matmul(po[:], keep.ident[:], probsT[:, 1, :], start=True, stop=True)

                def linear_work(it, name, n, lin):
                    if name == "hT":
                        pe.wait_ge(h_ready.sem, h_ready.at(it, n - 2))
                        for c in range(KC):
                            last = pe.transpose(lin[:, c * P:(c + 1) * P], h[:, n % TPG, c * P:(c + 1) * P], keep.ident[:])
                    elif name == "QK":
                        for m in range(2 * KC):
                            for c in range(KC):
                                last = pe.matmul(lin[:, m * P:(m + 1) * P], w_qkv[:, c, m * P:(m + 1) * P], hT[:, c, :],
                                                 start=(c == 0), stop=(c == KC - 1))
                    elif name == "V":
                        for c in range(KC):
                            last = pe.matmul(lin[:, 0:D], hT[:, c, :], w_qkv[:, c, 2 * D:], start=(c == 0), stop=(c == KC - 1))
                        if latents:
                            for c in range(KC):
                                last = pe.matmul(lin[:, D:D + P], w_rq[:, c, :, :].rearrange("p h d -> p (h d)"),
                                                 hT[:, c, :], start=(c == 0), stop=(c == KC - 1))
                            for c in range(KC):
                                last = pe.matmul(lin[:, D + P:D + P + EXPERTS], hT[:, c, :], keep.w_router[:, c, :],
                                                 start=(c == 0), stop=(c == KC - 1))
                    elif name == "R":
                        pe.wait_ge(pooled_ready.sem, pooled_ready.at(it, n + 1))
                        for c in range(KC):
                            pe.matmul(lin[:, 0:LAT], w_rk[:, c, :, :].rearrange("p h d -> p (h d)"), pooledT[:, c, 0:LAT],
                                      start=(c == 0), stop=(c == KC - 1))
                        for c in range(KC):
                            last = pe.matmul(lin[:, LAT:2 * LAT], pooledT[:, c, :], w_rv[:, c, :],
                                             start=(c == 0), stop=(c == KC - 1))
                    elif name == "latT":
                        pe.wait_ge(attn_ready.sem, attn_ready.at(it, n + 1))
                        last = pe.transpose(lin[:, 0:P], lat[:], keep.ident[:])
                    elif name == "rem":
                        last = pe.matmul(lin[:, 0:D], latT[:], w_rout[:], start=True, stop=True)
                    elif name == "oT":
                        pe.wait_ge(mixed_ready.sem, mixed_ready.at(it, n + 1))
                        for c in range(KC):
                            last = pe.transpose(lin[:, c * P:(c + 1) * P], attn[:, c * P:(c + 1) * P], keep.ident[:])
                    elif name == "out":
                        if not latents:
                            pe.wait_ge(attn_ready.sem, attn_ready.at(it, n + 1))
                        for c in range(KC):
                            last = pe.matmul(lin[:, 0:D], oT[:, c, :], w_out[:, c, :], start=(c == 0), stop=(c == KC - 1))
                    last.then_inc(lin_ready.sem, 1)

                def linear_step(it, name, n):
                    if name:
                        i = order.index((name, n))
                        pe.wait_ge(*taken(it, i - 2))
                        if name == "rem":
                            pe.wait_ge(*taken(it, i - 1))
                        linear_work(it, name, n, lin_banks[i % 2])

                def scores(it, g, u):
                    n, heads = heads_of(u)
                    bank = score[u % 4]
                    pe.wait_ge(exp_done.sem, exp_done.at(it, u - 3))
                    if u == 0:
                        pe.wait_ge(act_took.sem, acts_before)
                        pe.wait_ge(dve_took.sem, dve_took.credit)
                    elif u % ST == 0 and latents:
                        pe.wait_ge(*taken(it, order.index(("R", n))))
                    elif n > 1 and u % ST == 0:
                        pe.wait_ge(*taken(it, order.index(("QK", n))))
                    elif u % ST == 0:
                        pe.wait_ge(*taken(it, -2))
                    if heads is None:
                        pe.matmul(bank[:, 0:LAT_HEADS * LAT], keep.identb[:],
                                  lat_mask[:, bass.ds(g * TPG + n, 1), :].to_broadcast([P, LAT_HEADS, LAT]),
                                  start=True, stop=False)
                        last = pe.matmul(bank[:, 0:LAT_HEADS * LAT], RQT[:, n % 2, :], RKT[:, n % 2, :],
                                         start=False, stop=True)
                    else:
                        if latents:
                            m = mask[:, bass.ds(g + n // TPG, 1), :] if n % TPG == 0 else mask[:, 1:2, :]
                        else:
                            m = mask[:].unsqueeze(1)
                        pe.matmul(bank[:], keep.identb[:], m.to_broadcast([P, HU, KEYS]), start=True, stop=False)
                        cur = where(n) * P
                        old = cur - P
                        for i, head in enumerate(heads):
                            c, j, odd = head // 8, head % 8 // 2, head % 2
                            rows, a = slice(32 * j, 32 * j + 32), i * KEYS
                            q, k = QT[rows, n % 2, c, :], KT[rows, odd, c, :]
                            if latents:
                                last = pe.matmul(bank[:, a:a + KEYS], q, k[:, old:old + KEYS], start=False, stop=(i == HU - 1))
                            else:
                                pe.matmul(bank[:, a:a + HALF], q, k[:, cur:cur + HALF], start=False, stop=False)
                                pe.matmul(bank[0:HALF, a + HALF:a + P], q[:, 0:HALF], k[:, old + HALF:old + P],
                                          start=False, stop=(i == HU - 1))
                                last = pe.matmul(bank[HALF:P, a + HALF:a + P], q[:, HALF:P], k[:, cur + HALF:cur + P],
                                                 start=False, stop=(i == HU - 1))
                    last.then_inc(scores_ready.sem, 1)

                def turn(it, u):
                    n, heads = heads_of(u)
                    pe.wait_ge(probs_ready.sem, probs_ready.at(it, u + 1))
                    pe.wait_ge(probsT_ready.sem, probsT_ready.at(it, u))
                    for i in range(LAT_HEADS // 2 if heads is None else 4):
                        last = pe.transpose(turned[:, i * P:(i + 1) * P],
                                            probs[:, u % 4, i * P:(i + 1) * P], keep.ident[:])
                    last.then_inc(turned_ready.sem, 1)

                def weigh(it, u):
                    n, heads = heads_of(u)
                    pe.wait_ge(probsT_ready.sem, probsT_ready.at(it, u + 1))
                    if u % ST == 0:
                        pe.wait_ge(attn_ready.sem, attn_ready.at(it, n))
                    if heads is None:
                        for j in range(LAT_HEADS // 2):
                            last = pe.matmul(po[:, D + j * 2 * HD:D + (j + 1) * 2 * HD], probsT[:, u % 2, j * P:(j + 1) * P],
                                             RV[:, n % 2, j * 2 * HD:(j + 1) * 2 * HD], start=True, stop=True)
                    elif latents:
                        for i, head in enumerate(heads):
                            a = head * HD
                            for own in range(2):
                                last = pe.matmul(po[:, a:a + HD], probsT[:, u % 2, (2 * i + own) * P:(2 * i + own + 1) * P],
                                                 V[:, n % TPG + own, a:a + HD], start=(own == 0), stop=(own == 1))
                    else:
                        rows = slice(32 * (u % ST), 32 * (u % ST) + 32)
                        for c in range(KC):
                            for half in range(2):
                                values = V if half else V_first
                                for odd in range(2):
                                    q = (2 * c + odd) * P + half * HALF
                                    last = pe.matmul(po[rows, c * P + half * HALF:c * P + (half + 1) * HALF],
                                                     values[:, where(n), odd, c * P + 32 * (u % ST):c * P + 32 * (u % ST) + 32],
                                                     probsT[:, u % 2, q:q + HALF], start=(odd == 0), stop=(odd == 1))
                    last.then_inc(pv_done.sem, 1)

                for i, (name, n) in enumerate(prologue):
                    acts = sum(x in by_act for x, _ in prologue[:i])
                    if i > 0:
                        pe.wait_ge(act_took.sem, acts)
                        if i > acts:
                            pe.wait_ge(dve_took.sem, ends_short + i - acts)
                    if name == "hT":
                        pe.wait_ge(h_ready.sem, n + 1)
                        for c in range(KC):
                            last = pe.transpose(lin_banks[first_bank(i)][:, c * P:(c + 1) * P], h[:, n, c * P:(c + 1) * P], keep.ident[:])
                        last.then_inc(lin_ready.sem, 1)
                    else:
                        linear_work(0, name, n, lin_banks[first_bank(i)])
                for u in range(LEAD):
                    scores(0, 0, u)
                with pe.Fori(0, NG) as g:
                    for u in range(U):
                        n, st = divmod(u, ST)
                        one, two = plan[st]
                        linear_step(g, one[0], n + one[1])
                        scores(g, g, u + LEAD)
                        linear_step(g, two[0], n + two[1])
                        turn(g, u)
                        weigh(g, u - 1)
                weigh(NG - 1, U - 1)
                pe.wait_ge(*taken(NG, -2))
                pe.wait_ge(*taken(NG, -1))
                for i, name in enumerate(epilogue):
                    acts = sum(x in by_act for x in epilogue[:i])
                    if i > 0:
                        pe.wait_ge(act_took.sem, act_took.at(NG, acts))
                        pe.wait_ge(dve_took.sem, dve_took.at(NG, i - acts))
                    linear_work(NG - 1, name, TPG - 1, lin_banks[i % 2])

            @block.scalar
            def _(act):
                act.sem_inc(exp_done.sem, exp_done.credit)
                act.wait_ge(biases, 1)

                def take(name, lin):
                    if name == "hT" and not latents:
                        act.activation(hT[:, 0, :], lin[:, 0:P], ACT.Identity, bias=b1[:, 0:1], scale=g1[:, 0:1])
                        last = act.activation(hT[:, 1, :], lin[:, P:2 * P], ACT.Identity, bias=b1[:, 1:2], scale=g1[:, 1:2])
                    elif name in ("hT", "oT"):
                        dst = hT if name == "hT" else oT
                        last = act.activation(dst[:].rearrange("p c n -> p (c n)"), lin[:, 0:D], ACT.Copy)
                    else:
                        last = act.activation(latT[:], lin[0:LAT, 0:P], ACT.Copy)
                    last.then_inc(act_took.sem, 1)

                def linear_step(it, name, n):
                    if name in by_act:
                        i = order.index((name, n))
                        act.wait_ge(lin_ready.sem, lin_ready.at(it, i + 1))
                        take(name, lin_banks[i % 2])

                def softmax(it, u):
                    n, heads = heads_of(u)
                    act.wait_ge(max_ready.sem, max_ready.at(it, u + 1))
                    act.wait_ge(turned_ready.sem, turned_ready.at(it, u - 3))
                    width = LAT if heads is None else KEYS
                    cols = range(HEADS, HEADS + LAT_HEADS) if heads is None else heads
                    for i, col in enumerate(cols):
                        last = act.activation(probs[:, u % 4, i * width:(i + 1) * width],
                                              score[u % 4][:, i * width:(i + 1) * width], ACT.Exp,
                                              bias=negmax[:, u % 4, i:i + 1],
                                              accum_out=sums[:, n % 2, col:col + 1])
                    last.then_inc(exp_done.sem, 1)

                def take_output(it, n):
                    act.wait_ge(pv_done.sem, pv_done.at(it, (n + 1) * ST))
                    act.activation(oT[:].rearrange("p c n -> p (c n)"), po[:, 0:D], ACT.Copy).then_inc(attn_ready.sem, 1)

                def gates(it, n):
                    act.wait_ge(z_ready.sem, z_ready.at(it, n + 1))
                    act.activation(ez[:], z[:], ACT.Exp, scale=-1.0).then_inc(ez_ready.sem, 1)

                for i, (name, n) in enumerate(prologue):
                    if name in by_act:
                        act.wait_ge(lin_ready.sem, i + 1)
                        take(name, lin_banks[first_bank(i)])
                for u in range(LEAD):
                    softmax(0, u)
                with act.Fori(0, NG) as g:
                    for u in range(U):
                        n, st = divmod(u, ST)
                        one, two = plan[st]
                        linear_step(g, one[0], n + one[1])
                        softmax(g, u + LEAD)
                        linear_step(g, two[0], n + two[1])
                        if latents and st == 4:
                            gates(g, n - 1)
                        if not latents and st == 0:
                            take_output(g, n - 1)
                if not latents:
                    take_output(NG - 1, TPG - 1)
                for i, name in enumerate(epilogue):
                    if name in by_act:
                        if name == "oT" and latents:
                            gates(NG - 1, TPG - 1)
                        act.wait_ge(lin_ready.sem, lin_ready.at(NG, i + 1))
                        take(name, lin_banks[i % 2])

            @block.vector
            def _(dve):
                if ends_short:
                    dve.sem_inc(dve_took.sem, ends_short)
                dve.sem_inc(probsT_ready.sem, probsT_ready.credit)
                dve.memset(sums[:], 1.0)
                dve.wait_ge(biases, 1)
                dve.wait_ge(zeroed, 1)
                dve.tensor_scalar(b_qk[:, 0, :], b_qk[:, 0, :], HD ** -0.5, None, ALU.mult)
                for odd in range(2):
                    dve.tensor_scalar(b_k[:, odd, :], b_qk[:, 1, :], parity[:, odd:odd + 1], None, ALU.mult)
                dve.drain()

                def take(g, name, n, lin):
                    if name == "QK":
                        by_chunk = lin[:].rearrange("p (w c n) -> p w c n", w=2, c=KC)
                        dve.scalar_tensor_tensor(QT[:, n % 2, :, :], by_chunk[:, 0], HD ** -0.5,
                                                 bcast(b_qk[:, 0, :], [P, KC, P]), ALU.mult, ALU.add)
                        for odd in range(2):
                            last = dve.scalar_tensor_tensor(KT[:, odd, :, where(n) * P:(where(n) + 1) * P], by_chunk[:, 1],
                                                            parity[:, odd:odd + 1], bcast(b_k[:, odd, :], [P, KC, P]),
                                                            ALU.mult, ALU.add)
                        if where(n) == TPG:
                            dve.drain()
                            last = dve.tensor_scalar(KT[:, :, :, 0:P], KT[:, :, :, TPG * P:],
                                                     keep.going[:, bass.ds(g + n // TPG + 1, 1)], None, ALU.mult)
                    elif name == "V" and latents:
                        dve.tensor_tensor(V[:, where(n), :], lin[:, 0:D], b_v[:], ALU.add)
                        if where(n) == TPG:
                            dve.tensor_tensor(V[:, 0, :], lin[:, 0:D], b_v[:], ALU.add)
                        dve.tensor_scalar(RQT[:, n % 2, :], lin[:, D:D + P], b_rq[:, 0:1], HD ** -0.5, ALU.add, ALU.mult)
                        last = dve.tensor_copy(keep.logits[:, g * TPG + n, :], lin[:, D + P:D + P + EXPERTS])
                    elif name == "V":
                        for odd in range(2):
                            mine = lambda t: t.rearrange("p (h two d) -> p h two d", two=2, d=HD)[:, :, odd, :]
                            low, high = slice(0, HALF), slice(HALF, P)
                            dve.tensor_tensor(mine(V[:, where(n), odd, :]), mine(lin[:, 0:D]), mine(b_v[:]), ALU.add)
                            dve.tensor_tensor(mine(V_first[low, where(n), odd, :]), mine(lin[low, 0:D]), mine(b_v[low, :]), ALU.add)
                            last = dve.tensor_tensor(mine(V_first[high, where(n + 1), odd, :]), mine(lin[high, 0:D]),
                                                     mine(b_v[high, :]), ALU.add)
                        if where(n) == TPG:
                            dve.drain()
                            last = dve.tensor_scalar(V_first[high, where(n + 1), :, :], V_first[high, where(n + 1), :, :],
                                                     keep.going[high, bass.ds(g + n // TPG + 1, 1)], None, ALU.mult)
                    elif name == "R":
                        for j in range(LAT_HEADS):
                            quad = slice(32 * j, 32 * j + 32)
                            dve.tensor_scalar(RKT[quad, n % 2, j * LAT:(j + 1) * LAT], lin[quad, 0:LAT], 1.0 / CHUNK,
                                              b_rk[quad, 0:1], ALU.mult, ALU.add)
                        for odd in range(2):
                            rows = slice(odd * LAT, (odd + 1) * LAT)
                            pairs = lambda t: t.rearrange("p (j two d) -> p j two d", two=2, d=HD)[:, :, odd, :]
                            last = dve.scalar_tensor_tensor(pairs(RV[rows, n % 2, :]), pairs(lin[rows, LAT:2 * LAT]),
                                                            1.0 / CHUNK, pairs(b_rv[rows, :]), ALU.mult, ALU.add)
                    elif name == "rem":
                        last = dve.tensor_tensor(rem[:], lin[:, 0:D], b_rout[:], ALU.add)
                    elif latents:
                        last = dve.tensor_tensor(X2[:, g * TPG + (n + 1), :], lin[:, 0:D], b_out[:], ALU.add)
                    else:
                        last = dve.tensor_tensor(tmp[:], lin[:, 0:D], b_out[:], ALU.add)
                    last.then_inc(dve_took.sem, 1)
                    if name == "out" and not latents:
                        dve.drain()
                        dve.tensor_tensor(X2[:, g * TPG + (n + 1), :], tmp[:], XN[:, g * TPG + (n + 1), :], ALU.add)
                        dve.drain()
                        dve.bn_stats(stats[:], X2[:, g * TPG + (n + 1), :])
                        dve.drain()
                        dve.bn_aggr(mv1[:], stats[:])
                        dve.drain()
                        dve.tensor_copy(mv[:, g * TPG + (n + 1), :], mv1[:])

                def linear_step(it, g, name, n):
                    if name and name not in by_act:
                        i = order.index((name, n))
                        dve.wait_ge(lin_ready.sem, lin_ready.at(it, i + 1))
                        take(g, name, n, lin_banks[i % 2])

                def pool_latents(first):
                    for c in range(KC):
                        for twice in range(2):
                            last = dve.tensor_reduce(pooledT[:, c, bass.ds(first + twice * LAT, LPT)],
                                                     hT[:, c, :].rearrange("p (l n) -> p l n", n=CHUNK), AX.X, ALU.add)
                    last.then_inc(pooled_ready.sem, 1)

                def maxima(it, u):
                    _, heads = heads_of(u)
                    dve.wait_ge(scores_ready.sem, scores_ready.at(it, u + 1))
                    k = LAT_HEADS if heads is None else HU
                    w = LAT if heads is None else KEYS
                    dve.tensor_reduce(negmax[:, u % 4, 0:k], score[u % 4][:, 0:k * w].rearrange("p (h k) -> p h k", h=k),
                                      AX.X, ALU.max, negate=True).then_inc(max_ready.sem, 1)

                def invert(it, u):
                    n, heads = heads_of(u)
                    dve.wait_ge(exp_done.sem, exp_done.at(it, u + 1))
                    total = sums[:, n % 2, 0:HEADS].rearrange("p (c h) -> p c h", c=KC)[:, :, heads[0]:heads[0] + 2]
                    dve.reciprocal(rsum[:, u % 4, :].rearrange("p (c h) -> p c h", c=KC), total).then_inc(inverse_ready.sem, 1)

                def take_turned(it, u):
                    _, heads = heads_of(u)
                    dve.wait_ge(turned_ready.sem, turned_ready.at(it, u + 1))
                    dve.wait_ge(pv_done.sem, pv_done.at(it, u - 1))
                    k = LAT_HEADS // 2 * P if heads is None else BANK
                    dve.tensor_copy(probsT[:, u % 2, 0:k], turned[:, 0:k]).then_inc(probsT_ready.sem, 1)

                def normalise(it, g, n):
                    dve.wait_ge(pv_done.sem, pv_done.at(it, (n + 1) * ST))
                    dve.reciprocal(rsum[:], sums[:, n % 2, :])
                    dve.drain()
                    if n == 0:
                        dve.tensor_scalar(rsum[:, 0:HEADS], rsum[:, 0:HEADS], valid[:, g, 0:1], None, ALU.mult)
                        dve.tensor_scalar(rsum[:, HEADS:], rsum[:, HEADS:], valid[:, g, 1:2], None, ALU.mult)
                        dve.drain()
                    dve.tensor_tensor(attn[:].rearrange("p (h d) -> p h d", d=HD),
                                      po[:, 0:D].rearrange("p (h d) -> p h d", d=HD),
                                      bcast(rsum[:, 0:HEADS], [P, HEADS, HD]), ALU.mult)
                    dve.tensor_tensor(lat[:, 0:LAT].rearrange("p (h d) -> p h d", d=HD),
                                      po[:, D:D + LAT].rearrange("p (h d) -> p h d", d=HD),
                                      bcast(rsum[:, HEADS:], [P, LAT_HEADS, HD]), ALU.mult).then_inc(attn_ready.sem, 1)

                def gate_logits(it, n):
                    dve.wait_ge(parts_ready.sem, parts_ready.at(it, n + 1))
                    dve.tensor_reduce(z[:], local_part[:].rearrange("p (h d) -> p h d", d=HD), AX.X, ALU.add)\
                       .then_inc(z_ready.sem, 1)

                def gates(it, n):
                    dve.wait_ge(ez_ready.sem, ez_ready.at(it, n + 1))
                    dve.tensor_scalar(gate[:], ez[:], 1.0, None, ALU.add)
                    dve.drain()
                    dve.reciprocal(gate[:], gate[:]).then_inc(gate_ready.sem, 1)

                for i, (name, n) in enumerate(prologue):
                    if name == "R":
                        dve.wait_ge(act_took.sem, 1)
                        pool_latents(LAT - LPT)
                    if name not in by_act:
                        dve.wait_ge(lin_ready.sem, i + 1)
                        take(0, name, n, lin_banks[first_bank(i)])
                for u in range(LEAD):
                    maxima(0, u)
                if not latents:
                    for u in range(LEAD - 1):
                        invert(0, u)

                def group(it, gi):
                    for u in range(U):
                        n, st = divmod(u, ST)
                        one, two = plan[st]
                        maxima(it, u + LEAD)
                        take_turned(it, u)
                        if not latents:
                            invert(it, u + LEAD - 1)
                        if latents and st == 0:
                            normalise(it, it, n - 1)
                        linear_step(it, it, one[0], n + one[1])
                        linear_step(it, it, two[0], n + two[1])
                        if latents and st == 1:
                            dve.wait_ge(*taken(it, order.index(("hT", n + 1)) if n else -2))
                            pool_latents(gi * (TPG * LPT) + n * LPT)
                        if latents and st == 4:
                            gate_logits(it, n - 1)
                        if latents and st == 5:
                            gates(it, n - 1)

                if latents:
                    with dve.Fori(0, BATCH) as b:
                        with dve.Fori(0, GPB) as gi:
                            group(b * GPB + gi, gi)
                else:
                    with dve.Fori(0, NG) as g:
                        group(g, None)
                if latents:
                    normalise(NG - 1, NG - 1, TPG - 1)
                for i, name in enumerate(epilogue):
                    if name not in by_act:
                        dve.wait_ge(lin_ready.sem, lin_ready.at(NG, i + 1))
                        take(NG - 1, name, TPG - 1, lin_banks[i % 2])
                    if name == "rem":
                        gate_logits(NG - 1, TPG - 1)
                        gates(NG - 1, TPG - 1)
                if not latents:
                    dve.drain()
                    dve.tensor_copy(keep.mean[:, 0:NT], mv[:, 1:, 0])
                    dve.tensor_scalar(ve[:], mv[:, 1:, 1], 1e-5, None, ALU.add).then_inc(var_ready, 1)
                    dve.wait_ge(rstd_done, 1)
        s.clear_semaphores()


def route(nc, io, keep):
    with ExitStack() as ctx:
        s = Space(nc, ctx, "route")
        top, number = s.sb("top", [P, NT]), s.sb("number", [P, EXPERTS])
        chosen = s.sb("chosen", [P, NT])
        mask = s.sb("mask", [P, NT, EXPERTS])
        mask16 = s.sb("mask16", [P, NT, EXPERTS], BF16)
        before = s.sb("before", [P, NT + 1, EXPERTS])
        before16 = s.sb("before16", [P, NT + 1, EXPERTS], BF16)
        earlier = s.sb("earlier", [P, P], BF16)
        ones16 = s.sb("ones16", [P, P], BF16)
        iota = s.sb("iota", [P, SLOT_TILES])
        counts = s.sb("counts", [P, EXPERTS])
        over = s.sb("over", [P, EXPERTS, NT])
        tiles, ends, first = s.sb("tiles", [P, EXPERTS]), s.sb("ends", [P, EXPERTS]), s.sb("first", [P, EXPERTS])
        ones = s.sb("ones", [P, EXPERTS])
        place = s.sb("place", [P, NT, EXPERTS])
        slotf = s.sb("slotf", [P, NT])
        past = s.sb("past", [P, SLOT_TILES, EXPERTS])
        expertf = s.sb("expertf", [P, SLOT_TILES])
        copied = s.sb("copied", [P, 2, D])
        index_now = s.sb("index_now", [P, 2, 1], U32)
        rank, total = s.ps("rank", [P, NT * EXPERTS]), s.ps("total", [P, EXPERTS])
        loaded, masks_ready, ranks_ready = s.sem("loaded"), s.sem("masks_ready"), s.sem("ranks_ready")
        slots_ready, staged, started = s.sem("slots_ready"), s.sem("staged"), s.sem("started")
        scattered = [s.sem(f"scattered{i}") for i in range(2)]
        with nc.Block() as block:
            @block.sync
            def _(sp):
                sp.dma_start(earlier[:], io["const_earlier"]).then_inc(loaded, 16)
                sp.dma_start(iota[:], io["const_iota"]).then_inc(loaded, 16)

            @block.tensor
            def _(pe):
                pe.wait_ge(loaded, 32)
                pe.wait_ge(masks_ready, 1)
                pe.matmul(rank[:], earlier[:], mask16[:].rearrange("p t e -> p (t e)"), start=True, stop=False)
                pe.matmul(rank[:], ones16[:], before16[:, 0:NT, :].rearrange("p t e -> p (t e)"), start=False, stop=True)
                pe.matmul(total[:], ones16[:], before16[:, NT, :], start=True, stop=True).then_inc(ranks_ready, 1)

            @block.gpsimd
            def _(pool):
                pool.wait_ge(slots_ready, 1)
                with pool.Fori(0, NT // 2) as t2:
                    for i in range(2):
                        pool.wait_ge(staged, t2 * 2 + (i + 1))
                        pool.sem_inc(started, 1)
                        pool.indirect_dma_start(io["rows_in"], bass.IndirectOffsetOnAxis(ap=index_now[:, i, :], axis=0),
                                                copied[:, i, :], None).then_inc(scattered[i], 16)
                for i in range(2):
                    pool.wait_ge(scattered[i], 16 * NT // 2)

            @block.vector
            def _(dve):
                dve.memset(ones16[:], 1.0)
                dve.memset(ones[:], 1.0)
                dve.memset(before[:, 0, :], 0.0)
                dve.wait_ge(loaded, 32)
                dve.tensor_reduce(top[:], keep.logits[:, 0:NT, :], AX.X, ALU.max)
                dve.tensor_scalar(number[:], iota[:, 0:EXPERTS], float(EXPERTS), None, ALU.subtract)
                dve.drain()
                dve.tensor_tensor(mask[:], keep.logits[:, 0:NT, :], bcast(top[:], [P, NT, EXPERTS]), ALU.is_equal)
                dve.drain()
                numbers = number[:].unsqueeze(1).to_broadcast([P, NT, EXPERTS])
                dve.tensor_tensor(mask[:], mask[:], numbers, ALU.mult)
                dve.drain()
                dve.tensor_reduce(chosen[:], mask[:], AX.X, ALU.min)
                dve.drain()
                dve.tensor_tensor(mask[:], bcast(chosen[:], [P, NT, EXPERTS]), numbers, ALU.is_equal)
                dve.drain()
                dve.tensor_copy(mask16[:], mask[:])
                for t in range(NT):
                    dve.tensor_tensor(before[:, t + 1, :], before[:, t, :], mask[:, t, :], ALU.add)
                    dve.drain()
                dve.tensor_copy(before16[:], before[:]).then_inc(masks_ready, 1)
                dve.wait_ge(ranks_ready, 1)
                dve.tensor_copy(counts[:], total[:])
                dve.drain()
                dve.tensor_scalar(slotf[:], iota[:, 0:NT], float(P), None, ALU.mult)
                dve.drain()
                dve.tensor_tensor(over[:], bcast(counts[:], [P, EXPERTS, NT]),
                                  slotf[:].unsqueeze(1).to_broadcast([P, EXPERTS, NT]), ALU.is_gt)
                dve.drain()
                dve.tensor_reduce(tiles[:], over[:], AX.X, ALU.add)
                dve.drain()
                dve.tensor_tensor_scan(ends[:], ones[:], tiles[:], 0.0, ALU.mult, ALU.add)
                dve.drain()
                dve.tensor_tensor(first[:], ends[:], tiles[:], ALU.subtract)
                dve.drain()
                dve.tensor_scalar(first[:], first[:], float(P), None, ALU.mult)
                dve.drain()
                dve.tensor_tensor(place[:], rank[:].rearrange("p (t e) -> p t e", e=EXPERTS),
                                  first[:].unsqueeze(1).to_broadcast([P, NT, EXPERTS]), ALU.add)
                dve.drain()
                dve.tensor_tensor(place[:], place[:], mask[:], ALU.mult)
                dve.drain()
                dve.tensor_reduce(slotf[:], place[:], AX.X, ALU.add)
                dve.drain()
                dve.tensor_copy(keep.slot[:], slotf[:])
                dve.tensor_tensor(past[:], bcast(iota[:], [P, SLOT_TILES, EXPERTS]),
                                  ends[:].unsqueeze(1).to_broadcast([P, SLOT_TILES, EXPERTS]), ALU.is_ge)
                dve.drain()
                dve.tensor_reduce(expertf[:], past[:], AX.X, ALU.add)
                dve.drain()
                dve.tensor_scalar(expertf[:], expertf[:], float(EXPERTS - 1), None, ALU.min)
                dve.drain()
                dve.tensor_copy(keep.expert[:], expertf[0:1, :])
                dve.drain()
                dve.sem_inc(slots_ready, 1)

                def stage(t2, i):
                    dve.tensor_copy(copied[:, i, :], keep.XN[:, t2 * 2 + (i + 1), :])
                    dve.tensor_copy(index_now[:, i, :], keep.slot[:, bass.ds(t2 * 2 + i, 1)])
                    dve.drain()
                    dve.sem_inc(staged, 1)

                for i in range(2):
                    stage(0, i)
                with dve.Fori(1, NT // 2) as t2:
                    for i in range(2):
                        dve.wait_ge(scattered[i], t2 * 16)
                        stage(t2, i)
        s.clear_semaphores()


def experts(nc, io, keep):
    HB = INNER // BANK
    IC = INNER // P
    N = SLOT_TILES
    with ExitStack() as ctx:
        s = Space(nc, ctx, "experts")
        w1 = s.sb("w1", [P, KC, EXPERTS * INNER])
        b1 = s.sb("b1", [P, EXPERTS * INNER])
        wo = s.sb("wo", [P, IC, D])
        rows = s.sb("rows", [P, 2, D])
        rowsT = s.sb("rowsT", [P, KC, P])
        inner = s.sb("inner", [P, 1, INNER])
        innerT = s.sb("innerT", [P, IC, P])
        y = s.sb("y", [P, 2, D])
        turned = s.ps("turned")
        hidden = [[s.ps(f"hidden{i}{b}") for b in range(HB)] for i in range(2)]
        innerT_ps = [s.ps(f"innerT{b}") for b in range(HB)]
        out = s.ps("out")
        loaded = s.sem("loaded")
        rows_loaded = [s.sem(f"rows_loaded{i}") for i in range(2)]
        stored = [s.sem(f"stored{i}") for i in range(2)]
        turned_ready, rowsT_ready = s.sem("turned_ready"), s.sem("rowsT_ready")
        hidden_ready, biased, gelu_done = s.sem("hidden_ready"), s.sem("biased"), s.sem("gelu_done")
        innerT_turned, innerT_ready = s.sem("innerT_turned"), s.sem("innerT_ready")
        out_ready, y_ready = s.sem("out_ready"), s.sem("y_ready")
        rows_in = io["rows_in"].rearrange("(t p) d -> t p d", p=P)
        rows_out = io["rows_out"].rearrange("(t p) d -> t p d", p=P)
        with nc.Block() as block:
            @block.sync
            def _(sp):
                n = 0
                for dst, src in [(wo[:], io["L0_ffn_Wo"].rearrange("(c p) n -> p c n", p=P))] + \
                        [(w1[:, c, e * INNER:(e + 1) * INNER], io["L0_ffn_W1"][e, c * P:(c + 1) * P, :])
                         for e in range(EXPERTS) for c in range(KC)] + \
                        [(b1[:, e * INNER:(e + 1) * INNER], io["L0_ffn_b1"][e].partition_broadcast(P))
                         for e in range(EXPERTS)]:
                    sp.dma_start(dst, src).then_inc(loaded, 16)
                    n += 16
                for i in range(2):
                    sp.dma_start(rows[:, i, :], rows_in[i]).then_inc(rows_loaded[i], 16)
                with sp.Fori(1, N // 2) as j2:
                    for i in range(2):
                        sp.wait_ge(turned_ready, j2 * 2 + (i - 1))
                        sp.dma_start(rows[:, i, :], rows_in[j2 * 2 + i]).then_inc(rows_loaded[i], 16)

            @block.tensor
            def _(pe):
                def turn_rows(j, i, count):
                    pe.wait_ge(rows_loaded[i], 16 * count)
                    for c in range(KC):
                        last = pe.transpose(turned[:, c * P:(c + 1) * P], rows[:, i, c * P:(c + 1) * P], keep.ident[:])
                    last.then_inc(turned_ready, 1)

                def hide(j, i, later):
                    e = pe.value_load(keep.expert[0:1, bass.ds(j, 1)], min_val=0, max_val=EXPERTS - 1)
                    pe.wait_ge(rowsT_ready, j + 1)
                    if later:
                        pe.wait_ge(biased, (j - 1) * HB)
                    for b in range(HB):
                        for c in range(KC):
                            last = pe.matmul(hidden[i][b][:], rowsT[:, c, :],
                                             w1[:, c, bass.ds(e * INNER + b * BANK, BANK)],
                                             start=(c == 0), stop=(c == KC - 1))
                        last.then_inc(hidden_ready, 1)

                def project(j):
                    pe.wait_ge(gelu_done, j * HB + HB)
                    for b in range(HB):
                        for c in range(4):
                            a = b * BANK + c * P
                            last = pe.transpose(innerT_ps[b][:, c * P:(c + 1) * P], inner[:, 0, a:a + P], keep.ident[:])
                        last.then_inc(innerT_turned, 1)
                    for b in range(HB):
                        pe.wait_ge(innerT_ready, j * HB + (b + 1))
                        for c in range(4 * b, 4 * b + 4):
                            last = pe.matmul(out[:, 0:D], innerT[:, c, :], wo[:, c, :], start=(c == 0), stop=(c == IC - 1))
                    last.then_inc(out_ready, 1)

                pe.wait_ge(loaded, 16 * (1 + EXPERTS * (KC + 1)))
                turn_rows(0, 0, 1)
                hide(0, 0, False)
                turn_rows(1, 1, 1)
                pe.wait_ge(y_ready, 1)
                hide(1, 1, False)
                pe.wait_ge(rowsT_ready, 2)
                turn_rows(2, 0, 2)
                project(0)
                with pe.Fori(1, N // 2 - 1) as j2:
                    for i in range(2):
                        j = j2 * 2 + i
                        hide(j, i, True)
                        turn_rows(j2 * 2 + (i + 1), 1 - i, j2 + (i + 1))
                        pe.wait_ge(y_ready, j2 * 2 + i)
                        project(j2 * 2 + (i - 1))
                hide(N - 2, 0, True)
                turn_rows(N - 1, 1, N // 2)
                pe.wait_ge(y_ready, N - 2)
                project(N - 3)
                hide(N - 1, 1, True)
                pe.wait_ge(y_ready, N - 1)
                project(N - 2)
                pe.wait_ge(y_ready, N)
                project(N - 1)

            @block.vector
            def _(dve):
                dve.wait_ge(loaded, 16 * (1 + EXPERTS * (KC + 1)))
                def bias(j, i, first):
                    e = dve.value_load(keep.expert[0:1, bass.ds(j, 1)], min_val=0, max_val=EXPERTS - 1)
                    for b in range(HB):
                        dve.wait_ge(hidden_ready, j * HB + (b + 1))
                        if not first and b == 0:
                            dve.wait_ge(innerT_turned, j * HB)
                        dve.tensor_tensor(inner[:, 0, b * BANK:(b + 1) * BANK], hidden[i][b][:],
                                          b1[:, bass.ds(e * INNER + b * BANK, BANK)], ALU.add).then_inc(biased, 1)

                def take_inner(j, first):
                    for b in range(HB):
                        dve.wait_ge(innerT_turned, j * HB + (b + 1))
                        if not first and b == 0:
                            dve.wait_ge(out_ready, j)
                        dve.tensor_copy(innerT[:, 4 * b:4 * b + 4, :].rearrange("p c n -> p (c n)"), innerT_ps[b][:])\
                           .then_inc(innerT_ready, 1)

                bias(0, 0, True)
                take_inner(0, True)
                bias(1, 1, False)
                take_inner(1, False)
                with dve.Fori(1, N // 2) as j2:
                    for i in range(2):
                        bias(j2 * 2 + i, i, False)
                        take_inner(j2 * 2 + i, False)

            @block.scalar
            def _(act):
                act.sem_inc(y_ready, 1)
                def take_rows(j):
                    act.wait_ge(turned_ready, j + 1)
                    act.activation(rowsT[:].rearrange("p c n -> p (c n)"), turned[:, 0:D], ACT.Copy).then_inc(rowsT_ready, 1)

                def gelu(j):
                    for b in range(HB):
                        act.wait_ge(biased, j * HB + (b + 1))
                        act.activation(inner[:, 0, b * BANK:(b + 1) * BANK], inner[:, 0, b * BANK:(b + 1) * BANK],
                                       ACT.Gelu).then_inc(gelu_done, 1)

                def take_out(j, i, count):
                    act.wait_ge(out_ready, j + 1)
                    if count is not None:
                        act.wait_ge(stored[i], 16 * count)
                    act.activation(y[:, i, :], out[:, 0:D], ACT.Copy).then_inc(y_ready, 1)

                take_rows(0)
                take_rows(1)
                gelu(0)
                take_rows(2)
                take_out(0, 0, None)
                gelu(1)
                take_rows(3)
                take_out(1, 1, None)
                with act.Fori(1, N // 2 - 1) as j2:
                    for i in range(2):
                        gelu(j2 * 2 + i)
                        take_rows(j2 * 2 + (i + 2))
                        take_out(j2 * 2 + i, i, j2)
                for i in range(2):
                    gelu(N - 2 + i)
                    take_out(N - 2 + i, i, N // 2 - 1)

            @block.gpsimd
            def _(pool):
                with pool.Fori(0, N // 2) as j2:
                    for i in range(2):
                        pool.wait_ge(y_ready, j2 * 2 + (i + 2))
                        pool.dma_start(rows_out[j2 * 2 + i], y[:, i, :]).then_inc(stored[i], 16)
                for i in range(2):
                    pool.wait_ge(stored[i], 16 * N // 2)
        s.clear_semaphores()


def finish_layer0(nc, io, keep):
    with ExitStack() as ctx:
        s = Space(nc, ctx, "fin0")
        XN, X2 = keep.XN, keep.X2
        bo, gamma, beta = (s.sb(n, [P, D]) for n in ("bo", "gamma", "beta"))
        got = s.sb("got", [P, 2, TPG, D])
        xin = s.sb("xin", [P, 2, TPG, D])
        y = s.sb("y", [P, TPG, D])
        gate = s.sb("gate", [P, TPG, D])
        x1 = s.sb("x1", [P, 2, TPG, D])
        index_now = s.sb("index_now", [P, 2, TPG, 1], U32)
        stats, mv, ve, rs = s.sb("stats", [P, TPG, 6]), s.sb("mv", [P, TPG, 2]), s.sb("ve", [P, TPG]), s.sb("rs", [P, TPG])
        mv_all, ve_all = s.sb("mv_all", [P, NT, 2]), s.sb("ve_all", [P, NT])
        loaded = s.sem("loaded")
        x_loaded = [s.sem(f"x_loaded{i}") for i in range(2)]
        gathered = [s.sem(f"gathered{i}") for i in range(2)]
        x1_ready, biases, all_var_ready = s.sem("x1_ready"), s.sem("biases"), s.sem("all_var_ready")
        stored = [s.sem(f"stored{i}") for i in range(2)]
        var_ready, rstd_ready = s.sem("var_ready"), s.sem("rstd_ready")
        normed, gate_ready = s.sem("normed"), s.sem("gate_ready")
        groups = io["L0_attn_x"].rearrange("b (g n p) d -> (b g) p n d", p=P, n=TPG)
        x1_groups = io["x1"].rearrange("(g n p) d -> g p n d", p=P, n=TPG)
        rows4 = lambda row: row[:].unsqueeze(1).to_broadcast([P, TPG, D])
        with nc.Block() as block:
            @block.sync
            def _(sp):
                n = load_bias_rows(sp, loaded, [(bo[:], io["L0_ffn_bo"]), (gamma[:], io["L0_ffn_gamma"]),
                                                (beta[:], io["L0_ffn_beta"])])
                for i in range(2):
                    sp.dma_start(xin[:, i, :, :], groups[i]).then_inc(x_loaded[i], 16)
                sp.wait_ge(loaded, n)
                sp.sem_inc(biases, 1)
                with sp.Fori(0, NG // 2 - 1) as g2:
                    for i in range(2):
                        sp.wait_ge(x1_ready, g2 * 2 + (i + 1))
                        sp.dma_start(x1_groups[g2 * 2 + i], x1[:, i, :, :]).then_inc(stored[i], 16)
                        sp.dma_start(xin[:, i, :, :], groups[g2 * 2 + (i + 2)]).then_inc(x_loaded[i], 16)
                for i in range(2):
                    sp.wait_ge(x1_ready, NG - 1 + i)
                    sp.dma_start(x1_groups[NG - 2 + i], x1[:, i, :, :]).then_inc(stored[i], 16)
                for i in range(2):
                    sp.wait_ge(stored[i], 16 * (NG // 2 + 1))

            @block.gpsimd
            def _(pool):
                def gather(g, i):
                    for n in range(TPG):
                        pool.tensor_copy(index_now[:, i, n, :], keep.slot[:, bass.ds(g * TPG + n, 1)])
                    pool.drain()
                    for n in range(TPG):
                        pool.indirect_dma_start(got[:, i, n, :], None, io["rows_out"],
                                                bass.IndirectOffsetOnAxis(ap=index_now[:, i, n, :], axis=0))\
                            .then_inc(gathered[i], 16)

                def rstds(k):
                    pool.wait_ge(var_ready, k)
                    pool.tensor_tensor(rs[:], ve[:], keep.minus_half[:, 0:TPG], ALU.pow).then_inc(rstd_ready, 1)

                for i in range(2):
                    gather(i, i)
                with pool.Fori(0, NG // 2 - 1) as g2:
                    for i in range(2):
                        rstds(g2 * 4 + (2 * i + 1))
                        rstds(g2 * 4 + (2 * i + 2))
                        pool.wait_ge(x1_ready, g2 * 2 + (i + 1))
                        gather(g2 * 2 + (i + 2), i)
                for i in range(2):
                    rstds(2 * NG - 4 + 2 * i + 1)
                    rstds(2 * NG - 4 + 2 * i + 2)
                pool.wait_ge(all_var_ready, 1)
                pool.tensor_tensor(keep.rstd[:, 0:NT], ve_all[:], keep.minus_half[:], ALU.pow).then_inc(rstd_ready, 1)

            @block.scalar
            def _(act):
                with act.Fori(0, NG) as g:
                    act.wait_ge(normed, g + 1)
                    act.activation(gate[:], y[:], ACT.Silu).then_inc(gate_ready, 1)

            @block.vector
            def _(dve):
                for i in range(2):
                    dve.sem_inc(stored[i], 16)
                dve.wait_ge(biases, 1)

                def statistics(src, k, eps):
                    for n in range(TPG):
                        dve.bn_stats(stats[:, n, :], src(n))
                    dve.drain()
                    for n in range(TPG):
                        dve.bn_aggr(mv[:, n, :], stats[:, n, :])
                    dve.drain()
                    dve.tensor_scalar(ve[:], mv[:, :, 1], eps, None, ALU.add).then_inc(var_ready, 1)
                    dve.wait_ge(rstd_ready, k)

                def group(g2, i):
                    g = g2 * 2 + i
                    dve.tensor_tensor(y[:], XN[:, bass.ds(g * TPG + 1, TPG), :], rows4(bo), ALU.add)
                    dve.drain()
                    dve.wait_ge(gathered[i], g2 * (16 * TPG) + 16 * TPG)
                    dve.tensor_tensor(y[:], y[:], got[:, i, :, :], ALU.add)
                    dve.drain()
                    statistics(lambda n: y[:, n, :], g2 * 4 + (2 * i + 1), 1e-12)
                    for n in range(TPG):
                        dve.tensor_scalar(y[:, n, :], y[:, n, :], mv[:, n, 0:1], rs[:, n:n + 1], ALU.subtract, ALU.mult)
                    dve.drain()
                    dve.tensor_tensor(y[:], y[:], rows4(gamma), ALU.mult)
                    dve.drain()
                    dve.tensor_tensor(y[:], y[:], rows4(beta), ALU.add).then_inc(normed, 1)
                    dve.wait_ge(gate_ready, g + 1)
                    dve.tensor_tensor(gate[:], gate[:], X2[:, bass.ds(g * TPG + 1, TPG), :], ALU.mult)
                    dve.drain()
                    dve.wait_ge(x_loaded[i], g2 * 16 + 16)
                    dve.wait_ge(stored[i], g2 * 16 + 16)
                    dve.tensor_tensor(x1[:, i, :, :], xin[:, i, :, :], gate[:], ALU.add).then_inc(x1_ready, 1)
                    dve.drain()
                    statistics(lambda n: x1[:, i, n, :], g2 * 4 + (2 * i + 2), 1e-5)
                    for n in range(TPG):
                        dve.tensor_scalar(XN[:, g * TPG + (n + 1), :], x1[:, i, n, :], mv[:, n, 0:1], rs[:, n:n + 1],
                                          ALU.subtract, ALU.mult)
                    dve.drain()
                    for n in range(TPG):
                        dve.bn_stats(stats[:, n, :], XN[:, g * TPG + (n + 1), :])
                    dve.drain()
                    for n in range(TPG):
                        dve.bn_aggr(mv[:, n, :], stats[:, n, :])
                    dve.drain()
                    dve.tensor_copy(mv_all[:, bass.ds(g * TPG, TPG), :], mv[:])
                    dve.drain()

                with dve.Fori(0, NG // 2) as g2:
                    for i in range(2):
                        group(g2, i)
                dve.tensor_copy(keep.mean[:, 0:NT], mv_all[:, :, 0])
                dve.tensor_scalar(ve_all[:], mv_all[:, :, 1], 1e-5, None, ALU.add).then_inc(all_var_ready, 1)
                dve.wait_ge(rstd_ready, 2 * NG + 1)
        s.clear_semaphores()


def feed_forward(nc, io, keep, gated, layer=0):
    HID = int(D * 4 * 2 / 3) if gated else 4 * D
    IC = -(-HID // P)
    rows = [min(P, HID - m * P) for m in range(IC)]
    TOK = TPG * P
    RING = 2 if gated else 4
    with ExitStack() as ctx:
        s = Space(nc, ctx, "ffn" if gated else "mlp")
        XN, X2 = keep.XN, keep.X2
        W = 2 * HID if gated else HID
        w1 = s.sb("w1", [P, KC, W])
        w2 = s.sb("w2", [P, IC, D])
        b1 = s.sb("b1", [P, 1 + gated, IC])
        b2 = s.sb("b2", [P, D])
        gain, offset = s.sb("gain", [P, KC]), s.sb("offset", [P, KC])
        h = s.sb("h", [P, TPG, D])
        hT = s.sb("hT", [P, KC, TOK])
        inner = s.sb("inner", [P, IC, TOK])
        gel = s.sb("gel", [P, 2, TOK])
        result = s.sb("result", [P, TPG, D])
        stats, mv = s.sb("stats", [P, TPG, 6]), s.sb("mv", [P, TPG, 2])
        ve, rs = s.sb("ve", [P, TPG]), s.sb("rs", [P, TPG])
        turned = [s.ps(f"turned{c}") for c in range(KC)]
        hidden = [[s.ps(f"hidden{i}{k}") for k in range(1 + gated)] for i in range(RING)]
        out = [s.ps(f"out{i}") for i in range(2)]
        loaded, biases, h_loaded = s.sem("loaded"), s.sem("biases"), s.sem("h_loaded")
        var_ready, rstd_ready = s.sem("var_ready"), s.sem("rstd_ready")
        h_ready = s.count("h_ready", 1)
        turned_ready, hT_ready = s.count("turned_ready", KC), s.count("hT_ready", KC)
        hidden_ready, gel_ready = s.count("hidden_ready", IC), s.count("gel_ready", IC)
        inner_ready = s.count("inner_ready", IC, credit=RING)
        out_ready, out_taken = s.count("out_ready", TPG), s.count("out_taken", TPG, credit=2)
        stored = s.sem("stored")
        result_ready = s.sem("result_ready")
        with nc.Block() as block:
            @block.sync
            def _(sp):
                pre = "L1_ffn_" if gated else "L1_attn_"
                of = (lambda name: io[pre + name][layer]) if gated else (lambda name: io[pre + name])
                mine = (lambda name: io["ffn_" + name][layer]) if gated else (lambda name: io["mlp_" + name])
                whole = HID // P
                n = 0
                pairs = [(w1[:], of("w1").rearrange("(c p) n -> p c n", p=P)),
                         (w2[:, 0:whole, :], of("w2")[0:whole * P, :].rearrange("(c p) n -> p c n", p=P)),
                         (gain[:], mine("gain")), (offset[:], mine("offset")), (b1[:], mine("b1"))]
                if whole < IC:
                    pairs.append((w2[0:rows[-1], whole, :], of("w2")[whole * P:, :]))
                for dst, src in pairs:
                    sp.dma_start(dst, src).then_inc(loaded, 16)
                    n += 16
                n += load_bias_rows(sp, loaded, [(b2[:], of("b2"))])

                def load_h(g):
                    half = D // 2
                    sp.dma_start(h[:, :, 0:half], X2[:, bass.ds(g * TPG + 1, TPG), 0:half]).then_inc(h_loaded, 16)
                    sp.dma_start(h[1:P, :, half:], X2[0:P - 1, bass.ds(g * TPG + 1, TPG), half:]).then_inc(h_loaded, 16)
                    sp.dma_start(h[0:1, :, half:], X2[P - 1:P, bass.ds(g * TPG, TPG), half:]).then_inc(h_loaded, 16)

                if gated:
                    load_h(0)
                sp.wait_ge(loaded, n)
                sp.sem_inc(biases, 1)
                if gated:
                    with sp.Fori(1, NG) as g:
                        sp.wait_ge(turned_ready.sem, turned_ready.at(g, 0))
                        load_h(g)
                else:
                    groups = io["s1"].rearrange("(g n p) d -> g p n d", p=P, n=TPG)
                    with sp.Fori(0, NG) as g:
                        sp.wait_ge(result_ready, g + 1)
                        sp.dma_start(groups[g], result[:]).then_inc(stored, 16)
                    sp.wait_ge(stored, 16 * NG + 16)

            if gated:
                @block.gpsimd
                def _(pool):
                    with pool.Fori(0, NG) as g:
                        pool.wait_ge(var_ready, g + 1)
                        pool.tensor_tensor(rs[:], ve[:], keep.minus_half[:, 0:TPG], ALU.pow).then_inc(rstd_ready, 1)

            @block.tensor
            def _(pe):
                pe.wait_ge(biases, 1)

                def turn(g):
                    pe.wait_ge(h_ready.sem, h_ready.at(g, 1))
                    for c in range(KC):
                        for n in range(TPG):
                            last = pe.transpose(turned[c][:, n * P:(n + 1) * P], h[:, n, c * P:(c + 1) * P], keep.ident[:])
                        last.then_inc(turned_ready.sem, 1)

                def hide(g):
                    pe.wait_ge(hT_ready.sem, hT_ready.at(g, KC))
                    for m in range(IC):
                        pe.wait_ge(inner_ready.sem, inner_ready.at(g, m + 1 - RING))
                        for k in range(1 + gated):
                            for c in range(KC):
                                a = k * HID + m * P
                                last = pe.matmul(hidden[m % RING][k][0:rows[m], :], w1[:, c, a:a + rows[m]], hT[:, c, :],
                                                 start=(c == 0), stop=(c == KC - 1))
                        last.then_inc(hidden_ready.sem, 1)

                def project(g):
                    pe.wait_ge(inner_ready.sem, inner_ready.at(g, IC))
                    for n in range(TPG):
                        pe.wait_ge(out_taken.sem, out_taken.at(g, n - 1))
                        for m in range(IC):
                            last = pe.matmul(out[n % 2][:, 0:D],
                                             inner[0:rows[m], m, n * P:(n + 1) * P], w2[0:rows[m], m, :],
                                             start=(m == 0), stop=(m == IC - 1))
                        last.then_inc(out_ready.sem, 1)

                turn(0)
                with pe.Fori(0, NG - 1) as g:
                    hide(g)
                    turn(g + 1)
                    project(g)
                hide(NG - 1)
                project(NG - 1)

            @block.scalar
            def _(act):
                if not gated:
                    act.sem_inc(inner_ready.sem, RING)
                act.wait_ge(biases, 1)

                def take_turned(g):
                    for c in range(KC):
                        act.wait_ge(turned_ready.sem, turned_ready.at(g, c + 1))
                        act.activation(hT[:, c, :], turned[c][:], ACT.Identity, bias=offset[:, c:c + 1],
                                       scale=gain[:, c:c + 1]).then_inc(hT_ready.sem, 1)

                def gelus(g):
                    for m in range(IC):
                        act.wait_ge(hidden_ready.sem, hidden_ready.at(g, m + 1))
                        if gated:
                            act.wait_ge(inner_ready.sem, inner_ready.at(g, m + 1 - RING))
                            act.activation(gel[0:rows[m], m % 2, :], hidden[m % RING][1][0:rows[m], :], ACT.Gelu,
                                           bias=b1[0:rows[m], 1, m:m + 1]).then_inc(gel_ready.sem, 1)
                        else:
                            act.activation(inner[:, m, :], hidden[m % RING][0][:], ACT.Gelu,
                                           bias=b1[:, 0, m:m + 1]).then_inc(inner_ready.sem, 1)

                take_turned(0)
                with act.Fori(0, NG - 1) as g:
                    gelus(g)
                    take_turned(g + 1)
                gelus(NG - 1)

            @block.vector
            def _(dve):
                dve.sem_inc(out_taken.sem, out_taken.credit)
                if gated:
                    dve.sem_inc(inner_ready.sem, RING)
                else:
                    dve.sem_inc(stored, 16)
                dve.wait_ge(biases, 1)

                def make_h(g, first):
                    if gated:
                        dve.wait_ge(h_loaded, g * 48 + 48)
                        dve.tensor_scalar(h[0:1, 0, D // 2:], h[0:1, 0, D // 2:], keep.going[0:1, bass.ds(g, 1)], None, ALU.mult)
                        dve.drain()
                        for n in range(TPG):
                            dve.bn_stats(stats[:, n, :], h[:, n, :])
                        dve.drain()
                        for n in range(TPG):
                            dve.bn_aggr(mv[:, n, :], stats[:, n, :])
                        dve.drain()
                        dve.tensor_scalar(ve[:], mv[:, :, 1], 1e-5, None, ALU.add).then_inc(var_ready, 1)
                        dve.wait_ge(rstd_ready, g + 1)
                        for n in range(TPG):
                            dve.tensor_scalar(h[:, n, :], h[:, n, :], mv[:, n, 0:1], rs[:, n:n + 1], ALU.subtract, ALU.mult)
                    else:
                        if not first:
                            dve.wait_ge(turned_ready.sem, turned_ready.at(g, 0))
                        for n in range(TPG):
                            t = g * TPG + n
                            dve.tensor_scalar(h[:, n, :], X2[:, g * TPG + (n + 1), :], keep.mean[:, bass.ds(t, 1)],
                                              keep.rstd[:, bass.ds(t, 1)], ALU.subtract, ALU.mult)
                    dve.drain()
                    dve.sem_inc(h_ready.sem, 1)

                def multiply(g):
                    for m in range(IC):
                        dve.wait_ge(gel_ready.sem, gel_ready.at(g, m + 1))
                        dve.scalar_tensor_tensor(inner[0:rows[m], m, :], hidden[m % RING][0][0:rows[m], :],
                                                 b1[0:rows[m], 0, m:m + 1], gel[0:rows[m], m % 2, :],
                                                 ALU.add, ALU.mult).then_inc(inner_ready.sem, 1)

                def take_out(g):
                    if not gated:
                        dve.wait_ge(stored, g * 16 + 16)
                    for n in range(TPG):
                        dve.wait_ge(out_ready.sem, out_ready.at(g, n + 1))
                        dve.tensor_tensor(result[:, n, :], out[n % 2][:, 0:D], b2[:], ALU.add)\
                           .then_inc(out_taken.sem, 1)
                    dve.drain()
                    slots = bass.ds(g * TPG + 1, TPG)
                    if gated:
                        dve.tensor_tensor(XN[:, slots, :], result[:], X2[:, slots, :], ALU.add)
                        dve.drain()
                    else:
                        dve.tensor_tensor(result[:], result[:], X2[:, slots, :], ALU.add).then_inc(result_ready, 1)

                make_h(0, True)
                with dve.Fori(0, NG - 1) as g:
                    make_h(g + 1, False)
                    if gated:
                        multiply(g)
                    take_out(g)
                if gated:
                    multiply(NG - 1)
                take_out(NG - 1)
        s.clear_semaphores()


RH, RD = 8, 64
RI = RH * RD


def rotary_attention(nc, io, keep, layer):
    ST = RH // 2
    U = ST * TPG
    prologue = [("hT", 0), ("q", 0), ("k", 0), ("v", 0), ("hT", 1), ("q", 1), ("k", 1), ("v", 1), ("QT", 0), ("KT", 0),
                ("hT", 2)]
    plan = [(("q", 2), ("k", 2)), (("QT", 1), ("KT", 1)), (("v", 2), ("oT", -1)), (("hT", 3), ("out", -1))]
    order = [(name, n + ahead) for n in range(TPG) for pair in plan for name, ahead in pair]
    NACT = len(order) - TPG
    where = lambda m: 1 + m % TPG

    with ExitStack() as ctx:
        s = Space(nc, ctx, "rot")
        XN, X2 = keep.XN, keep.X2
        w_qkv = s.sb("w_qkv", [P, KC, 3 * RI])
        w_out = s.sb("w_out", [P, RI // P, D])
        scales = s.sb("scales", [P, 2, RD])
        NTAB = SEQ // P + 2
        cos, sin = s.sb("cos", [P, 2, NTAB, RD]), s.sb("sin", [P, 2, NTAB, RD])
        mask = s.sb("mask", [P, NG + 1, 2 * P], BF16)
        h = s.sb("h", [P, TPG, D])
        hT = s.sb("hT", [P, KC, P])
        qk = s.sb("qk", [P, 2, 2, RI])
        square, turn_a = s.sb("square", [P, 2, RI]), s.sb("turn_a", [P, 2, RI])
        rot = s.sb("rot", [P, 2, RI])
        ss, rnorm = s.sb("ss", [P, 2 * RH]), s.sb("rnorm", [P, 2 * RH])
        QT = s.sb("QT", [P, 2, 4, P])
        KT = s.sb("KT", [P, 4, (TPG + 1) * P])
        V = s.sb("V", [P, TPG + 1, RI])
        probs, probsT = s.sb("probs", [P, 4, BANK]), s.sb("probsT", [P, 2, BANK])
        negmax = s.sb("negmax", [P, 4, 2])
        sums, rsum = s.sb("sums", [P, 2, RH]), s.sb("rsum", [P, RH])
        attn, oT = s.sb("attn", [P, RI]), s.sb("oT", [P, RI // P, P])
        score = [s.ps(f"score{i}") for i in range(4)]
        turned, po = s.ps("turned"), s.ps("po")
        lin = [s.ps(f"lin{i}") for i in range(2)]

        loaded, biases, zeroed = s.sem("loaded"), s.sem("biases"), s.sem("zeroed")
        front_loaded, back_loaded = s.sem("front_loaded"), s.sem("back_loaded")
        h_ready = s.count("h_ready", 1)
        lin_ready = s.count("lin_ready", len(order), credit=len(prologue))
        act_took = s.count("act_took", NACT, credit=len(prologue))
        dve_took = s.count("dve_took", TPG, credit=1)
        scores_ready, max_ready = s.count("scores_ready", U), s.count("max_ready", U)
        probs_ready = s.count("probs_ready", U, credit=4)
        turned_ready = s.count("turned_ready", U, credit=4)
        probsT_ready = s.count("probsT_ready", U, credit=1)
        pv_done = s.count("pv_done", U, credit=2)
        attn_ready = s.count("attn_ready", TPG, credit=1)
        squared, ss_ready, rn_ready = s.count("squared", TPG), s.count("ss_ready", TPG), s.count("rn_ready", TPG)
        normed, turned_a, rot_ready = s.count("normed", TPG), s.count("turned_a", TPG), s.count("rot_ready", TPG)

        def taken(it, i):
            if order[i][0] == "out":
                return dve_took.sem, dve_took.at(it, sum(name == "out" for name, _ in order[:max(i + 1, 0)]))
            return act_took.sem, act_took.at(it, sum(name != "out" for name, _ in order[:max(i + 1, 0)]))

        def heads_of(u):
            n, i = divmod(u, ST)
            return n, [4 * (i // 2) + i % 2, 4 * (i // 2) + i % 2 + 2]

        with nc.Block() as block:
            @block.sync
            def _(sp):
                n = 0
                pairs = [(w_qkv[:], io["L1_ffn_wqkv"][layer].rearrange("(c p) n -> p c n", p=P)),
                         (w_out[:], io["L1_ffn_wo"][layer].rearrange("(c p) n -> p c n", p=P)),
                         (cos[:], io["const_cos"]), (sin[:], io["const_sin"]), (mask[:], io["const_mask2"])]

                def load_h(g, first, done):
                    half = D // 2
                    two, at = slice(first, first + 2), g * TPG + first
                    sp.dma_start(h[:, two, 0:half], XN[:, bass.ds(at + 1, 2), 0:half]).then_inc(done, 16)
                    sp.dma_start(h[1:P, two, half:], XN[0:P - 1, bass.ds(at + 1, 2), half:]).then_inc(done, 16)
                    sp.dma_start(h[0:1, two, half:], XN[P - 1:P, bass.ds(at, 2), half:]).then_inc(done, 16)

                load_h(0, 0, front_loaded)
                for dst, src in pairs:
                    sp.dma_start(dst, src).then_inc(loaded, 16)
                    n += 16
                n += load_bias_rows(sp, loaded, [(scales[:, 0, :], io["L1_ffn_q_scale"][layer]),
                                                 (scales[:, 1, :], io["L1_ffn_k_scale"][layer])])
                load_h(0, 2, back_loaded)
                sp.wait_ge(loaded, n)
                sp.sem_inc(biases, 1)
                sp.wait_ge(lin_ready.sem, prologue.index(("hT", 1)) + 1)
                load_h(1, 0, front_loaded)

                def after(g, back, front):
                    sp.wait_ge(lin_ready.sem, lin_ready.at(g, order.index(("hT", 3)) + 1))
                    load_h(back, 2, back_loaded)
                    if front is not None:
                        sp.wait_ge(lin_ready.sem, lin_ready.at(g, order.index(("hT", 5)) + 1))
                        load_h(front, 0, front_loaded)

                with sp.Fori(0, NG - 2) as g:
                    after(g, g + 1, g + 2)
                after(NG - 2, NG - 1, 0)
                after(NG - 1, 0, None)
                sp.wait_ge(back_loaded, 48 * (NG + 1))

            @block.gpsimd
            def _(pool):
                pool.memset(KT[:, :, 0:P], 0.0)
                pool.memset(V[:], 0.0)
                pool.memset(probsT[:], 0.0)
                pool.drain()
                pool.sem_inc(zeroed, 1)
                pool.wait_ge(biases, 2)
                by_head = lambda t, i: t[:, i, :].rearrange("p (h d) -> p h d", d=RD)

                def square_up(it, m):
                    if m < 2:
                        pool.wait_ge(act_took.sem, prologue.index(("k", m)) + 1)
                    else:
                        pool.wait_ge(*taken(it, order.index(("k", m))))
                    pool.tensor_tensor(square[:], qk[:, m % 2, :, :], qk[:, m % 2, :, :], ALU.mult).then_inc(squared.sem, 1)
                    pool.wait_ge(ss_ready.sem, ss_ready.at(it, m + 1))
                    pool.tensor_tensor(rnorm[:], ss[:], keep.minus_half[:, 0:2 * RH], ALU.pow).then_inc(rn_ready.sem, 1)

                def times_cos(it, gi, m):
                    pool.wait_ge(normed.sem, normed.at(it, m + 1))
                    for i in range(2):
                        last = pool.tensor_tensor(by_head(turn_a, i), by_head(qk[:, m % 2], i),
                                                  cos[:, i, bass.ds(gi * TPG + m, 1), :].to_broadcast([P, RH, RD]),
                                                  ALU.mult)
                    last.then_inc(turned_a.sem, 1)

                for m in range(2):
                    square_up(0, m)
                    times_cos(0, 0, m)
                with pool.Fori(0, BATCH) as b:
                    with pool.Fori(0, GPB) as gi:
                        for n in range(TPG):
                            square_up(b * GPB + gi, n + 2)
                            times_cos(b * GPB + gi, gi, n + 2)

            @block.tensor
            def _(pe):
                pe.sem_inc(turned_ready.sem, turned_ready.credit)
                pe.sem_inc(pv_done.sem, 1)
                pe.wait_ge(zeroed, 1)
                pe.wait_ge(biases, 1)
                pe.matmul(po[:], keep.ident[:], V[:, 0, :], start=True, stop=True)

                def linear_work(it, name, m, lin):
                    if name == "hT":
                        for c in range(KC):
                            last = pe.transpose(lin[:, c * P:(c + 1) * P], h[:, m % TPG, c * P:(c + 1) * P], keep.ident[:])
                    elif name in ("q", "k", "v"):
                        a = "qkv".index(name) * RI
                        for c in range(KC):
                            last = pe.matmul(lin[:], hT[:, c, :], w_qkv[:, c, a:a + RI], start=(c == 0), stop=(c == KC - 1))
                    elif name in ("QT", "KT"):
                        pe.wait_ge(rot_ready.sem, rot_ready.at(it, m + 1))
                        for c in range(4):
                            last = pe.transpose(lin[:, c * P:(c + 1) * P], rot[:, "QK".index(name[0]), c * P:(c + 1) * P],
                                                keep.ident[:])
                    elif name == "oT":
                        pe.wait_ge(attn_ready.sem, attn_ready.at(it, m + 1))
                        for c in range(RI // P):
                            last = pe.transpose(lin[:, c * P:(c + 1) * P], attn[:, c * P:(c + 1) * P], keep.ident[:])
                    else:
                        for c in range(RI // P):
                            last = pe.matmul(lin[:, 0:D], oT[:, c, :], w_out[:, c, :], start=(c == 0), stop=(c == RI // P - 1))
                    last.then_inc(lin_ready.sem, 1)

                def linear_step(it, name, m):
                    i = order.index((name, m))
                    pe.wait_ge(*taken(it, i - 2))
                    if name == "hT" and m == TPG:
                        pe.wait_ge(h_ready.sem, h_ready.at(it, 2))
                    if name == "hT" and m == TPG + 2:
                        pe.wait_ge(back_loaded, it * 48 + 96)
                    linear_work(it, name, m, lin[i % 2])

                def scores(it, g, u):
                    n, heads = heads_of(u)
                    bank = score[u % 4]
                    pe.wait_ge(probs_ready.sem, probs_ready.at(it, u - 3))
                    if u == 0:
                        pe.wait_ge(act_took.sem, prologue.index(("KT", 0)) + 1)
                    elif u % ST == 0:
                        i = order.index(("KT", n))
                        pe.wait_ge(*taken(it, i))
                    m = mask[:, bass.ds(g + n // TPG, 1), :] if n % TPG == 0 else mask[:, 1:2, :]
                    pe.matmul(bank[:], keep.identb[:], m.to_broadcast([P, 2, 2 * P]), start=True, stop=False)
                    for j in range(2):
                        c, half = divmod(heads[j], 2)
                        rows = slice(RD * half, RD * (half + 1))
                        first = n % TPG * P
                        last = pe.matmul(bank[:, j * 2 * P:(j + 1) * 2 * P], QT[rows, n % 2, c, :],
                                         KT[rows, c, first:first + 2 * P], start=False, stop=(j == 1))
                    last.then_inc(scores_ready.sem, 1)

                def turn(it, u):
                    pe.wait_ge(probs_ready.sem, probs_ready.at(it, u + 1))
                    pe.wait_ge(probsT_ready.sem, probsT_ready.at(it, u))
                    for i in range(4):
                        last = pe.transpose(turned[:, i * P:(i + 1) * P], probs[:, u % 4, i * P:(i + 1) * P], keep.ident[:])
                    last.then_inc(turned_ready.sem, 1)

                def weigh(it, u):
                    n, heads = heads_of(u)
                    pe.wait_ge(probsT_ready.sem, probsT_ready.at(it, u + 1))
                    if u % ST == 0:
                        pe.wait_ge(attn_ready.sem, attn_ready.at(it, n))
                    for j in range(2):
                        a = heads[j] * RD
                        for kb in range(2):
                            last = pe.matmul(po[:, a:a + RD], probsT[:, u % 2, (2 * j + kb) * P:(2 * j + kb + 1) * P],
                                             V[:, n % TPG + kb, a:a + RD], start=(kb == 0), stop=(kb == 1))
                    last.then_inc(pv_done.sem, 1)

                for i, (name, m) in enumerate(prologue):
                    if i > 0:
                        pe.wait_ge(act_took.sem, i)
                    if (name, m) == ("hT", 0):
                        pe.wait_ge(h_ready.sem, 1)
                    if (name, m) == ("hT", 2):
                        pe.wait_ge(back_loaded, 48)
                    linear_work(0, name, m, lin[i % 2])
                scores(0, 0, 0)
                scores(0, 0, 1)
                with pe.Fori(0, NG) as g:
                    for u in range(U):
                        n, st = divmod(u, ST)
                        one, two = plan[st]
                        linear_step(g, one[0], n + one[1])
                        scores(g, g, u + 2)
                        linear_step(g, two[0], n + two[1])
                        turn(g, u)
                        weigh(g, u - 1)
                weigh(NG - 1, U - 1)
                pe.wait_ge(*taken(NG, -2))
                linear_work(NG - 1, "oT", TPG - 1, lin[0])
                pe.wait_ge(*taken(NG, -1))
                pe.wait_ge(act_took.sem, act_took.at(NG, 1))
                linear_work(NG - 1, "out", TPG - 1, lin[1])

            @block.scalar
            def _(act):
                act.sem_inc(probs_ready.sem, probs_ready.credit)
                act.wait_ge(biases, 1)
                act.wait_ge(zeroed, 1)

                def take(name, m, lin):
                    if name == "hT":
                        last = act.activation(hT[:].rearrange("p c n -> p (c n)"), lin[:, 0:D], ACT.Copy)
                    elif name in ("q", "k"):
                        last = act.activation(qk[:, m % 2, "qk".index(name), :], lin[:], ACT.Copy)
                    elif name == "v":
                        last = act.activation(V[:, where(m), :], lin[:], ACT.Copy)
                        if where(m) == TPG:
                            last = act.activation(V[:, 0, :], lin[:], ACT.Copy)
                    elif name == "QT":
                        last = act.activation(QT[:, m % 2, :, :].rearrange("p c n -> p (c n)"), lin[:], ACT.Copy)
                    elif name == "KT":
                        by_chunk = lin[:].rearrange("p (c n) -> p c n", c=4)
                        last = act.activation(KT[:, :, where(m) * P:(where(m) + 1) * P], by_chunk, ACT.Copy)
                        if where(m) == TPG:
                            last = act.activation(KT[:, :, 0:P], by_chunk, ACT.Copy)
                    else:
                        last = act.activation(oT[:].rearrange("p c n -> p (c n)"), lin[:], ACT.Copy)
                    last.then_inc(act_took.sem, 1)

                def linear_step(it, name, m):
                    if name != "out":
                        i = order.index((name, m))
                        act.wait_ge(lin_ready.sem, lin_ready.at(it, i + 1))
                        take(name, m, lin[i % 2])

                def softmax(it, u):
                    n, heads = heads_of(u)
                    act.wait_ge(max_ready.sem, max_ready.at(it, u + 1))
                    act.wait_ge(turned_ready.sem, turned_ready.at(it, u - 3))
                    for j in range(2):
                        a = heads[j]
                        last = act.activation(probs[:, u % 4, j * 2 * P:(j + 1) * 2 * P],
                                              score[u % 4][:, j * 2 * P:(j + 1) * 2 * P], ACT.Exp,
                                              bias=negmax[:, u % 4, j:j + 1], accum_out=sums[:, n % 2, a:a + 1])
                    last.then_inc(probs_ready.sem, 1)

                for i, (name, m) in enumerate(prologue):
                    act.wait_ge(lin_ready.sem, i + 1)
                    take(name, m, lin[i % 2])
                softmax(0, 0)
                softmax(0, 1)
                with act.Fori(0, NG) as g:
                    for u in range(U):
                        n, st = divmod(u, ST)
                        one, two = plan[st]
                        linear_step(g, one[0], n + one[1])
                        softmax(g, u + 2)
                        linear_step(g, two[0], n + two[1])
                act.wait_ge(lin_ready.sem, lin_ready.at(NG, 1))
                take("oT", TPG - 1, lin[0])

            @block.vector
            def _(dve):
                dve.sem_inc(probsT_ready.sem, probsT_ready.credit)
                dve.sem_inc(dve_took.sem, dve_took.credit)
                dve.memset(sums[:], 1.0)
                dve.wait_ge(zeroed, 1)
                dve.wait_ge(biases, 1)
                half = RD // 2
                for i in range(2):
                    sc = lambda a, b: scales[:, i:i + 1, a:b].to_broadcast([P, NTAB, b - a])
                    dve.tensor_tensor(cos[:, i, :, :], cos[:, i, :, :], sc(0, RD), ALU.mult)
                    dve.tensor_tensor(sin[:, i, :, 0:half], sin[:, i, :, 0:half], sc(half, RD), ALU.mult)
                    dve.tensor_tensor(sin[:, i, :, half:], sin[:, i, :, half:], sc(0, half), ALU.mult)
                dve.drain()
                dve.sem_inc(biases, 1)
                every = lambda t: t.rearrange("p i (h d) -> p (i h) d", d=RD)

                def start_of_sequence(it):
                    dve.wait_ge(front_loaded, it * 48 + 48)
                    dve.tensor_scalar(h[0:1, 0, D // 2:], h[0:1, 0, D // 2:], keep.going[0:1, bass.ds(it, 1)], None, ALU.mult)
                    dve.drain()
                    dve.sem_inc(h_ready.sem, 1)

                def norms(it, m):
                    dve.wait_ge(squared.sem, squared.at(it, m + 1))
                    dve.tensor_reduce(ss[:], every(square[:]), AX.X, ALU.add)
                    dve.drain()
                    dve.tensor_scalar(ss[:], ss[:], 1e-24, None, ALU.max).then_inc(ss_ready.sem, 1)

                def divide(it, m):
                    dve.wait_ge(rn_ready.sem, rn_ready.at(it, m + 1))
                    both = every(qk[:, m % 2, :, :])
                    dve.tensor_tensor(both, both, bcast(rnorm[:], [P, 2 * RH, RD]), ALU.mult).then_inc(normed.sem, 1)

                def times_sin(it, gi, m):
                    by = lambda t, i, a, b: t[:, i, :].rearrange("p (h d) -> p h d", d=RD)[:, :, a:b]
                    table = lambda i, a, b: sin[:, i, bass.ds(gi * TPG + m, 1), a:b].to_broadcast([P, RH, b - a])
                    dve.drain()
                    for i in range(2):
                        dve.tensor_tensor(by(rot, i, 0, half), by(qk[:, m % 2], i, half, RD), table(i, 0, half), ALU.mult)
                        dve.tensor_tensor(by(rot, i, half, RD), by(qk[:, m % 2], i, 0, half), table(i, half, RD), ALU.mult)

                def rotate(it, m):
                    dve.drain()
                    dve.wait_ge(turned_a.sem, turned_a.at(it, m + 1))
                    dve.tensor_tensor(rot[:], rot[:], turn_a[:], ALU.add).then_inc(rot_ready.sem, 1)

                def maxima(it, u):
                    dve.wait_ge(scores_ready.sem, scores_ready.at(it, u + 1))
                    dve.tensor_reduce(negmax[:, u % 4, :], score[u % 4][:].rearrange("p (h k) -> p h k", h=2),
                                      AX.X, ALU.max, negate=True).then_inc(max_ready.sem, 1)

                def take_turned(it, u):
                    dve.wait_ge(turned_ready.sem, turned_ready.at(it, u + 1))
                    dve.wait_ge(pv_done.sem, pv_done.at(it, u - 1))
                    dve.tensor_copy(probsT[:, u % 2, :], turned[:]).then_inc(probsT_ready.sem, 1)

                def normalise(it, n):
                    dve.wait_ge(pv_done.sem, pv_done.at(it, (n + 1) * ST))
                    dve.reciprocal(rsum[:], sums[:, n % 2, :])
                    dve.drain()
                    dve.tensor_tensor(attn[:].rearrange("p (h d) -> p h d", d=RD), po[:].rearrange("p (h d) -> p h d", d=RD),
                                      bcast(rsum[:], [P, RH, RD]), ALU.mult).then_inc(attn_ready.sem, 1)

                def take_out(g, n, lin):
                    dve.tensor_tensor(X2[:, g * TPG + (n + 1), :], lin[:, 0:D], XN[:, g * TPG + (n + 1), :], ALU.add)\
                       .then_inc(dve_took.sem, 1)

                start_of_sequence(0)
                for m in range(2):
                    norms(0, m)
                    divide(0, m)
                    if m == 1:
                        dve.wait_ge(lin_ready.sem, prologue.index(("KT", 0)) + 1)
                    times_sin(0, 0, m)
                    if m == 0:
                        rotate(0, 0)
                maxima(0, 0)
                maxima(0, 1)

                def group(it, gi):
                    for u in range(U):
                        n, st = divmod(u, ST)
                        if st == 0:
                            rotate(it, n + 1)
                        maxima(it, u + 2)
                        take_turned(it, u)
                        if st == 0:
                            normalise(it, n - 1)
                        if u == 1:
                            start_of_sequence(it + 1)
                        if st == 1:
                            norms(it, n + 2)
                        if st == 2:
                            divide(it, n + 2)
                        if st == 3:
                            i = order.index(("out", n - 1))
                            dve.wait_ge(lin_ready.sem, lin_ready.at(it, i + 1))
                            take_out(it, n - 1, lin[i % 2])
                            times_sin(it, gi, n + 2)

                with dve.Fori(0, BATCH) as b:
                    with dve.Fori(0, GPB) as gi:
                        group(b * GPB + gi, gi)
                normalise(NG - 1, TPG - 1)
                dve.wait_ge(lin_ready.sem, lin_ready.at(NG, 2))
                take_out(NG - 1, TPG - 1, lin[1])
        s.clear_semaphores()


def combine(nc, io, keep):
    with ExitStack() as ctx:
        s = Space(nc, ctx, "comb")
        x1, s1 = s.sb("x1", [P, 2, TPG, D]), s.sb("s1", [P, 2, TPG, D])
        gate = s.sb("gate", [P, 2, TPG, D])
        x_loaded = [s.sem(f"x_loaded{i}") for i in range(2)]
        stored = [s.sem(f"stored{i}") for i in range(2)]
        gate_ready, result_ready = s.sem("gate_ready"), s.sem("result_ready")
        by_group = lambda name: io[name].rearrange("(g n p) d -> g p n d", p=P, n=TPG)
        with nc.Block() as block:
            @block.sync
            def _(sp):
                def load(g, i):
                    sp.dma_start(x1[:, i, :, :], by_group("x1")[g]).then_inc(x_loaded[i], 16)
                    sp.dma_start(s1[:, i, :, :], by_group("s1")[g]).then_inc(x_loaded[i], 16)

                for i in range(2):
                    load(i, i)
                def store(g2, i):
                    sp.wait_ge(result_ready, g2 * 2 + (i + 1))
                    sp.dma_start(by_group("out")[g2 * 2 + i], gate[:, i, :, :]).then_inc(stored[i], 16)

                with sp.Fori(0, NG // 2 - 1) as g2:
                    for i in range(2):
                        store(g2, i)
                        load(g2 * 2 + (i + 2), i)
                for i in range(2):
                    store(NG // 2 - 1, i)
                for i in range(2):
                    sp.wait_ge(stored[i], 16 * (NG // 2 + 1))

            @block.scalar
            def _(act):
                for i in range(2):
                    act.sem_inc(stored[i], 16)
                with act.Fori(0, NG // 2) as g2:
                    for i in range(2):
                        act.wait_ge(stored[i], g2 * 16 + 16)
                        act.activation(gate[:, i, :, :], keep.XN[:, bass.ds(g2 * (2 * TPG) + (i * TPG + 1), TPG), :],
                                       ACT.Silu).then_inc(gate_ready, 1)

            @block.vector
            def _(dve):
                with dve.Fori(0, NG // 2) as g2:
                    for i in range(2):
                        dve.wait_ge(gate_ready, g2 * 2 + (i + 1))
                        dve.wait_ge(x_loaded[i], g2 * 32 + 32)
                        dve.tensor_tensor(gate[:, i, :, :], gate[:, i, :, :], s1[:, i, :, :], ALU.mult)
                        dve.drain()
                        dve.tensor_tensor(gate[:, i, :, :], gate[:, i, :, :], x1[:, i, :, :], ALU.add)\
                           .then_inc(result_ready, 1)


def build(nc, io):
    rows = [SLOT_TILES * P, D]
    for name, shape in (("rows_in", rows), ("rows_out", rows), ("x1", [NT * P, D]), ("s1", [NT * P, D])):
        io[name] = nc.dram_tensor("scratch_" + name, shape, F32).ap()
    with ExitStack() as ctx:
        keep = Keep(nc, ctx)
        normalise_input(nc, io, keep)
        window_attention(nc, io, keep, 0)
        route(nc, io, keep)
        experts(nc, io, keep)
        finish_layer0(nc, io, keep)
        window_attention(nc, io, keep, 1)
        feed_forward(nc, io, keep, False)
        with nc.Fori(0, 2) as layer:
            rotary_attention(nc, io, keep, layer)
            feed_forward(nc, io, keep, True, layer)
        combine(nc, io, keep)


def layouts(inputs):
    def columns(v):
        c = -(-v.shape[0] // P)
        out = np.zeros((c * P,), v.dtype)
        out[:v.shape[0]] = v
        return out.reshape(c, P).T

    def heads_down(v):
        out = np.zeros((4, 32, v.shape[0] // 64), v.dtype)
        out[:, 0:HD, :] = v.reshape(-1, 4, HD).transpose(1, 2, 0)
        return out.reshape(P, -1)

    def heads_apart(w):
        out = np.zeros((P, KC, w.shape[1] // HD, 32), w.dtype)
        out[:, :, :, 0:HD] = w.reshape(KC, P, -1, HD).transpose(1, 0, 2, 3)
        return out

    x = {name: np.asarray(a) for name, a in inputs.items()}
    a = {"w_router": x["L0_ffn_Wr"].T.reshape(KC, P, EXPERTS).transpose(1, 0, 2),
         "win0_w_rq": heads_apart(x["L0_attn_rq_w"]), "win0_w_rk": heads_apart(x["L0_attn_rkv_w"][:, 0:LAT]),
         "win0_b_rq": heads_down(x["L0_attn_rq_b"]), "win0_b_rk": heads_down(x["L0_attn_rkv_b"][0:LAT]),
         "win1_gain": columns(x["L1_attn_ln1_g"]), "win1_offset": columns(x["L1_attn_ln1_b"]),
         "mlp_gain": columns(x["L1_attn_ln2_g"]), "mlp_offset": columns(x["L1_attn_ln2_b"]),
         "mlp_b1": columns(x["L1_attn_b1"])[:, None, :]}
    for layer, b in enumerate(("L0_attn_qkv_b", "L1_attn_b_qkv")):
        a[f"win{layer}_b_qk"] = columns(x[b][0:2 * D]).reshape(P, 2, KC)
    a["ffn_gain"] = np.stack([columns(v) for v in x["L1_ffn_ln_g"]])
    a["ffn_offset"] = np.stack([columns(v) for v in x["L1_ffn_ln_b"]])
    a["ffn_b1"] = np.stack([np.stack([columns(half) for half in np.split(v, 2)], axis=1) for v in x["L1_ffn_b1"]])
    return {name: np.ascontiguousarray(v) for name, v in a.items()}


def constants():
    bf16 = mybir.dt.np(BF16)
    c = {}
    q, k = np.arange(P)[:, None], np.arange(P)[None, :]
    c["ident"] = np.eye(P, dtype=np.float32)
    c["identb"] = np.eye(P).astype(bf16)
    c["earlier"] = (q < k).astype(bf16)
    first = np.arange(NG + 1) % GPB == 0
    c["going"] = np.broadcast_to(np.where(first, 0.0, 1.0), (P, NG + 1)).astype(np.float32)
    c["iota"] = np.broadcast_to(np.arange(SLOT_TILES), (P, SLOT_TILES)).astype(np.float32)

    def window(prev, cur, closed_at_start):
        m = np.zeros((P, NG + 1, 2 * P))
        for g in range(NG + 1):
            m[:, g, 0:P] = np.where(prev & ~(closed_at_start & first[g]), 0.0, NEG)
            m[:, g, P:] = np.where(cur, 0.0, NEG)
        return m.astype(bf16)

    c["mask0"] = window((k >= q) & (k >= 1), k < q, True)
    own_first = (q < P // 2) == (k < P // 2)
    c["mask1"] = np.where(~own_first | (k <= q), 0.0, NEG).astype(bf16)
    c["mask2"] = window(k >= q, k <= q, True)
    c["parity"] = np.stack([(np.arange(P) // HD % 2 == odd).astype(np.float32) for odd in range(2)], axis=1)
    tile = np.arange(NT + 1) % (SEQ // P)
    chunk = tile[None, :, None] * LPT + (np.arange(P) // CHUNK)[:, None, None]
    c["lat_mask"] = np.where((np.arange(LAT) + LPT)[None, None, :] % LAT < chunk, 0.0, NEG).astype(bf16)
    valid = np.ones((P, NG + 1, 2), np.float32)
    valid[0, first, 0] = 0.0
    valid[0:CHUNK, first, 1] = 0.0
    c["valid"] = valid

    f = np.float32
    half = np.arange(0, RD, 2, dtype=f)
    inv_freq = f(1.0) / np.power(f(10000.0), half / f(RD))
    t = np.arange(SEQ, dtype=f)
    freqs = t[:, None] * inv_freq[None, :]
    base = (half + f(0.4 * RD)) / f(1.4 * RD)
    power = (t - f(SEQ // 2)) / f(P // 2)
    scale = np.power(base[None, :], power[:, None])
    cos, sin = np.cos(freqs), np.sin(freqs)
    two = lambda a, b: np.concatenate([a, b], axis=-1)
    tables = {"cos": (two(cos * scale, cos * scale) * f(8.0), two(cos / scale, cos / scale)),
              "sin": (two(-sin * scale, sin * scale) * f(8.0), two(-sin / scale, sin / scale))}
    for name, pair in tables.items():
        a = np.stack([x.reshape(SEQ // P, P, RD) for x in pair]).transpose(2, 0, 1, 3)
        c[name] = np.ascontiguousarray(np.concatenate([a, a[:, :, 0:2]], axis=2)).astype(f)
    return {f"const_{k}": np.ascontiguousarray(v) for k, v in c.items()}


_INS = ["L0_attn_x", "L0_attn_qkv_w", "L0_attn_qkv_b", "L0_attn_rq_w", "L0_attn_rq_b", "L0_attn_rkv_w", "L0_attn_rkv_b",
        "L0_attn_rout_w", "L0_attn_rout_b", "L0_attn_out_w", "L0_attn_out_b", "L0_attn_gl_w", "L0_attn_gr_w", "L0_ffn_Wr",
        "L0_ffn_W1", "L0_ffn_b1", "L0_ffn_Wo", "L0_ffn_bo", "L0_ffn_gamma", "L0_ffn_beta", "L1_attn_ln1_g",
        "L1_attn_ln1_b", "L1_attn_w_qkv", "L1_attn_b_qkv", "L1_attn_w_out", "L1_attn_b_out", "L1_attn_ln2_g",
        "L1_attn_ln2_b", "L1_attn_w1", "L1_attn_b1", "L1_attn_w2", "L1_attn_b2", "L1_ffn_wqkv", "L1_ffn_q_scale",
        "L1_ffn_k_scale", "L1_ffn_wo", "L1_ffn_ln_g", "L1_ffn_ln_b", "L1_ffn_w1", "L1_ffn_b1", "L1_ffn_w2", "L1_ffn_b2"]


def kernel(**inputs):
    import concourse.bacc as bacc
    from concourse.bass_utils import run_bass_kernel_spmd

    nc = bacc.Bacc("TRN2", target_bir_lowering=False, num_devices=1)
    arrays = {name: np.ascontiguousarray(inputs[name]) for name in _INS}
    arrays.update(layouts(inputs))
    arrays.update(constants())
    io = {name: nc.dram_tensor("in_" + name, a.shape, mybir.dt.from_np(a.dtype), kind="ExternalInput").ap()
          for name, a in arrays.items()}
    out = nc.dram_tensor("out", (BATCH, SEQ, D), F32, kind="ExternalOutput").ap()
    io["out"] = out.rearrange("b n d -> (b n) d")
    build(nc, io)
    r = run_bass_kernel_spmd(nc, [{"in_" + name: a for name, a in arrays.items()}], core_ids=[0])
    return r.results[0]["out"]
```

```python
from contextlib import ExitStack

import numpy as np
import concourse.bass as bass
from concourse import mybir

F32 = mybir.dt.float32
BF16 = mybir.dt.bfloat16
U32 = mybir.dt.uint32
ALU = mybir.AluOpType
ACT = mybir.ActivationFunctionType
AX = mybir.AxisListType

P = 128
D = 256
KC = D // P
BATCH, SEQ = 2, 2048
NT = BATCH * SEQ // P
TPG = 4
NG = NT // TPG
GPB = SEQ // P // TPG
BANK = 512
NEG = -1.0e30
EXPERTS, INNER = 8, 1024
SLOT_TILES = NT + EXPERTS


class Count:

    def __init__(self, sem, per, credit=0):
        self.sem, self.per, self.credit = sem, per, credit

    def at(self, it, k):
        return it * self.per + (k + self.credit)


class Space:

    def __init__(self, nc, ctx, stage):
        self.nc, self.ctx, self.stage = nc, ctx, stage
        self.sems = []

    def sb(self, name, shape, dt=F32):
        return self.ctx.enter_context(self.nc.sbuf_tensor(f"{self.stage}_{name}", shape, dt))

    def ps(self, name, shape=(P, BANK), dt=F32):
        return self.ctx.enter_context(self.nc.psum_tensor(f"{self.stage}_{name}", list(shape), dt))

    def sem(self, name):
        self.sems.append(self.ctx.enter_context(self.nc.semaphore(f"{self.stage}_{name}")))
        return self.sems[-1]

    def clear_semaphores(self):
        with self.nc.Block() as block:
            @block.gpsimd
            def _(pool):
                for sem in self.sems:
                    pool.sem_clear(sem)

    def count(self, name, per, credit=0):
        return Count(self.sem(name), per, credit)


def bcast(row, shape):
    return row.unsqueeze(2).to_broadcast(shape)


def load_bias_rows(sp, done, pairs):
    for dst, src in pairs:
        sp.dma_start(dst, src.partition_broadcast(P)).then_inc(done, 16)
    return 16 * len(pairs)


def normalise_input(nc, io, keep):
    with ExitStack() as ctx:
        s = Space(nc, ctx, "norm")
        stats = s.sb("stats", [P, TPG, 6])
        mv, mv4 = s.sb("mv", [P, NT, 2]), s.sb("mv4", [P, TPG, 2])
        ve = s.sb("ve", [P, NT])
        PARTS = 4
        tpp = NT // PARTS
        of = lambda i: slice(i * tpp, (i + 1) * tpp)
        x_loaded = [s.sem(f"x_loaded{i}") for i in range(PARTS)]
        consts_loaded = s.sem("consts_loaded")
        var_ready, rstd_ready = s.sem("var_ready"), s.sem("rstd_ready")
        XN = keep.XN
        parts = io["L0_attn_x"].rearrange("b (i n p) d -> (b i) p n d", p=P, n=tpp)
        with nc.Block() as block:
            @block.sync
            def _(sp):
                for i in range(PARTS):
                    sp.dma_start(XN[:, 1 + i * tpp:1 + (i + 1) * tpp, :], parts[i]).then_inc(x_loaded[i], 16)
                sp.dma_start(keep.ident[:], io["const_ident"]).then_inc(consts_loaded, 16)
                sp.dma_start(keep.identb[:], io["const_identb"]).then_inc(consts_loaded, 16)
                sp.dma_start(keep.going[:], io["const_going"]).then_inc(consts_loaded, 16)
                sp.dma_start(keep.w_router[:], io["w_router"]).then_inc(consts_loaded, 16)
                sp.wait_ge(consts_loaded, 64)

            @block.gpsimd
            def _(pool):
                pool.memset(keep.minus_half[:], -0.5)
                pool.memset(XN[:, 0, :], 0.0)
                pool.memset(XN[:, NT + 1:, :], 0.0)
                pool.memset(keep.rstd[:, NT:], 0.0)
                pool.drain()
                for i in range(PARTS):
                    pool.wait_ge(var_ready, i + 1)
                    pool.tensor_tensor(keep.rstd[:, of(i)], ve[:, of(i)], keep.minus_half[:, of(i)], ALU.pow)\
                        .then_inc(rstd_ready, 1)

            @block.vector
            def _(dve):
                for i in range(PARTS):
                    dve.wait_ge(x_loaded[i], 16)
                    with dve.Fori(i * NG // PARTS, (i + 1) * NG // PARTS) as g:
                        for n in range(TPG):
                            dve.bn_stats(stats[:, n, :], XN[:, g * TPG + (n + 1), :])
                        dve.drain()
                        for n in range(TPG):
                            dve.bn_aggr(mv4[:, n, :], stats[:, n, :])
                        dve.drain()
                        dve.tensor_copy(mv[:, bass.ds(g * TPG, TPG), :], mv4[:])
                        dve.drain()
                    dve.tensor_scalar(ve[:, of(i)], mv[:, of(i), 1], 1e-5, None, ALU.add).then_inc(var_ready, 1)
                for i in range(PARTS):
                    dve.wait_ge(rstd_ready, i + 1)
                    with dve.Fori(i * NG // PARTS, (i + 1) * NG // PARTS) as g:
                        for n in range(TPG):
                            t = g * TPG + n
                            dve.tensor_scalar(XN[:, g * TPG + (n + 1), :], XN[:, g * TPG + (n + 1), :],
                                              mv[:, t, 0:1], keep.rstd[:, bass.ds(g * TPG + n, 1)],
                                              ALU.subtract, ALU.mult)
        s.clear_semaphores()


class Keep:

    def __init__(self, nc, ctx):
        s = Space(nc, ctx, "keep")
        self.XN = s.sb("xn", [P, NT + 4, D])
        self.X2 = s.sb("x2", [P, NT + 1, D])
        self.ident = s.sb("ident", [P, P])
        self.identb = s.sb("identb", [P, P], BF16)
        self.going = s.sb("going", [P, NG + 1])
        self.minus_half = s.sb("minus_half", [P, NT])
        self.rstd = s.sb("rstd", [P, NT + 3])
        self.mean = s.sb("mean", [P, NT])
        self.w_router = s.sb("w_router", [P, KC, EXPERTS])
        self.logits = s.sb("logits", [P, NT + 1, EXPERTS])
        self.slot = s.sb("slot", [P, NT], U32)
        self.expert = s.sb("expert", [1, SLOT_TILES], U32)


HEADS, HD = 16, 16
LAT, LAT_HEADS = 64, 4
CHUNK = SEQ // LAT
LPT = P // CHUNK


def window_attention(nc, io, keep, layer, following=None):
    latents = layer == 0
    pre = "L0_attn_" if latents else "L1_attn_"
    HU = 2 if latents else 4
    KEYS = 2 * P if latents else P
    WU = HEADS // HU
    ST = WU + latents
    U = ST * TPG
    HALF = P // 2
    LEAD = 3
    none = (None, 0)
    if latents:
        plan = [(("QK", 1), none), (none, ("rem", -1)), (("V", 1), none), (("z", -1), none), (("R", 1), none),
                (none, none), (none, none), (("hT", 2), none), (none, ("out", -1))]
        ends_short = 1
        prologue = [("hT", 0), ("QK", 0), ("V", 0), ("R", 0), ("hT", 1)]
        epilogue = ["rem", "z", "out"]
    else:
        plan = [(none, none), (("hT", 2), ("out", -1)), (("QK", 2), none), (("V", 2), none)]
        ends_short = 0
        prologue = [("hT", 0), ("QK", 0), ("V", 0), ("hT", 1), ("QK", 1), ("V", 1)]
        epilogue = ["out"]
    by_act = ("hT", "rem", "z")
    order = [(name, n + ahead) for n in range(TPG) for pair in plan for name, ahead in pair if name]
    NACT = sum(name in by_act for name, _ in order)
    NDVE = len(order) - NACT
    acts_before = sum(name in by_act for name, _ in prologue)
    where = lambda m: 1 + m % TPG
    first_bank = lambda i: (i - len(prologue) - ends_short) % 2

    with ExitStack() as ctx:
        s = Space(nc, ctx, f"win{layer}")
        XN, X2 = keep.XN, keep.X2
        w_qkv = s.sb("w_qkv", [P, KC, 3 * D])
        w_out = s.sb("w_out", [P, KC, D])
        b_qk = s.sb("b_qk", [P, 2, KC])
        b_k = s.sb("b_k", [P, 2, KC])
        parity = s.sb("parity", [P, 2])
        b_v, b_out = s.sb("b_v", [P, D]), s.sb("b_out", [P, D])
        h = s.sb("h", [P, TPG, D])
        hT = s.sb("hT", [P, KC, P])
        QT = s.sb("QT", [P, 2, KC, P])
        KT = s.sb("KT", [P, 2, KC, (TPG + 1) * P])
        probs = s.sb("probs", [P, 4, BANK])
        probsT = s.sb("probsT", [P, 2, BANK])
        negmax = s.sb("negmax", [P, 4, 4])
        sums = s.sb("sums", [P, 2, HEADS + LAT_HEADS])
        oT = s.sb("oT", [P, KC, P])
        V = s.sb("V", [P, TPG + 1, 2, D])
        rsum = s.sb("rsum", [P, 4, 4])
        if latents:
            mask = s.sb("mask", [P, NG + 1, KEYS], BF16)
            w_rq = s.sb("w_rq", [P, KC, LAT_HEADS, 32])
            w_rk = s.sb("w_rk", [P, KC, LAT_HEADS, 32])
            w_rv = s.sb("w_rv", [P, KC, LAT])
            w_rout = s.sb("w_rout", [LAT, D])
            b_rq, b_rk = s.sb("b_rq", [P, 1]), s.sb("b_rk", [P, 1])
            b_rv, b_rout = s.sb("b_rv", [P, LAT]), s.sb("b_rout", [P, KC])
            gate_columns = s.sb("gate_columns", [P, 2])
            same_head = s.sb("same_head", [P, P])
            gate_local, gate_remote = s.sb("gate_local", [P, P]), s.sb("gate_remote", [P, P])
            pooledT = s.sb("pooledT", [P, KC, 2 * LAT])
            RQT = s.sb("RQT", [P, 2, P])
            RKT = s.sb("RKT", [P, 2, LAT_HEADS * LAT])
            RV = s.sb("RV", [P, 2, LAT])
            lat_mask = s.sb("lat_mask", [P, NT + 1, LAT], BF16)
            valid = s.sb("valid", [P, NG + 1, 2])
            localT, latT, remT = s.sb("localT", [P, KC, P]), s.sb("latT", [LAT, P]), s.sb("remT", [P, KC, P])
            apart = s.sb("apart", [P, KC, P])
            tanh_half, gate = s.sb("tanh_half", [P, KC, P]), s.sb("gate", [P, KC, P])
        else:
            mask = s.sb("mask", [P, KEYS], BF16)
            V_first = s.sb("V_first", [P, TPG + 1, 2, D])
            tmp = s.sb("tmp", [P, D])
            g1, b1 = s.sb("g1", [P, KC]), s.sb("b1", [P, KC])
            stats, mv, mv1 = s.sb("stats", [P, 6]), s.sb("mv", [P, NT + 1, 2]), s.sb("mv1", [P, 2])
            ve = s.sb("ve", [P, NT])

        score = [s.ps(f"score{i}") for i in range(4)]
        turned, po = s.ps("turned"), s.ps("po")
        lin_banks = [s.ps(f"lin{i}") for i in range(2)]

        loaded, zeroed, biases = s.sem("loaded"), s.sem("zeroed"), s.sem("biases")
        h_ready = s.count("h_ready", TPG, credit=3)
        lin_ready = s.count("lin_ready", len(order), credit=len(prologue))
        act_took = s.count("act_took", NACT, credit=acts_before)
        dve_took = s.count("dve_took", NDVE, credit=len(prologue) - acts_before + ends_short)
        scores_ready = s.count("scores_ready", U)
        max_ready = s.count("max_ready", U)
        exp_done = s.count("exp_done", U, credit=4)
        probs_ready = s.count("probs_ready", U)
        inverse_ready = s.count("inverse_ready", U)
        turned_ready = s.count("turned_ready", U, credit=4)
        probsT_ready = s.count("probsT_ready", U, credit=1)
        pv_done = s.count("pv_done", U, credit=2)
        attn_ready = s.count("attn_ready", TPG, credit=1)
        pooled_ready = s.count("pooled_ready", TPG)
        gate_ready = s.count("gate_ready", TPG, credit=1)
        mixed_ready = s.count("mixed_ready", TPG, credit=1)
        var_ready, rstd_done = s.sem("var_ready"), s.sem("rstd_done")
        rows_zeroed = s.sem("rows_zeroed")

        def taken(it, i):
            upto = [name in by_act for name, _ in order[:max(i + 1, 0)]]
            if order[i][0] in by_act:
                return act_took.sem, act_took.at(it, sum(upto))
            return dve_took.sem, dve_took.at(it, len(upto) - sum(upto))

        def heads_of(u):
            n, i = divmod(u, ST)
            if i == WU:
                return n, None
            return n, [2 * i, 2 * i + 1] if latents else [2 * i, 2 * i + 1, 8 + 2 * i, 8 + 2 * i + 1]

        def shape_of(u):
            return (LAT_HEADS, LAT) if heads_of(u)[1] is None else (HU, KEYS)

        with nc.Block() as block:
            @block.sync
            def _(sp):
                qkv = io[pre + ("qkv_w" if latents else "w_qkv")].rearrange("(c p) n -> p c n", p=P)
                bqkv = io[pre + ("qkv_b" if latents else "b_qkv")]
                pairs = [(w_qkv[:], qkv), (b_qk[:], io[f"win{layer}_b_qk"]), (parity[:], io["const_parity"]),
                         (w_out[:], io[pre + ("out_w" if latents else "w_out")].rearrange("(c p) n -> p c n", p=P)),
                         (mask[:], io["const_mask0" if latents else "const_mask1"])]
                if latents:
                    rkv = io[pre + "rkv_w"].rearrange("(c p) n -> p c n", p=P)
                    pairs += [(w_rq[:], io["win0_w_rq"]), (w_rk[:], io["win0_w_rk"]),
                              (b_rq[:], io["win0_b_rq"]), (b_rk[:], io["win0_b_rk"])]
                    pairs += [(w_rv[:], rkv[:, :, LAT:]), (w_rout[:], io[pre + "rout_w"]),
                              (b_rout[:], io["win0_b_rout"]), (gate_columns[:], io["win0_gate_columns"]),
                              (same_head[:], io["const_same_head"]),
                              (lat_mask[:], io["const_lat_mask"]), (valid[:], io["const_valid"])]
                else:
                    pairs += [(g1[:], io["win1_gain"]), (b1[:], io["win1_offset"])]
                n = 0
                for dst, src in pairs:
                    sp.dma_start(dst, src).then_inc(loaded, 16)
                    n += 16
                rows = [(b_v[:], bqkv[2 * D:3 * D]), (b_out[:], io[pre + ("out_b" if latents else "b_out")])]
                if latents:
                    rows.append((b_rv[:], io[pre + "rkv_b"][LAT:]))
                n += load_bias_rows(sp, loaded, rows)
                sp.wait_ge(loaded, n)
                sp.sem_inc(biases, 1)
                if following:
                    sp.wait_ge(loaded, n + following.load(sp, io, loaded, None))
                if latents:
                    sp.dma_start(io["rows_in"].rearrange("(t p) d -> p t d", p=P),
                                 XN[:, 0:1, :].to_broadcast([P, SLOT_TILES, D])).then_inc(rows_zeroed, 16)
                    sp.wait_ge(rows_zeroed, 16)

            @block.gpsimd
            def _(pool):
                pool.memset(KT[:, :, :, 0:P], 0.0)
                pool.memset(V[:], 0.0)
                pool.memset(probsT[:], 0.0)
                if latents:
                    pool.memset(pooledT[:], 0.0)
                    pool.memset(RKT[:], 0.0)
                    pool.memset(RV[:], 0.0)
                else:
                    pool.memset(V_first[:], 0.0)
                pool.drain()
                pool.sem_inc(zeroed, 1)

                def prepare(g, m):
                    if m > 2:
                        before = order.index(("hT", m - 2)) + 1 if m > 3 else 0
                        pool.wait_ge(lin_ready.sem, lin_ready.at(g, before))
                    if latents:
                        last = pool.tensor_copy(h[:, m % TPG, :], XN[:, g * TPG + (m + 1), :])
                    else:
                        last = pool.tensor_tensor(h[:, m % TPG, :], XN[:, g * TPG + (m + 1), :],
                                                  keep.rstd[:, bass.ds(g * TPG + m, 1)].to_broadcast([P, D]), ALU.mult)
                    last.then_inc(h_ready.sem, 1)

                def separate(it, n, rem_taken):
                    pool.wait_ge(*rem_taken)
                    pool.tensor_tensor(apart[:], localT[:], remT[:], ALU.subtract)

                def weigh_apart(it, n):
                    pool.drain()
                    pool.wait_ge(gate_ready.sem, gate_ready.at(it, n + 1))
                    pool.tensor_tensor(apart[:], apart[:], gate[:], ALU.mult)

                def mix():
                    pool.drain()
                    pool.tensor_tensor(oT[:], apart[:], remT[:], ALU.add).then_inc(mixed_ready.sem, 1)

                def divide(it, u):
                    pool.wait_ge(inverse_ready.sem, inverse_ready.at(it, u + 1))
                    heads, keys = shape_of(u)
                    mine = probs[:, u % 4, 0:heads * keys].rearrange("p (h k) -> p h k", h=heads)
                    pool.tensor_tensor(mine, mine, bcast(rsum[:, u % 4, 0:heads], [P, heads, keys]), ALU.mult)\
                        .then_inc(probs_ready.sem, 1)

                for m in range(3):
                    prepare(0, m)
                for u in range(LEAD - 1):
                    divide(0, u)
                with pool.Fori(0, NG) as g:
                    for u in range(U):
                        n, st = divmod(u, ST)
                        divide(g, u + LEAD - 1)
                        if st == 0:
                            prepare(g, n + 3)
                        if latents and st == 2:
                            separate(g, n - 1, taken(g, order.index(("rem", n - 1))))
                        if latents and st == 4:
                            weigh_apart(g, n - 1)
                        if latents and st == 5:
                            mix()
                if latents:
                    separate(NG - 1, TPG - 1, (act_took.sem, act_took.at(NG, 1)))
                    weigh_apart(NG - 1, TPG - 1)
                    mix()
                if not latents:
                    pool.wait_ge(var_ready, 1)
                    pool.tensor_tensor(keep.rstd[:, 0:NT], ve[:], keep.minus_half[:], ALU.pow).then_inc(rstd_done, 1)

            @block.tensor
            def _(pe):
                pe.sem_inc(turned_ready.sem, turned_ready.credit)
                pe.sem_inc(pv_done.sem, 1)
                pe.wait_ge(zeroed, 1)
                pe.wait_ge(biases, 1)
                pe.matmul(po[:], keep.ident[:], probsT[:, 1, :], start=True, stop=True)

                def linear_work(it, name, n, lin):
                    if name == "hT":
                        pe.wait_ge(h_ready.sem, h_ready.at(it, n - 2))
                        for c in range(KC):
                            last = pe.transpose(lin[:, c * P:(c + 1) * P], h[:, n % TPG, c * P:(c + 1) * P], keep.ident[:])
                    elif name == "QK":
                        for m in range(2 * KC):
                            for c in range(KC):
                                last = pe.matmul(lin[:, m * P:(m + 1) * P], w_qkv[:, c, m * P:(m + 1) * P], hT[:, c, :],
                                                 start=(c == 0), stop=(c == KC - 1))
                    elif name == "V":
                        for c in range(KC):
                            last = pe.matmul(lin[:, 0:D], hT[:, c, :], w_qkv[:, c, 2 * D:], start=(c == 0), stop=(c == KC - 1))
                        if latents:
                            for c in range(KC):
                                last = pe.matmul(lin[:, D:D + P], w_rq[:, c, :, :].rearrange("p h d -> p (h d)"),
                                                 hT[:, c, :], start=(c == 0), stop=(c == KC - 1))
                            for c in range(KC):
                                last = pe.matmul(lin[:, D + P:D + P + EXPERTS], hT[:, c, :], keep.w_router[:, c, :],
                                                 start=(c == 0), stop=(c == KC - 1))
                    elif name == "R":
                        pe.wait_ge(pooled_ready.sem, pooled_ready.at(it, n + 1))
                        for c in range(KC):
                            pe.matmul(lin[:, 0:LAT], w_rk[:, c, :, :].rearrange("p h d -> p (h d)"), pooledT[:, c, 0:LAT],
                                      start=(c == 0), stop=(c == KC - 1))
                        for c in range(KC):
                            last = pe.matmul(lin[:, LAT:2 * LAT], pooledT[:, c, :], w_rv[:, c, :],
                                             start=(c == 0), stop=(c == KC - 1))
                    elif name == "rem":
                        pe.wait_ge(attn_ready.sem, attn_ready.at(it, n + 1))
                        for c in range(KC):
                            last = pe.matmul(lin[:, c * P:(c + 1) * P], w_rout[:, c * P:(c + 1) * P], latT[:],
                                             start=True, stop=True)
                    elif name == "z":
                        pe.matmul(lin[:, 0:D], gate_local[:], localT[:].rearrange("p c n -> p (c n)"), start=True, stop=False)
                        last = pe.matmul(lin[:, 0:D], gate_remote[:], remT[:].rearrange("p c n -> p (c n)"),
                                         start=False, stop=True)
                    elif name == "out":
                        ready = mixed_ready if latents else attn_ready
                        pe.wait_ge(ready.sem, ready.at(it, n + 1))
                        for c in range(KC):
                            last = pe.matmul(lin[:, 0:D], oT[:, c, :], w_out[:, c, :], start=(c == 0), stop=(c == KC - 1))
                    last.then_inc(lin_ready.sem, 1)

                def linear_step(it, name, n):
                    if name:
                        i = order.index((name, n))
                        pe.wait_ge(*taken(it, i - 2))
                        linear_work(it, name, n, lin_banks[i % 2])

                def scores(it, g, u):
                    n, heads = heads_of(u)
                    bank = score[u % 4]
                    pe.wait_ge(exp_done.sem, exp_done.at(it, u - 3))
                    if u == 0:
                        pe.wait_ge(act_took.sem, acts_before)
                        pe.wait_ge(dve_took.sem, dve_took.credit)
                    elif u % ST == 0 and latents:
                        pe.wait_ge(*taken(it, order.index(("R", n))))
                    elif n > 1 and u % ST == 0:
                        pe.wait_ge(*taken(it, order.index(("QK", n))))
                    elif u % ST == 0:
                        pe.wait_ge(*taken(it, -2))
                    if heads is None:
                        pe.matmul(bank[:, 0:LAT_HEADS * LAT], keep.identb[:],
                                  lat_mask[:, bass.ds(g * TPG + n, 1), :].to_broadcast([P, LAT_HEADS, LAT]),
                                  start=True, stop=False)
                        last = pe.matmul(bank[:, 0:LAT_HEADS * LAT], RQT[:, n % 2, :], RKT[:, n % 2, :],
                                         start=False, stop=True)
                    else:
                        if latents:
                            m = mask[:, bass.ds(g + n // TPG, 1), :] if n % TPG == 0 else mask[:, 1:2, :]
                        else:
                            m = mask[:].unsqueeze(1)
                        pe.matmul(bank[:], keep.identb[:], m.to_broadcast([P, HU, KEYS]), start=True, stop=False)
                        cur = where(n) * P
                        old = cur - P
                        for i, head in enumerate(heads):
                            c, j, odd = head // 8, head % 8 // 2, head % 2
                            rows, a = slice(32 * j, 32 * j + 32), i * KEYS
                            q, k = QT[rows, n % 2, c, :], KT[rows, odd, c, :]
                            if latents:
                                last = pe.matmul(bank[:, a:a + KEYS], q, k[:, old:old + KEYS], start=False, stop=(i == HU - 1))
                            else:
                                pe.matmul(bank[:, a:a + HALF], q, k[:, cur:cur + HALF], start=False, stop=False)
                                pe.matmul(bank[0:HALF, a + HALF:a + P], q[:, 0:HALF], k[:, old + HALF:old + P],
                                          start=False, stop=(i == HU - 1))
                                last = pe.matmul(bank[HALF:P, a + HALF:a + P], q[:, HALF:P], k[:, cur + HALF:cur + P],
                                                 start=False, stop=(i == HU - 1))
                    last.then_inc(scores_ready.sem, 1)

                def turn(it, u):
                    n, heads = heads_of(u)
                    pe.wait_ge(probs_ready.sem, probs_ready.at(it, u + 1))
                    pe.wait_ge(probsT_ready.sem, probsT_ready.at(it, u))
                    for i in range(LAT_HEADS // 2 if heads is None else 4):
                        last = pe.transpose(turned[:, i * P:(i + 1) * P],
                                            probs[:, u % 4, i * P:(i + 1) * P], keep.ident[:])
                    last.then_inc(turned_ready.sem, 1)

                def weigh(it, u):
                    n, heads = heads_of(u)
                    pe.wait_ge(probsT_ready.sem, probsT_ready.at(it, u + 1))
                    if u % ST == 0:
                        pe.wait_ge(attn_ready.sem, attn_ready.at(it, n))
                    if heads is None:
                        for j in range(LAT_HEADS // 2):
                            rows = slice(2 * HD * j, 2 * HD * (j + 1))
                            last = pe.matmul(po[rows, D:D + P], RV[:, n % 2, rows], probsT[:, u % 2, j * P:(j + 1) * P],
                                             start=True, stop=True)
                    elif latents:
                        c, j = divmod(u % ST, 4)
                        for odd in range(2):
                            for own in range(2):
                                last = pe.matmul(po[32 * j:32 * j + 32, c * P:(c + 1) * P],
                                                 V[:, n % TPG + own, odd, c * P + 32 * j:c * P + 32 * j + 32],
                                                 probsT[:, u % 2, (2 * odd + own) * P:(2 * odd + own + 1) * P],
                                                 start=(odd + own == 0), stop=(odd + own == 2))
                    else:
                        rows = slice(32 * (u % ST), 32 * (u % ST) + 32)
                        for c in range(KC):
                            for half in range(2):
                                values = V if half else V_first
                                for odd in range(2):
                                    q = (2 * c + odd) * P + half * HALF
                                    last = pe.matmul(po[rows, c * P + half * HALF:c * P + (half + 1) * HALF],
                                                     values[:, where(n), odd, c * P + 32 * (u % ST):c * P + 32 * (u % ST) + 32],
                                                     probsT[:, u % 2, q:q + HALF], start=(odd == 0), stop=(odd == 1))
                    last.then_inc(pv_done.sem, 1)

                for i, (name, n) in enumerate(prologue):
                    acts = sum(x in by_act for x, _ in prologue[:i])
                    if i > 0:
                        pe.wait_ge(act_took.sem, acts)
                        if i > acts:
                            pe.wait_ge(dve_took.sem, ends_short + i - acts)
                    if name == "hT":
                        pe.wait_ge(h_ready.sem, n + 1)
                        for c in range(KC):
                            last = pe.transpose(lin_banks[first_bank(i)][:, c * P:(c + 1) * P], h[:, n, c * P:(c + 1) * P], keep.ident[:])
                        last.then_inc(lin_ready.sem, 1)
                    else:
                        linear_work(0, name, n, lin_banks[first_bank(i)])
                for u in range(LEAD):
                    scores(0, 0, u)
                with pe.Fori(0, NG) as g:
                    for u in range(U):
                        n, st = divmod(u, ST)
                        one, two = plan[st]
                        linear_step(g, one[0], n + one[1])
                        scores(g, g, u + LEAD)
                        linear_step(g, two[0], n + two[1])
                        turn(g, u)
                        weigh(g, u - 1)
                weigh(NG - 1, U - 1)
                pe.wait_ge(*taken(NG, -2))
                pe.wait_ge(*taken(NG, -1))
                for i, name in enumerate(epilogue):
                    acts = sum(x in by_act for x in epilogue[:i])
                    if i > 0:
                        pe.wait_ge(act_took.sem, act_took.at(NG, acts))
                        pe.wait_ge(dve_took.sem, dve_took.at(NG, i - acts))
                    linear_work(NG - 1, name, TPG - 1, lin_banks[i % 2])

            @block.scalar
            def _(act):
                act.sem_inc(exp_done.sem, exp_done.credit)
                act.wait_ge(biases, 1)

                def take(name, lin):
                    by_chunk = lambda c: lin[:, c * P:(c + 1) * P]
                    for c in range(KC):
                        if name == "hT" and latents:
                            last = act.activation(hT[:, c, :], by_chunk(c), ACT.Copy)
                        elif name == "hT":
                            last = act.activation(hT[:, c, :], by_chunk(c), ACT.Identity, bias=b1[:, c:c + 1], scale=g1[:, c:c + 1])
                        elif name == "rem":
                            last = act.activation(remT[:, c, :], by_chunk(c), ACT.Identity, bias=b_rout[:, c:c + 1])
                    if name == "z":
                        last = act.activation(tanh_half[:].rearrange("p c n -> p (c n)"), lin[:, 0:D], ACT.Tanh, scale=0.5)
                    last.then_inc(act_took.sem, 1)

                def linear_step(it, name, n):
                    if name in by_act:
                        i = order.index((name, n))
                        act.wait_ge(lin_ready.sem, lin_ready.at(it, i + 1))
                        take(name, lin_banks[i % 2])

                def softmax(it, u):
                    n, heads = heads_of(u)
                    act.wait_ge(max_ready.sem, max_ready.at(it, u + 1))
                    act.wait_ge(turned_ready.sem, turned_ready.at(it, u - 3))
                    width = LAT if heads is None else KEYS
                    cols = range(HEADS, HEADS + LAT_HEADS) if heads is None else heads
                    for i, col in enumerate(cols):
                        last = act.activation(probs[:, u % 4, i * width:(i + 1) * width],
                                              score[u % 4][:, i * width:(i + 1) * width], ACT.Exp,
                                              bias=negmax[:, u % 4, i:i + 1],
                                              accum_out=sums[:, n % 2, col:col + 1])
                    last.then_inc(exp_done.sem, 1)

                def take_output(it, n):
                    act.wait_ge(pv_done.sem, pv_done.at(it, (n + 1) * ST))
                    dst = localT if latents else oT
                    last = act.activation(dst[:].rearrange("p c n -> p (c n)"), po[:, 0:D], ACT.Copy)
                    if latents:
                        last = act.activation(latT[:], po[0:LAT, D:D + P], ACT.Copy)
                    last.then_inc(attn_ready.sem, 1)

                for i, (name, n) in enumerate(prologue):
                    if name in by_act:
                        act.wait_ge(lin_ready.sem, i + 1)
                        take(name, lin_banks[first_bank(i)])
                for u in range(LEAD):
                    softmax(0, u)
                with act.Fori(0, NG) as g:
                    for u in range(U):
                        n, st = divmod(u, ST)
                        one, two = plan[st]
                        linear_step(g, one[0], n + one[1])
                        softmax(g, u + LEAD)
                        linear_step(g, two[0], n + two[1])
                        if st == 0:
                            take_output(g, n - 1)
                take_output(NG - 1, TPG - 1)
                for i, name in enumerate(epilogue):
                    if name in by_act:
                        act.wait_ge(lin_ready.sem, lin_ready.at(NG, i + 1))
                        take(name, lin_banks[i % 2])

            @block.vector
            def _(dve):
                if ends_short:
                    dve.sem_inc(dve_took.sem, ends_short)
                dve.sem_inc(probsT_ready.sem, probsT_ready.credit)
                dve.memset(sums[:], 1.0)
                dve.wait_ge(biases, 1)
                dve.wait_ge(zeroed, 1)
                dve.tensor_scalar(b_qk[:, 0, :], b_qk[:, 0, :], HD ** -0.5, None, ALU.mult)
                if latents:
                    dve.tensor_scalar(gate_local[:], same_head[:], gate_columns[:, 0:1], None, ALU.mult)
                    dve.tensor_scalar(gate_remote[:], same_head[:], gate_columns[:, 1:2], None, ALU.mult)
                for odd in range(2):
                    dve.tensor_scalar(b_k[:, odd, :], b_qk[:, 1, :], parity[:, odd:odd + 1], None, ALU.mult)
                dve.drain()

                def take(g, name, n, lin):
                    if name == "QK":
                        by_chunk = lin[:].rearrange("p (w c n) -> p w c n", w=2, c=KC)
                        dve.scalar_tensor_tensor(QT[:, n % 2, :, :], by_chunk[:, 0], HD ** -0.5,
                                                 bcast(b_qk[:, 0, :], [P, KC, P]), ALU.mult, ALU.add)
                        for odd in range(2):
                            last = dve.scalar_tensor_tensor(KT[:, odd, :, where(n) * P:(where(n) + 1) * P], by_chunk[:, 1],
                                                            parity[:, odd:odd + 1], bcast(b_k[:, odd, :], [P, KC, P]),
                                                            ALU.mult, ALU.add)
                        if where(n) == TPG:
                            dve.drain()
                            last = dve.tensor_scalar(KT[:, :, :, 0:P], KT[:, :, :, TPG * P:],
                                                     keep.going[:, bass.ds(g + n // TPG + 1, 1)], None, ALU.mult)
                    elif name == "V" and latents:
                        for odd in range(2):
                            mine = lambda t: t.rearrange("p (h two d) -> p h two d", two=2, d=HD)[:, :, odd, :]
                            dve.tensor_tensor(mine(V[:, where(n), odd, :]), mine(lin[:, 0:D]), mine(b_v[:]), ALU.add)
                            if where(n) == TPG:
                                dve.tensor_tensor(mine(V[:, 0, odd, :]), mine(lin[:, 0:D]), mine(b_v[:]), ALU.add)
                        dve.tensor_scalar(RQT[:, n % 2, :], lin[:, D:D + P], b_rq[:, 0:1], HD ** -0.5, ALU.add, ALU.mult)
                        last = dve.tensor_copy(keep.logits[:, g * TPG + n, :], lin[:, D + P:D + P + EXPERTS])
                    elif name == "V":
                        for odd in range(2):
                            mine = lambda t: t.rearrange("p (h two d) -> p h two d", two=2, d=HD)[:, :, odd, :]
                            low, high = slice(0, HALF), slice(HALF, P)
                            dve.tensor_tensor(mine(V[:, where(n), odd, :]), mine(lin[:, 0:D]), mine(b_v[:]), ALU.add)
                            dve.tensor_tensor(mine(V_first[low, where(n), odd, :]), mine(lin[low, 0:D]), mine(b_v[low, :]), ALU.add)
                            last = dve.tensor_tensor(mine(V_first[high, where(n + 1), odd, :]), mine(lin[high, 0:D]),
                                                     mine(b_v[high, :]), ALU.add)
                        if where(n) == TPG:
                            dve.drain()
                            last = dve.tensor_scalar(V_first[high, where(n + 1), :, :], V_first[high, where(n + 1), :, :],
                                                     keep.going[high, bass.ds(g + n // TPG + 1, 1)], None, ALU.mult)
                    elif name == "R":
                        for j in range(LAT_HEADS):
                            quad = slice(32 * j, 32 * j + 32)
                            dve.tensor_scalar(RKT[quad, n % 2, j * LAT:(j + 1) * LAT], lin[quad, 0:LAT], 1.0 / CHUNK,
                                              b_rk[quad, 0:1], ALU.mult, ALU.add)
                        for odd in range(2):
                            rows = slice(odd * LAT, (odd + 1) * LAT)
                            pairs = lambda t: t.rearrange("p (j two d) -> p j two d", two=2, d=HD)[:, :, odd, :]
                            last = dve.scalar_tensor_tensor(pairs(RV[rows, n % 2, :]), pairs(lin[rows, LAT:2 * LAT]),
                                                            1.0 / CHUNK, pairs(b_rv[rows, :]), ALU.mult, ALU.add)
                    elif latents:
                        last = dve.tensor_tensor(X2[:, g * TPG + (n + 1), :], lin[:, 0:D], b_out[:], ALU.add)
                    else:
                        last = dve.tensor_tensor(tmp[:], lin[:, 0:D], b_out[:], ALU.add)
                    last.then_inc(dve_took.sem, 1)
                    if name == "out" and not latents:
                        dve.drain()
                        dve.tensor_tensor(X2[:, g * TPG + (n + 1), :], tmp[:], XN[:, g * TPG + (n + 1), :], ALU.add)
                        dve.drain()
                        dve.bn_stats(stats[:], X2[:, g * TPG + (n + 1), :])
                        dve.drain()
                        dve.bn_aggr(mv1[:], stats[:])
                        dve.drain()
                        dve.tensor_copy(mv[:, g * TPG + (n + 1), :], mv1[:])

                def linear_step(it, g, name, n):
                    if name and name not in by_act:
                        i = order.index((name, n))
                        dve.wait_ge(lin_ready.sem, lin_ready.at(it, i + 1))
                        take(g, name, n, lin_banks[i % 2])

                def pool_latents(first):
                    for c in range(KC):
                        for twice in range(2):
                            last = dve.tensor_reduce(pooledT[:, c, bass.ds(first + twice * LAT, LPT)],
                                                     hT[:, c, :].rearrange("p (l n) -> p l n", n=CHUNK), AX.X, ALU.add)
                    last.then_inc(pooled_ready.sem, 1)

                def maxima(it, u):
                    dve.wait_ge(scores_ready.sem, scores_ready.at(it, u + 1))
                    heads, keys = shape_of(u)
                    dve.tensor_reduce(negmax[:, u % 4, 0:heads],
                                      score[u % 4][:, 0:heads * keys].rearrange("p (h k) -> p h k", h=heads),
                                      AX.X, ALU.max, negate=True).then_inc(max_ready.sem, 1)

                def invert(it, g, u):
                    n, heads = heads_of(u)
                    dve.wait_ge(exp_done.sem, exp_done.at(it, u + 1))
                    inverse = rsum[:, u % 4, 0:shape_of(u)[0]]
                    if heads is None:
                        last = dve.reciprocal(inverse, sums[:, n % 2, HEADS:])
                    elif latents:
                        last = dve.reciprocal(inverse, sums[:, n % 2, heads[0]:heads[0] + HU])
                    else:
                        by_chunk = lambda t: t.rearrange("p (c h) -> p c h", c=KC)
                        last = dve.reciprocal(by_chunk(inverse), by_chunk(sums[:, n % 2, 0:HEADS])[:, :, heads[0]:heads[0] + 2])
                    if latents and n % TPG == 0:
                        dve.drain()
                        of = int(heads is None)
                        last = dve.tensor_scalar(inverse, inverse, valid[:, bass.ds(g + n // TPG, 1), of], None, ALU.mult)
                    last.then_inc(inverse_ready.sem, 1)

                def take_turned(it, u):
                    _, heads = heads_of(u)
                    dve.wait_ge(turned_ready.sem, turned_ready.at(it, u + 1))
                    dve.wait_ge(pv_done.sem, pv_done.at(it, u - 1))
                    k = LAT_HEADS // 2 * P if heads is None else BANK
                    dve.tensor_copy(probsT[:, u % 2, 0:k], turned[:, 0:k]).then_inc(probsT_ready.sem, 1)

                def gates(z_taken):
                    dve.wait_ge(*z_taken)
                    dve.tensor_scalar(gate[:], tanh_half[:], 0.5, 0.5, ALU.mult, ALU.add).then_inc(gate_ready.sem, 1)

                for i, (name, n) in enumerate(prologue):
                    if name == "R":
                        dve.wait_ge(act_took.sem, 1)
                        pool_latents(LAT - LPT)
                    if name not in by_act:
                        dve.wait_ge(lin_ready.sem, i + 1)
                        take(0, name, n, lin_banks[first_bank(i)])
                for u in range(LEAD):
                    maxima(0, u)
                for u in range(LEAD - 1):
                    invert(0, 0, u)

                def group(it, gi):
                    for u in range(U):
                        n, st = divmod(u, ST)
                        one, two = plan[st]
                        maxima(it, u + LEAD)
                        take_turned(it, u)
                        invert(it, it, u + LEAD - 1)
                        linear_step(it, it, one[0], n + one[1])
                        linear_step(it, it, two[0], n + two[1])
                        if latents and st == 1:
                            dve.wait_ge(*taken(it, order.index(("hT", n + 1)) if n else -2))
                            pool_latents(gi * (TPG * LPT) + n * LPT)
                        if latents and st == 4:
                            gates(taken(it, order.index(("z", n - 1))))

                if latents:
                    with dve.Fori(0, BATCH) as b:
                        with dve.Fori(0, GPB) as gi:
                            group(b * GPB + gi, gi)
                else:
                    with dve.Fori(0, NG) as g:
                        group(g, None)
                for i, name in enumerate(epilogue):
                    if name not in by_act:
                        dve.wait_ge(lin_ready.sem, lin_ready.at(NG, i + 1))
                        take(NG - 1, name, TPG - 1, lin_banks[i % 2])
                    if name == "z":
                        gates((act_took.sem, act_took.at(NG, 2)))
                if not latents:
                    dve.drain()
                    dve.tensor_copy(keep.mean[:], mv[:, 1:, 0])
                    dve.tensor_scalar(ve[:], mv[:, 1:, 1], 1e-5, None, ALU.add).then_inc(var_ready, 1)
                    dve.wait_ge(rstd_done, 1)
        s.clear_semaphores()


class ExpertWeights:

    def __init__(self, nc, ctx):
        s = Space(nc, ctx, "weights")
        self.w1 = s.sb("w1", [P, KC, EXPERTS * INNER])
        self.b1 = s.sb("b1", [P, EXPERTS * INNER])
        self.wo = s.sb("wo", [P, INNER // P, D])
        self.bo, self.gamma, self.beta = s.sb("bo", [P, D]), s.sb("gamma", [P, D]), s.sb("beta", [P, D])
        self.loaded = s.sem("loaded")
        self.clear_semaphores = s.clear_semaphores

    def load(self, sp, io):
        loads = [(self.w1[:, c, e * INNER:(e + 1) * INNER], io["L0_ffn_W1"][e, c * P:(c + 1) * P, :])
                 for e in range(EXPERTS) for c in range(KC)]
        loads += [(self.b1[:, e * INNER:(e + 1) * INNER], io["L0_ffn_b1"][e].partition_broadcast(P)) for e in range(EXPERTS)]
        loads.append((self.wo[:], io["L0_ffn_Wo"].rearrange("(c p) n -> p c n", p=P)))
        loads += [(dst[:], io["L0_ffn_" + name].partition_broadcast(P))
                  for dst, name in ((self.bo, "bo"), (self.gamma, "gamma"), (self.beta, "beta"))]
        for dst, src in loads:
            sp.dma_start(dst, src).then_inc(self.loaded, 16)
        self.all_loaded = 16 * len(loads)


def route(nc, io, keep, weights):
    with ExitStack() as ctx:
        s = Space(nc, ctx, "route")
        top, number = s.sb("top", [P, NT]), s.sb("number", [P, EXPERTS])
        chosen = s.sb("chosen", [P, NT])
        mask = s.sb("mask", [P, NT, EXPERTS])
        mask16 = s.sb("mask16", [P, NT, EXPERTS], BF16)
        before = s.sb("before", [P, 2, NT + 1, EXPERTS])
        before16 = s.sb("before16", [P, NT + 1, EXPERTS], BF16)
        earlier = s.sb("earlier", [P, P], BF16)
        ones16 = s.sb("ones16", [P, P], BF16)
        iota = s.sb("iota", [P, SLOT_TILES])
        counts = s.sb("counts", [P, EXPERTS])
        over = s.sb("over", [P, EXPERTS, NT])
        tiles, ends, first = s.sb("tiles", [P, EXPERTS]), s.sb("ends", [P, EXPERTS]), s.sb("first", [P, EXPERTS])
        ones = s.sb("ones", [P, EXPERTS])
        place = s.sb("place", [P, NT, EXPERTS])
        slotf = s.sb("slotf", [P, NT])
        past = s.sb("past", [P, SLOT_TILES, EXPERTS])
        expertf = s.sb("expertf", [P, SLOT_TILES])
        rank, total = s.ps("rank", [P, NT * EXPERTS]), s.ps("total", [P, EXPERTS])
        loaded, masks_ready, ranks_ready = s.sem("loaded"), s.sem("masks_ready"), s.sem("ranks_ready")
        slots_ready, scattered = s.sem("slots_ready"), s.sem("scattered")
        with nc.Block() as block:
            @block.sync
            def _(sp):
                sp.dma_start(earlier[:], io["const_earlier"]).then_inc(loaded, 16)
                sp.dma_start(iota[:], io["const_iota"]).then_inc(loaded, 16)
                weights.load(sp, io)

            @block.tensor
            def _(pe):
                pe.wait_ge(loaded, 32)
                pe.wait_ge(masks_ready, 1)
                pe.matmul(rank[:], earlier[:], mask16[:].rearrange("p t e -> p (t e)"), start=True, stop=False)
                pe.matmul(rank[:], ones16[:], before16[:, 0:NT, :].rearrange("p t e -> p (t e)"), start=False, stop=True)
                pe.matmul(total[:], ones16[:], before16[:, NT, :], start=True, stop=True).then_inc(ranks_ready, 1)

            @block.gpsimd
            def _(pool):
                pool.wait_ge(slots_ready, 1)
                for t in range(NT):
                    pool.indirect_dma_start(io["rows_in"], bass.IndirectOffsetOnAxis(ap=keep.slot[:, t:t + 1], axis=0),
                                            keep.XN[:, 1 + t, :], None).then_inc(scattered, 16)
                pool.wait_ge(scattered, 16 * NT)

            @block.vector
            def _(dve):
                dve.memset(ones16[:], 1.0)
                dve.memset(ones[:], 1.0)
                dve.memset(before[:, :, 0, :], 0.0)
                dve.wait_ge(loaded, 32)
                dve.tensor_reduce(top[:], keep.logits[:, 0:NT, :], AX.X, ALU.max)
                dve.tensor_scalar(number[:], iota[:, 0:EXPERTS], float(EXPERTS), None, ALU.subtract)
                dve.drain()
                dve.tensor_tensor(mask[:], keep.logits[:, 0:NT, :], bcast(top[:], [P, NT, EXPERTS]), ALU.is_equal)
                dve.drain()
                numbers = number[:].unsqueeze(1).to_broadcast([P, NT, EXPERTS])
                dve.tensor_tensor(mask[:], mask[:], numbers, ALU.mult)
                dve.drain()
                dve.tensor_reduce(chosen[:], mask[:], AX.X, ALU.min)
                dve.drain()
                dve.tensor_tensor(mask[:], bcast(chosen[:], [P, NT, EXPERTS]), numbers, ALU.is_equal)
                dve.drain()
                dve.tensor_copy(mask16[:], mask[:])
                dve.tensor_copy(before[:, 0, 1:, :], mask[:])
                dve.drain()
                steps = NT.bit_length() - 1
                for i in range(steps):
                    old, new = before[:, i % 2], before[:, (i + 1) % 2]
                    dve.tensor_copy(new[:, 1:1 + 2 ** i, :], old[:, 1:1 + 2 ** i, :])
                    dve.tensor_tensor(new[:, 1 + 2 ** i:, :], old[:, 1 + 2 ** i:, :], old[:, 1:NT + 1 - 2 ** i, :], ALU.add)
                    dve.drain()
                dve.tensor_copy(before16[:], before[:, steps % 2]).then_inc(masks_ready, 1)
                dve.wait_ge(ranks_ready, 1)
                dve.tensor_copy(counts[:], total[:])
                dve.drain()
                dve.tensor_scalar(slotf[:], iota[:, 0:NT], float(P), None, ALU.mult)
                dve.drain()
                dve.tensor_tensor(over[:], bcast(counts[:], [P, EXPERTS, NT]),
                                  slotf[:].unsqueeze(1).to_broadcast([P, EXPERTS, NT]), ALU.is_gt)
                dve.drain()
                dve.tensor_reduce(tiles[:], over[:], AX.X, ALU.add)
                dve.drain()
                dve.tensor_tensor_scan(ends[:], ones[:], tiles[:], 0.0, ALU.mult, ALU.add)
                dve.drain()
                dve.tensor_tensor(first[:], ends[:], tiles[:], ALU.subtract)
                dve.drain()
                dve.tensor_scalar(first[:], first[:], float(P), None, ALU.mult)
                dve.drain()
                dve.tensor_tensor(place[:], rank[:].rearrange("p (t e) -> p t e", e=EXPERTS),
                                  first[:].unsqueeze(1).to_broadcast([P, NT, EXPERTS]), ALU.add)
                dve.drain()
                dve.tensor_tensor(place[:], place[:], mask[:], ALU.mult)
                dve.drain()
                dve.tensor_reduce(slotf[:], place[:], AX.X, ALU.add)
                dve.drain()
                dve.tensor_copy(keep.slot[:], slotf[:])
                dve.tensor_tensor(past[:], bcast(iota[:], [P, SLOT_TILES, EXPERTS]),
                                  ends[:].unsqueeze(1).to_broadcast([P, SLOT_TILES, EXPERTS]), ALU.is_ge)
                dve.drain()
                dve.tensor_reduce(expertf[:], past[:], AX.X, ALU.add)
                dve.drain()
                dve.tensor_scalar(expertf[:], expertf[:], float(EXPERTS - 1), None, ALU.min)
                dve.drain()
                dve.tensor_copy(keep.expert[:], expertf[0:1, :])
                dve.drain()
                dve.sem_inc(slots_ready, 1)
        s.clear_semaphores()


def experts(nc, io, keep, weights):
    HB = INNER // BANK
    IC = INNER // P
    N = SLOT_TILES
    with ExitStack() as ctx:
        s = Space(nc, ctx, "experts")
        w1, b1, wo = weights.w1, weights.b1, weights.wo
        rows = s.sb("rows", [P, 2, D])
        rowsT = s.sb("rowsT", [P, KC, P])
        inner = s.sb("inner", [P, 1, INNER])
        innerT = s.sb("innerT", [P, IC, P])
        base = s.sb("base", [P, 2, D])
        z = s.sb("z", [P, D])
        y = s.sb("y", [P, 2, D])
        stats, mv, ve, rs = s.sb("stats", [P, 6]), s.sb("mv", [P, 2]), s.sb("ve", [P, 1]), s.sb("rs", [P, 1])
        turned = s.ps("turned")
        hidden = [[s.ps(f"hidden{i}{b}") for b in range(HB)] for i in range(2)]
        innerT_ps = [s.ps(f"innerT{b}") for b in range(HB)]
        out = s.ps("out")
        rows_loaded = [s.sem(f"rows_loaded{i}") for i in range(2)]
        stored = [s.sem(f"stored{i}") for i in range(2)]
        turned_ready, rowsT_ready = s.sem("turned_ready"), s.sem("rowsT_ready")
        hidden_ready, biased, gelu_done = s.sem("hidden_ready"), s.sem("biased"), s.sem("gelu_done")
        innerT_turned, innerT_ready = s.sem("innerT_turned"), s.sem("innerT_ready")
        out_ready, out_taken = s.sem("out_ready"), s.sem("out_taken")
        base_ready, var_ready, rstd_ready, y_ready = s.sem("base_ready"), s.sem("var_ready"), s.sem("rstd_ready"), s.sem("y_ready")
        rows_in = io["rows_in"].rearrange("(t p) d -> t p d", p=P)
        rows_out = io["rows_out"].rearrange("(t p) d -> t p d", p=P)
        with nc.Block() as block:
            @block.sync
            def _(sp):
                for i in range(2):
                    sp.dma_start(rows[:, i, :], rows_in[i]).then_inc(rows_loaded[i], 16)
                with sp.Fori(1, N // 2) as j2:
                    for i in range(2):
                        sp.wait_ge(turned_ready, j2 * 2 + (i - 1))
                        sp.wait_ge(base_ready, j2 * 2 + (i - 1))
                        sp.dma_start(rows[:, i, :], rows_in[j2 * 2 + i]).then_inc(rows_loaded[i], 16)

            @block.tensor
            def _(pe):
                def turn_rows(j, i, count):
                    pe.wait_ge(rows_loaded[i], 16 * count)
                    for c in range(KC):
                        last = pe.transpose(turned[:, c * P:(c + 1) * P], rows[:, i, c * P:(c + 1) * P], keep.ident[:])
                    last.then_inc(turned_ready, 1)

                def hide(j, i, later):
                    e = pe.value_load(keep.expert[0:1, bass.ds(j, 1)], min_val=0, max_val=EXPERTS - 1)
                    pe.wait_ge(rowsT_ready, j + 1)
                    if later:
                        pe.wait_ge(biased, (j - 1) * HB)
                    for b in range(HB):
                        for c in range(KC):
                            last = pe.matmul(hidden[i][b][:], rowsT[:, c, :],
                                             w1[:, c, bass.ds(e * INNER + b * BANK, BANK)],
                                             start=(c == 0), stop=(c == KC - 1))
                        last.then_inc(hidden_ready, 1)

                def project(j):
                    pe.wait_ge(gelu_done, j * HB + HB)
                    for b in range(HB):
                        for c in range(4):
                            a = b * BANK + c * P
                            last = pe.transpose(innerT_ps[b][:, c * P:(c + 1) * P], inner[:, 0, a:a + P], keep.ident[:])
                        last.then_inc(innerT_turned, 1)
                    for b in range(HB):
                        pe.wait_ge(innerT_ready, j * HB + (b + 1))
                        for c in range(4 * b, 4 * b + 4):
                            last = pe.matmul(out[:, 0:D], innerT[:, c, :], wo[:, c, :], start=(c == 0), stop=(c == IC - 1))
                    last.then_inc(out_ready, 1)

                pe.wait_ge(weights.loaded, weights.all_loaded)
                turn_rows(0, 0, 1)
                hide(0, 0, False)
                turn_rows(1, 1, 1)
                pe.wait_ge(out_taken, 1)
                hide(1, 1, False)
                pe.wait_ge(rowsT_ready, 2)
                turn_rows(2, 0, 2)
                project(0)
                with pe.Fori(1, N // 2 - 1) as j2:
                    for i in range(2):
                        j = j2 * 2 + i
                        hide(j, i, True)
                        turn_rows(j2 * 2 + (i + 1), 1 - i, j2 + (i + 1))
                        pe.wait_ge(out_taken, j2 * 2 + i)
                        project(j2 * 2 + (i - 1))
                hide(N - 2, 0, True)
                turn_rows(N - 1, 1, N // 2)
                pe.wait_ge(out_taken, N - 2)
                project(N - 3)
                hide(N - 1, 1, True)
                pe.wait_ge(out_taken, N - 1)
                project(N - 2)
                pe.wait_ge(out_taken, N)
                project(N - 1)

            @block.vector
            def _(dve):
                dve.wait_ge(weights.loaded, weights.all_loaded)
                def bias(j, i, first):
                    e = dve.value_load(keep.expert[0:1, bass.ds(j, 1)], min_val=0, max_val=EXPERTS - 1)
                    for b in range(HB):
                        dve.wait_ge(hidden_ready, j * HB + (b + 1))
                        if not first and b == 0:
                            dve.wait_ge(innerT_turned, j * HB)
                        dve.tensor_tensor(inner[:, 0, b * BANK:(b + 1) * BANK], hidden[i][b][:],
                                          b1[:, bass.ds(e * INNER + b * BANK, BANK)], ALU.add).then_inc(biased, 1)

                def take_inner(j, first):
                    for b in range(HB):
                        dve.wait_ge(innerT_turned, j * HB + (b + 1))
                        if not first and b == 0:
                            dve.wait_ge(out_ready, j)
                        dve.tensor_copy(innerT[:, 4 * b:4 * b + 4, :].rearrange("p c n -> p (c n)"), innerT_ps[b][:])\
                           .then_inc(innerT_ready, 1)

                def take_out(j, i, count):
                    dve.drain()
                    dve.wait_ge(out_ready, j + 1)
                    dve.wait_ge(base_ready, j + 1)
                    dve.tensor_tensor(z[:], out[:, 0:D], base[:, i, :], ALU.add).then_inc(out_taken, 1)
                    dve.drain()
                    dve.bn_stats(stats[:], z[:])
                    dve.drain()
                    dve.bn_aggr(mv[:], stats[:])
                    dve.drain()
                    dve.tensor_scalar(ve[:], mv[:, 1:2], 1e-12, None, ALU.add).then_inc(var_ready, 1)

                def normalise(j, i, count):
                    dve.wait_ge(rstd_ready, j + 1)
                    dve.tensor_scalar(z[:], z[:], mv[:, 0:1], rs[:], ALU.subtract, ALU.mult)
                    dve.drain()
                    dve.tensor_tensor(z[:], z[:], weights.gamma[:], ALU.mult)
                    dve.drain()
                    if count is not None:
                        dve.wait_ge(stored[i], 16 * count)
                    dve.tensor_tensor(y[:, i, :], z[:], weights.beta[:], ALU.add).then_inc(y_ready, 1)

                bias(0, 0, True)
                take_inner(0, True)
                for i in (1, 0):
                    j = 2 - i
                    bias(j, i, False)
                    take_out(j - 1, 1 - i, None)
                    take_inner(j, False)
                    normalise(j - 1, 1 - i, None)
                with dve.Fori(1, N // 2 - 1) as j2:
                    for i in (1, 0):
                        j = j2 * 2 + (2 - i)
                        bias(j, i, False)
                        take_out(j2 * 2 + (1 - i), 1 - i, j2)
                        take_inner(j, False)
                        normalise(j2 * 2 + (1 - i), 1 - i, j2)
                bias(N - 1, 1, False)
                take_out(N - 2, 0, None)
                take_inner(N - 1, False)
                normalise(N - 2, 0, N // 2 - 1)
                take_out(N - 1, 1, None)
                normalise(N - 1, 1, N // 2 - 1)

            @block.scalar
            def _(act):
                act.sem_inc(out_taken, 1)
                def take_rows(j):
                    act.wait_ge(turned_ready, j + 1)
                    act.activation(rowsT[:].rearrange("p c n -> p (c n)"), turned[:, 0:D], ACT.Copy).then_inc(rowsT_ready, 1)

                def gelu(j):
                    for b in range(HB):
                        act.wait_ge(biased, j * HB + (b + 1))
                        act.activation(inner[:, 0, b * BANK:(b + 1) * BANK], inner[:, 0, b * BANK:(b + 1) * BANK],
                                       ACT.Gelu).then_inc(gelu_done, 1)

                take_rows(0)
                take_rows(1)
                gelu(0)
                take_rows(2)
                gelu(1)
                take_rows(3)
                with act.Fori(1, N // 2 - 1) as j2:
                    for i in range(2):
                        gelu(j2 * 2 + i)
                        take_rows(j2 * 2 + (i + 2))
                for i in range(2):
                    gelu(N - 2 + i)

            @block.gpsimd
            def _(pool):
                pool.wait_ge(weights.loaded, weights.all_loaded)

                def add_bias(j, i, count, later):
                    pool.wait_ge(rows_loaded[i], 16 * count)
                    if later:
                        pool.wait_ge(out_taken, j)
                    pool.tensor_tensor(base[:, i, :], rows[:, i, :], weights.bo[:], ALU.add).then_inc(base_ready, 1)

                def rstd_and_store(j, i):
                    pool.wait_ge(var_ready, j + 1)
                    pool.tensor_tensor(rs[:], ve[:], keep.minus_half[:, 0:1], ALU.pow).then_inc(rstd_ready, 1)
                    pool.wait_ge(y_ready, j + 1)
                    pool.dma_start(rows_out[j], y[:, i, :]).then_inc(stored[i], 16)

                for i in range(2):
                    add_bias(i, i, 1, False)
                with pool.Fori(1, N // 2) as j2:
                    for i in range(2):
                        rstd_and_store(j2 * 2 + (i - 2), i)
                        add_bias(j2 * 2 + i, i, j2 + 1, True)
                for i in range(2):
                    rstd_and_store(N - 2 + i, i)
                for i in range(2):
                    pool.wait_ge(stored[i], 16 * N // 2)
        s.clear_semaphores()


def finish_layer0(nc, io, keep):
    ends = list(range(2, NG - 1, 2)) + [NG - 1, NG]
    runs = list(zip([0] + ends, ends))
    run_of = lambda g: next(i for i, end in enumerate(ends) if g < end)
    with ExitStack() as ctx:
        s = Space(nc, ctx, "fin0")
        XN, X2 = keep.XN, keep.X2
        got = s.sb("got", [P, NG, TPG, D])
        x1 = s.sb("x1", [P, NG, TPG, D])
        stats, mv = s.sb("stats", [P, TPG, 6]), s.sb("mv", [P, TPG, 2])
        var, ve, negmean = (s.sb(name, [P, NT]) for name in ("var", "ve", "negmean"))
        rs, shift = s.sb("rs", [P, NT]), s.sb("shift", [P, NT])
        x_loaded = [s.sem(f"x_loaded{pair}") for pair in range(NG // 2)]
        gathered = [s.sem(f"gathered{g}") for g in range(NG)]
        silu_ready, x1_ready, stored = s.sem("silu_ready"), s.sem("x1_ready"), s.sem("stored")
        var_ready, rstd_ready = s.sem("var_ready"), s.sem("rstd_ready")
        groups = io["L0_attn_x"].rearrange("b (g n p) d -> (b g) p n d", p=P, n=TPG)
        x1_groups = io["x1"].rearrange("(g n p) d -> g p n d", p=P, n=TPG)
        with nc.Block() as block:
            @block.sync
            def _(sp):
                for g in range(NG):
                    if g >= 2 and g % 2 == 0:
                        sp.wait_ge(gathered[g - 2], 16 * TPG)
                    sp.dma_start(x1[:, g, :, :], groups[g]).then_inc(x_loaded[g // 2], 16)
                with sp.Fori(0, NG) as g:
                    sp.wait_ge(x1_ready, g + 1)
                    sp.dma_start(x1_groups[g], x1[:, g, :, :]).then_inc(stored, 16)
                sp.wait_ge(stored, 16 * NG)

            @block.gpsimd
            def _(pool):
                def scales(run):
                    first, end = runs[run]
                    of = slice(first * TPG, end * TPG)
                    pool.wait_ge(var_ready, end)
                    pool.tensor_tensor(rs[:, of], ve[:, of], keep.minus_half[:, of], ALU.pow)
                    pool.drain()
                    pool.tensor_tensor(shift[:, of], negmean[:, of], rs[:, of], ALU.mult).then_inc(rstd_ready, 1)
                    pool.tensor_tensor(var[:, of], var[:, of], rs[:, of], ALU.mult)
                    pool.drain()
                    pool.tensor_tensor(var[:, of], var[:, of], rs[:, of], ALU.mult)

                for g in range(NG):
                    for n in range(TPG):
                        t = g * TPG + n
                        pool.indirect_dma_start(got[:, g, n, :], None, io["rows_out"],
                                                bass.IndirectOffsetOnAxis(ap=keep.slot[:, t:t + 1], axis=0))\
                            .then_inc(gathered[g], 16)
                    if g == NG - 3:
                        scales(0)
                for run in range(1, len(runs)):
                    scales(run)
                pool.drain()
                pool.tensor_scalar(var[:], var[:], 1e-5, None, ALU.add)
                pool.drain()
                pool.tensor_tensor(keep.rstd[:, 0:NT], var[:], keep.minus_half[:], ALU.pow)

            @block.scalar
            def _(act):
                def silu(g):
                    act.wait_ge(gathered[g], 16 * TPG)
                    act.activation(got[:, g, :, :], got[:, g, :, :], ACT.Silu).then_inc(silu_ready, 1)

                def normalise(g):
                    act.wait_ge(rstd_ready, run_of(g) + 1)
                    for n in range(TPG):
                        t = g * TPG + n
                        act.activation(XN[:, t + 1, :], x1[:, g, n, :], ACT.Identity, bias=shift[:, t:t + 1], scale=rs[:, t:t + 1])

                for g in range(NG):
                    silu(g)
                    if g >= 6:
                        normalise(g - 6)
                for g in range(NG - 6, NG):
                    normalise(g)

            @block.vector
            def _(dve):
                for pair in range(NG // 2):
                    dve.wait_ge(x_loaded[pair], 32)
                    with dve.Fori(pair * 2, pair * 2 + 2) as g:
                        tiles = bass.ds(g * TPG, TPG)
                        dve.wait_ge(silu_ready, g + 1)
                        gate = got[:, bass.ds(g, 1), :, :].rearrange("p o n d -> p (o n) d")
                        total = x1[:, bass.ds(g, 1), :, :].rearrange("p o n d -> p (o n) d")
                        dve.tensor_tensor(gate, gate, X2[:, bass.ds(g * TPG + 1, TPG), :], ALU.mult)
                        dve.drain()
                        dve.tensor_tensor(total, total, gate, ALU.add).then_inc(x1_ready, 1)
                        dve.drain()
                        for n in range(TPG):
                            dve.bn_stats(stats[:, n, :], x1[:, bass.ds(g, 1), n, :].rearrange("p o d -> p (o d)"))
                        dve.drain()
                        for n in range(TPG):
                            dve.bn_aggr(mv[:, n, :], stats[:, n, :])
                        dve.drain()
                        dve.tensor_copy(var[:, tiles], mv[:, :, 1])
                        dve.tensor_scalar(negmean[:, tiles], mv[:, :, 0], -1.0, None, ALU.mult)
                        dve.tensor_scalar(ve[:, tiles], mv[:, :, 1], 1e-5, None, ALU.add).then_inc(var_ready, 1)
        s.clear_semaphores()


GATED = int(D * 4 * 2 / 3)
REST = GATED % P


class FeedForwardWeights:

    def __init__(self, nc, ctx, gated):
        s = Space(nc, ctx, "ffn_weights" if gated else "mlp_weights")
        self.gated = gated
        self.hid = GATED if gated else 4 * D
        self.chunks = -(-self.hid // P)
        self.w1 = s.sb("w1", [P, KC, (1 + gated) * self.hid])
        if gated:
            self.w1_rest = s.sb("w1_rest", [P, KC, P])
        self.w2 = s.sb("w2", [P, self.chunks, D])
        self.b1 = s.sb("b1", [P, 1 + gated, self.chunks])
        self.b2 = s.sb("b2", [P, D])
        self.gain, self.offset = s.sb("gain", [P, KC]), s.sb("offset", [P, KC])

    def load(self, sp, io, done, layer):
        pre, mine = ("L1_ffn_", "ffn_") if self.gated else ("L1_attn_", "mlp_")
        at = (lambda a: a[layer]) if self.gated else (lambda a: a)
        whole = self.hid // P
        w1 = at(io[pre + "w1"]).rearrange("(c p) n -> p c n", p=P)
        loads = [(self.w1[:], w1),
                 (self.w2[:, 0:whole, :], at(io[pre + "w2"])[0:whole * P, :].rearrange("(c p) n -> p c n", p=P)),
                 (self.gain[:], at(io[mine + "gain"])), (self.offset[:], at(io[mine + "offset"])),
                 (self.b1[:], at(io[mine + "b1"])), (self.b2[:], at(io[pre + "b2"]).partition_broadcast(P))]
        if self.gated:
            loads += [(self.w2[0:REST, whole, :], at(io[pre + "w2"])[whole * P:, :]),
                      (self.w1_rest[:, :, 0:REST], w1[:, :, whole * P:self.hid]),
                      (self.w1_rest[:, :, P // 2:P // 2 + REST], w1[:, :, self.hid + whole * P:])]
        for dst, src in loads:
            sp.dma_start(dst, src).then_inc(done, 16)
        return 16 * len(loads)


RH, RD = 8, 64
RI = RH * RD


class RotaryWeights:

    def __init__(self, nc, ctx):
        s = Space(nc, ctx, "rot_weights")
        self.w_qkv = s.sb("w_qkv", [P, KC, 3 * RI])
        self.w_out = s.sb("w_out", [P, RI // P, D])
        self.scales = s.sb("scales", [P, 2, RD])
        self.ntab = SEQ // P + 2
        self.cos, self.sin = s.sb("cos", [P, 2, self.ntab, RD]), s.sb("sin", [P, 2, self.ntab, RD])
        self.mask = s.sb("mask", [P, NG + 1, 2 * P], BF16)

    def load(self, sp, io, done, layer):
        loads = [(self.w_qkv[:], io["L1_ffn_wqkv"][layer].rearrange("(c p) n -> p c n", p=P)),
                 (self.w_out[:], io["L1_ffn_wo"][layer].rearrange("(c p) n -> p c n", p=P)),
                 (self.cos[:], io["const_cos"]), (self.sin[:], io["const_sin"]), (self.mask[:], io["const_mask2"]),
                 (self.scales[:, 0, :], io["L1_ffn_q_scale"][layer].partition_broadcast(P)),
                 (self.scales[:, 1, :], io["L1_ffn_k_scale"][layer].partition_broadcast(P))]
        for dst, src in loads:
            sp.dma_start(dst, src).then_inc(done, 16)
        return 16 * len(loads)

    def scale(self, pool):
        half = RD // 2
        for i in range(2):
            sc = lambda a, b: self.scales[:, i:i + 1, a:b].to_broadcast([P, self.ntab, b - a])
            pool.tensor_tensor(self.cos[:, i, :, :], self.cos[:, i, :, :], sc(0, RD), ALU.mult)
            pool.tensor_tensor(self.sin[:, i, :, 0:half], self.sin[:, i, :, 0:half], sc(half, RD), ALU.mult)
            pool.tensor_tensor(self.sin[:, i, :, half:], self.sin[:, i, :, half:], sc(0, half), ALU.mult)


def feed_forward(nc, io, keep, weights, rotary, next_layer):
    gated = weights.gated
    HID, IC = weights.hid, weights.chunks
    rows = [min(P, HID - m * P) for m in range(IC)]
    TOK = TPG * P
    RING = 2 if gated else 4
    with ExitStack() as ctx:
        s = Space(nc, ctx, "ffn" if gated else "mlp")
        XN, X2 = keep.XN, keep.X2
        w1, w2, b1, b2, gain, offset = weights.w1, weights.w2, weights.b1, weights.b2, weights.gain, weights.offset
        h = s.sb("h", [P, TPG, D])
        hT = s.sb("hT", [P, KC, TOK])
        inner = s.sb("inner", [P, IC, TOK])
        gel = s.sb("gel", [P, 2, TOK])
        result = s.sb("result", [P, TPG, D])
        stats, mv = s.sb("stats", [P, TPG, 6]), s.sb("mv", [P, TPG, 2])
        ve, rs = s.sb("ve", [P, TPG]), s.sb("rs", [P, TPG])
        turned = [s.ps(f"turned{c}") for c in range(KC)]
        hidden = [[s.ps(f"hidden{i}{k}") for k in range(1 + gated)] for i in range(RING)]
        out = [s.ps(f"out{i}") for i in range(2)]
        next_loaded, h_loaded = s.sem("next_loaded"), s.sem("h_loaded")
        var_ready, rstd_ready = s.sem("var_ready"), s.sem("rstd_ready")
        h_ready = s.count("h_ready", 1)
        turned_ready, hT_ready = s.count("turned_ready", KC), s.count("hT_ready", KC)
        hidden_ready, gel_ready = s.count("hidden_ready", IC), s.count("gel_ready", IC)
        inner_ready = s.count("inner_ready", IC, credit=RING)
        out_ready, out_taken = s.count("out_ready", TPG), s.count("out_taken", TPG, credit=2)
        stored = s.sem("stored")
        result_ready = s.sem("result_ready")
        with nc.Block() as block:
            @block.sync
            def _(sp):
                def load_h(g):
                    half = D // 2
                    sp.dma_start(h[:, :, 0:half], X2[:, bass.ds(g * TPG + 1, TPG), 0:half]).then_inc(h_loaded, 16)
                    sp.dma_start(h[1:P, :, half:], X2[0:P - 1, bass.ds(g * TPG + 1, TPG), half:]).then_inc(h_loaded, 16)
                    sp.dma_start(h[0:1, :, half:], X2[P - 1:P, bass.ds(g * TPG, TPG), half:]).then_inc(h_loaded, 16)

                if gated:
                    load_h(0)
                rotary_loads = rotary.load(sp, io, next_loaded, next_layer)
                if gated:
                    with sp.Fori(1, NG) as g:
                        sp.wait_ge(turned_ready.sem, turned_ready.at(g, 0))
                        load_h(g)
                else:
                    groups = io["s1"].rearrange("(g n p) d -> g p n d", p=P, n=TPG)
                    with sp.Fori(0, NG) as g:
                        sp.wait_ge(result_ready, g + 1)
                        sp.dma_start(groups[g], result[:]).then_inc(stored, 16)
                    sp.wait_ge(stored, 16 * NG + 16)

                sp.wait_ge(next_loaded, rotary_loads)

            @block.gpsimd
            def _(pool):
                if gated:
                    with pool.Fori(0, NG) as g:
                        pool.wait_ge(var_ready, g + 1)
                        pool.tensor_tensor(rs[:], ve[:], keep.minus_half[:, 0:TPG], ALU.pow).then_inc(rstd_ready, 1)
                pool.wait_ge(next_loaded, 16 * 7)
                rotary.scale(pool)

            @block.tensor
            def _(pe):

                def turn(g):
                    pe.wait_ge(h_ready.sem, h_ready.at(g, 1))
                    for c in range(KC):
                        for n in range(TPG):
                            last = pe.transpose(turned[c][:, n * P:(n + 1) * P], h[:, n, c * P:(c + 1) * P], keep.ident[:])
                        last.then_inc(turned_ready.sem, 1)

                def hide(g):
                    pe.wait_ge(hT_ready.sem, hT_ready.at(g, KC))
                    for m in range(IC):
                        pe.wait_ge(inner_ready.sem, inner_ready.at(g, m + 1 - RING))
                        if rows[m] < P:
                            for c in range(KC):
                                last = pe.matmul(hidden[m % RING][0][:], weights.w1_rest[:, c, :], hT[:, c, :],
                                                 start=(c == 0), stop=(c == KC - 1))
                        else:
                            for k in range(1 + gated):
                                for c in range(KC):
                                    a = k * HID + m * P
                                    last = pe.matmul(hidden[m % RING][k][:], w1[:, c, a:a + P], hT[:, c, :],
                                                     start=(c == 0), stop=(c == KC - 1))
                        last.then_inc(hidden_ready.sem, 1)

                def project(g, tiles):
                    for n in tiles:
                        pe.wait_ge(out_taken.sem, out_taken.at(g, n - 1))
                        for m in range(IC):
                            if n == 0:
                                pe.wait_ge(inner_ready.sem, inner_ready.at(g, m + 1))
                            last = pe.matmul(out[n % 2][:, 0:D],
                                             inner[0:rows[m], m, n * P:(n + 1) * P], w2[0:rows[m], m, :],
                                             start=(m == 0), stop=(m == IC - 1))
                        last.then_inc(out_ready.sem, 1)

                turn(0)
                with pe.Fori(0, NG - 1) as g:
                    hide(g)
                    project(g, range(0, 2))
                    turn(g + 1)
                    project(g, range(2, TPG))
                hide(NG - 1)
                project(NG - 1, range(TPG))

            @block.scalar
            def _(act):
                if not gated:
                    act.sem_inc(inner_ready.sem, RING)

                def take_turned(g):
                    for c in range(KC):
                        act.wait_ge(turned_ready.sem, turned_ready.at(g, c + 1))
                        act.activation(hT[:, c, :], turned[c][:], ACT.Identity, bias=offset[:, c:c + 1],
                                       scale=gain[:, c:c + 1]).then_inc(hT_ready.sem, 1)

                def gelus(g):
                    for m in range(IC):
                        act.wait_ge(hidden_ready.sem, hidden_ready.at(g, m + 1))
                        if gated:
                            act.wait_ge(inner_ready.sem, inner_ready.at(g, m + 1 - RING))
                            src, at = (hidden[m % RING][1], 0) if rows[m] == P else (hidden[m % RING][0], P // 2)
                            act.activation(gel[0:rows[m], m % 2, :], src[at:at + rows[m], :], ACT.Gelu,
                                           bias=b1[at:at + rows[m], 1, m:m + 1]).then_inc(gel_ready.sem, 1)
                        else:
                            act.activation(inner[:, m, :], hidden[m % RING][0][:], ACT.Gelu,
                                           bias=b1[:, 0, m:m + 1]).then_inc(inner_ready.sem, 1)

                take_turned(0)
                with act.Fori(0, NG - 1) as g:
                    gelus(g)
                    take_turned(g + 1)
                gelus(NG - 1)

            @block.vector
            def _(dve):
                dve.sem_inc(out_taken.sem, out_taken.credit)
                if gated:
                    dve.sem_inc(inner_ready.sem, RING)
                else:
                    dve.sem_inc(stored, 16)

                def make_h(g, first):
                    if gated:
                        dve.wait_ge(h_loaded, g * 48 + 48)
                        dve.tensor_scalar(h[0:1, 0, D // 2:], h[0:1, 0, D // 2:], keep.going[0:1, bass.ds(g, 1)], None, ALU.mult)
                        dve.drain()
                        for n in range(TPG):
                            dve.bn_stats(stats[:, n, :], h[:, n, :])
                        dve.drain()
                        for n in range(TPG):
                            dve.bn_aggr(mv[:, n, :], stats[:, n, :])
                        dve.drain()
                        dve.tensor_scalar(ve[:], mv[:, :, 1], 1e-5, None, ALU.add).then_inc(var_ready, 1)
                        dve.wait_ge(rstd_ready, g + 1)
                        for n in range(TPG):
                            dve.tensor_scalar(h[:, n, :], h[:, n, :], mv[:, n, 0:1], rs[:, n:n + 1], ALU.subtract, ALU.mult)
                    else:
                        if not first:
                            dve.wait_ge(turned_ready.sem, turned_ready.at(g, 0))
                        for n in range(TPG):
                            t = g * TPG + n
                            dve.tensor_scalar(h[:, n, :], X2[:, g * TPG + (n + 1), :], keep.mean[:, bass.ds(t, 1)],
                                              keep.rstd[:, bass.ds(t, 1)], ALU.subtract, ALU.mult)
                    dve.drain()
                    dve.sem_inc(h_ready.sem, 1)

                def multiply(g):
                    for m in range(IC):
                        dve.wait_ge(gel_ready.sem, gel_ready.at(g, m + 1))
                        dve.scalar_tensor_tensor(inner[0:rows[m], m, :], hidden[m % RING][0][0:rows[m], :],
                                                 b1[0:rows[m], 0, m:m + 1], gel[0:rows[m], m % 2, :],
                                                 ALU.add, ALU.mult).then_inc(inner_ready.sem, 1)

                def take_out(g):
                    if not gated:
                        dve.wait_ge(stored, g * 16 + 16)
                    for n in range(TPG):
                        dve.wait_ge(out_ready.sem, out_ready.at(g, n + 1))
                        dve.tensor_tensor(result[:, n, :], out[n % 2][:, 0:D], b2[:], ALU.add)\
                           .then_inc(out_taken.sem, 1)
                    dve.drain()
                    slots = bass.ds(g * TPG + 1, TPG)
                    if gated:
                        dve.tensor_tensor(XN[:, slots, :], result[:], X2[:, slots, :], ALU.add)
                        dve.drain()
                    else:
                        dve.tensor_tensor(result[:], result[:], X2[:, slots, :], ALU.add).then_inc(result_ready, 1)

                make_h(0, True)
                with dve.Fori(0, NG - 1) as g:
                    make_h(g + 1, False)
                    if gated:
                        multiply(g)
                    take_out(g)
                if gated:
                    multiply(NG - 1)
                take_out(NG - 1)
        s.clear_semaphores()


def rotary_attention(nc, io, keep, weights, following, layer):
    ST = RH // 2
    U = ST * TPG
    prologue = [("hT", 0), ("q", 0), ("k", 0), ("v", 0), ("hT", 1), ("q", 1), ("k", 1), ("v", 1), ("QT", 0), ("KT", 0),
                ("hT", 2)]
    plan = [(("q", 2), ("k", 2)), (("QT", 1), ("KT", 1)), (("v", 2), ("oT", -1)), (("hT", 3), ("out", -1))]
    order = [(name, n + ahead) for n in range(TPG) for pair in plan for name, ahead in pair]
    NACT = len(order) - TPG
    where = lambda m: 1 + m % TPG

    with ExitStack() as ctx:
        s = Space(nc, ctx, "rot")
        XN, X2 = keep.XN, keep.X2
        w_qkv, w_out, cos, sin, mask = weights.w_qkv, weights.w_out, weights.cos, weights.sin, weights.mask
        h = s.sb("h", [P, TPG, D])
        hT = s.sb("hT", [P, KC, P])
        qk = s.sb("qk", [P, 2, 2, RI])
        square, turn_a = s.sb("square", [P, 2, RI]), s.sb("turn_a", [P, 2, RI])
        rot = s.sb("rot", [P, 2, RI])
        ss, rnorm = s.sb("ss", [P, 2 * RH]), s.sb("rnorm", [P, 2 * RH])
        QT = s.sb("QT", [P, 2, 4, P])
        KT = s.sb("KT", [P, 4, (TPG + 1) * P])
        V = s.sb("V", [P, TPG + 1, RI])
        probs, probsT = s.sb("probs", [P, 4, BANK]), s.sb("probsT", [P, 2, BANK])
        mask_now = s.sb("mask_now", [P, 2, 2 * P])
        negmax = s.sb("negmax", [P, 4, 2])
        sums, rsum = s.sb("sums", [P, 2, RH]), s.sb("rsum", [P, RH])
        attn, oT = s.sb("attn", [P, RI]), s.sb("oT", [P, RI // P, P])
        score = [s.ps(f"score{i}") for i in range(4)]
        turned, po = s.ps("turned"), s.ps("po")
        lin = [s.ps(f"lin{i}") for i in range(2)]

        next_loaded, zeroed, masking = s.sem("next_loaded"), s.sem("zeroed"), s.sem("masking")
        front_loaded, back_loaded = s.sem("front_loaded"), s.sem("back_loaded")
        h_ready = s.count("h_ready", 1)
        lin_ready = s.count("lin_ready", len(order), credit=len(prologue))
        act_took = s.count("act_took", NACT, credit=len(prologue))
        dve_took = s.count("dve_took", TPG, credit=1)
        scores_ready = s.count("scores_ready", U)
        max_ready = s.count("max_ready", U, credit=4)
        probs_ready = s.count("probs_ready", U)
        turned_ready = s.count("turned_ready", U, credit=4)
        probsT_ready = s.count("probsT_ready", U, credit=1)
        pv_done = s.count("pv_done", U, credit=2)
        attn_ready = s.count("attn_ready", TPG, credit=1)
        squared, ss_ready, rn_ready = s.count("squared", TPG), s.count("ss_ready", TPG), s.count("rn_ready", TPG)
        normed, turned_a, rot_ready = s.count("normed", TPG), s.count("turned_a", TPG), s.count("rot_ready", TPG)

        def taken(it, i):
            if order[i][0] == "out":
                return dve_took.sem, dve_took.at(it, sum(name == "out" for name, _ in order[:max(i + 1, 0)]))
            return act_took.sem, act_took.at(it, sum(name != "out" for name, _ in order[:max(i + 1, 0)]))

        def heads_of(u):
            n, i = divmod(u, ST)
            return n, [4 * (i // 2) + i % 2, 4 * (i // 2) + i % 2 + 2]

        with nc.Block() as block:
            @block.sync
            def _(sp):
                def load_h(g, first, done):
                    half = D // 2
                    two, at = slice(first, first + 2), g * TPG + first
                    sp.dma_start(h[:, two, 0:half], XN[:, bass.ds(at + 1, 2), 0:half]).then_inc(done, 16)
                    sp.dma_start(h[1:P, two, half:], XN[0:P - 1, bass.ds(at + 1, 2), half:]).then_inc(done, 16)
                    sp.dma_start(h[0:1, two, half:], XN[P - 1:P, bass.ds(at, 2), half:]).then_inc(done, 16)

                load_h(0, 0, front_loaded)
                load_h(0, 2, back_loaded)
                following_loads = following.load(sp, io, next_loaded, layer)
                sp.wait_ge(lin_ready.sem, prologue.index(("hT", 1)) + 1)
                load_h(1, 0, front_loaded)

                def after(g, back, front):
                    sp.wait_ge(lin_ready.sem, lin_ready.at(g, order.index(("hT", 3)) + 1))
                    load_h(back, 2, back_loaded)
                    if front is not None:
                        sp.wait_ge(lin_ready.sem, lin_ready.at(g, order.index(("hT", 5)) + 1))
                        load_h(front, 0, front_loaded)

                with sp.Fori(0, NG - 2) as g:
                    after(g, g + 1, g + 2)
                after(NG - 2, NG - 1, 0)
                after(NG - 1, 0, None)
                sp.wait_ge(back_loaded, 48 * (NG + 1))
                sp.wait_ge(next_loaded, following_loads)

            @block.gpsimd
            def _(pool):
                pool.memset(KT[:, :, 0:P], 0.0)
                pool.memset(V[:], 0.0)
                pool.memset(following.w1_rest[:, :, REST:P // 2], 0.0)
                pool.memset(following.w1_rest[:, :, P // 2 + REST:], 0.0)
                pool.memset(probsT[:], 0.0)
                pool.drain()
                pool.sem_inc(zeroed, 1)
                by_head = lambda t, i: t[:, i, :].rearrange("p (h d) -> p h d", d=RD)

                def square_up(it, m):
                    if m < 2:
                        pool.wait_ge(act_took.sem, prologue.index(("k", m)) + 1)
                    else:
                        pool.wait_ge(*taken(it, order.index(("k", m))))
                    pool.tensor_tensor(square[:], qk[:, m % 2, :, :], qk[:, m % 2, :, :], ALU.mult).then_inc(squared.sem, 1)
                    pool.wait_ge(ss_ready.sem, ss_ready.at(it, m + 1))
                    pool.tensor_tensor(rnorm[:], ss[:], keep.minus_half[:, 0:2 * RH], ALU.pow).then_inc(rn_ready.sem, 1)

                def times_cos(it, gi, m):
                    pool.wait_ge(normed.sem, normed.at(it, m + 1))
                    for i in range(2):
                        last = pool.tensor_tensor(by_head(turn_a, i), by_head(qk[:, m % 2], i),
                                                  cos[:, i, bass.ds(gi * TPG + m, 1), :].to_broadcast([P, RH, RD]),
                                                  ALU.mult)
                    last.then_inc(turned_a.sem, 1)

                for m in range(2):
                    square_up(0, m)
                    times_cos(0, 0, m)
                with pool.Fori(0, BATCH) as b:
                    with pool.Fori(0, GPB) as gi:
                        for n in range(TPG):
                            square_up(b * GPB + gi, n + 2)
                            times_cos(b * GPB + gi, gi, n + 2)

            @block.tensor
            def _(pe):
                pe.sem_inc(turned_ready.sem, turned_ready.credit)
                pe.sem_inc(pv_done.sem, 1)
                pe.wait_ge(zeroed, 1)
                pe.matmul(po[:], keep.ident[:], V[:, 0, :], start=True, stop=True)

                def linear_work(it, name, m, lin):
                    if name == "hT":
                        for c in range(KC):
                            last = pe.transpose(lin[:, c * P:(c + 1) * P], h[:, m % TPG, c * P:(c + 1) * P], keep.ident[:])
                    elif name in ("q", "k", "v"):
                        a = "qkv".index(name) * RI
                        for c in range(KC):
                            last = pe.matmul(lin[:], hT[:, c, :], w_qkv[:, c, a:a + RI], start=(c == 0), stop=(c == KC - 1))
                    elif name in ("QT", "KT"):
                        pe.wait_ge(rot_ready.sem, rot_ready.at(it, m + 1))
                        for c in range(4):
                            last = pe.transpose(lin[:, c * P:(c + 1) * P], rot[:, "QK".index(name[0]), c * P:(c + 1) * P],
                                                keep.ident[:])
                    elif name == "oT":
                        pe.wait_ge(attn_ready.sem, attn_ready.at(it, m + 1))
                        for c in range(RI // P):
                            last = pe.transpose(lin[:, c * P:(c + 1) * P], attn[:, c * P:(c + 1) * P], keep.ident[:])
                    else:
                        for c in range(RI // P):
                            last = pe.matmul(lin[:, 0:D], oT[:, c, :], w_out[:, c, :], start=(c == 0), stop=(c == RI // P - 1))
                    last.then_inc(lin_ready.sem, 1)

                def linear_step(it, name, m):
                    i = order.index((name, m))
                    pe.wait_ge(*taken(it, i - 2))
                    if name == "hT" and m == TPG:
                        pe.wait_ge(h_ready.sem, h_ready.at(it, 2))
                    if name == "hT" and m == TPG + 2:
                        pe.wait_ge(back_loaded, it * 48 + 96)
                    linear_work(it, name, m, lin[i % 2])

                def scores(it, u):
                    n, heads = heads_of(u)
                    bank = score[u % 4]
                    pe.wait_ge(max_ready.sem, max_ready.at(it, u - 3))
                    if u == 0:
                        pe.wait_ge(act_took.sem, prologue.index(("KT", 0)) + 1)
                    elif u % ST == 0:
                        i = order.index(("KT", n))
                        pe.wait_ge(*taken(it, i))
                    for j in range(2):
                        c, half = divmod(heads[j], 2)
                        rows = slice(RD * half, RD * (half + 1))
                        first = n % TPG * P
                        last = pe.matmul(bank[:, j * 2 * P:(j + 1) * 2 * P], QT[rows, n % 2, c, :],
                                         KT[rows, c, first:first + 2 * P], start=True, stop=True)
                    last.then_inc(scores_ready.sem, 1)

                def turn(it, u):
                    pe.wait_ge(probs_ready.sem, probs_ready.at(it, u + 1))
                    pe.wait_ge(probsT_ready.sem, probsT_ready.at(it, u))
                    for i in range(4):
                        last = pe.transpose(turned[:, i * P:(i + 1) * P], probs[:, u % 4, i * P:(i + 1) * P], keep.ident[:])
                    last.then_inc(turned_ready.sem, 1)

                def weigh(it, u):
                    n, heads = heads_of(u)
                    pe.wait_ge(probsT_ready.sem, probsT_ready.at(it, u + 1))
                    if u % ST == 0:
                        pe.wait_ge(attn_ready.sem, attn_ready.at(it, n))
                    for j in range(2):
                        a = heads[j] * RD
                        for kb in range(2):
                            last = pe.matmul(po[:, a:a + RD], probsT[:, u % 2, (2 * j + kb) * P:(2 * j + kb + 1) * P],
                                             V[:, n % TPG + kb, a:a + RD], start=(kb == 0), stop=(kb == 1))
                    last.then_inc(pv_done.sem, 1)

                for i, (name, m) in enumerate(prologue):
                    if i > 0:
                        pe.wait_ge(act_took.sem, i)
                    if (name, m) == ("hT", 0):
                        pe.wait_ge(h_ready.sem, 1)
                    if (name, m) == ("hT", 2):
                        pe.wait_ge(back_loaded, 48)
                    linear_work(0, name, m, lin[i % 2])
                scores(0, 0)
                scores(0, 1)
                with pe.Fori(0, NG) as g:
                    for u in range(U):
                        n, st = divmod(u, ST)
                        one, two = plan[st]
                        linear_step(g, one[0], n + one[1])
                        scores(g, u + 2)
                        linear_step(g, two[0], n + two[1])
                        turn(g, u)
                        weigh(g, u - 1)
                weigh(NG - 1, U - 1)
                pe.wait_ge(*taken(NG, -2))
                linear_work(NG - 1, "oT", TPG - 1, lin[0])
                pe.wait_ge(*taken(NG, -1))
                pe.wait_ge(act_took.sem, act_took.at(NG, 1))
                linear_work(NG - 1, "out", TPG - 1, lin[1])

            @block.scalar
            def _(act):
                act.wait_ge(zeroed, 1)

                def take(name, m, lin):
                    if name == "hT":
                        last = act.activation(hT[:].rearrange("p c n -> p (c n)"), lin[:, 0:D], ACT.Copy)
                    elif name in ("q", "k"):
                        last = act.activation(qk[:, m % 2, "qk".index(name), :], lin[:], ACT.Copy)
                    elif name == "v":
                        last = act.activation(V[:, where(m), :], lin[:], ACT.Copy)
                        if where(m) == TPG:
                            last = act.activation(V[:, 0, :], lin[:], ACT.Copy)
                    elif name == "QT":
                        last = act.activation(QT[:, m % 2, :, :].rearrange("p c n -> p (c n)"), lin[:], ACT.Copy)
                    elif name == "KT":
                        by_chunk = lin[:].rearrange("p (c n) -> p c n", c=4)
                        last = act.activation(KT[:, :, where(m) * P:(where(m) + 1) * P], by_chunk, ACT.Copy)
                        if where(m) == TPG:
                            last = act.activation(KT[:, :, 0:P], by_chunk, ACT.Copy)
                    else:
                        last = act.activation(oT[:].rearrange("p c n -> p (c n)"), lin[:], ACT.Copy)
                    last.then_inc(act_took.sem, 1)

                def linear_step(it, name, m):
                    if name != "out":
                        i = order.index((name, m))
                        act.wait_ge(lin_ready.sem, lin_ready.at(it, i + 1))
                        take(name, m, lin[i % 2])

                def softmax(it, u):
                    n, heads = heads_of(u)
                    act.wait_ge(max_ready.sem, max_ready.at(it, u + 1))
                    for j in range(2):
                        a = heads[j]
                        of_head = probs[:, u % 4, j * 2 * P:(j + 1) * 2 * P]
                        last = act.activation(of_head, of_head, ACT.Exp, bias=negmax[:, u % 4, j:j + 1], scale=-1.0,
                                              accum_out=sums[:, n % 2, a:a + 1])
                    last.then_inc(probs_ready.sem, 1)

                for i, (name, m) in enumerate(prologue):
                    act.wait_ge(lin_ready.sem, i + 1)
                    take(name, m, lin[i % 2])
                softmax(0, 0)
                softmax(0, 1)
                with act.Fori(0, NG) as g:
                    for u in range(U):
                        n, st = divmod(u, ST)
                        one, two = plan[st]
                        linear_step(g, one[0], n + one[1])
                        softmax(g, u + 2)
                        linear_step(g, two[0], n + two[1])
                act.wait_ge(lin_ready.sem, lin_ready.at(NG, 1))
                take("oT", TPG - 1, lin[0])

            @block.vector
            def _(dve):
                dve.sem_inc(probsT_ready.sem, probsT_ready.credit)
                dve.sem_inc(max_ready.sem, max_ready.credit)
                dve.sem_inc(dve_took.sem, dve_took.credit)
                dve.memset(sums[:], 1.0)
                dve.wait_ge(zeroed, 1)
                half = RD // 2
                every = lambda t: t.rearrange("p i (h d) -> p (i h) d", d=RD)

                def start_of_sequence(it):
                    dve.wait_ge(front_loaded, it * 48 + 48)
                    dve.tensor_scalar(h[0:1, 0, D // 2:], h[0:1, 0, D // 2:], keep.going[0:1, bass.ds(it, 1)], None, ALU.mult)
                    dve.drain()
                    dve.sem_inc(h_ready.sem, 1)

                def norms(it, m):
                    dve.wait_ge(squared.sem, squared.at(it, m + 1))
                    dve.tensor_reduce(ss[:], every(square[:]), AX.X, ALU.add)
                    dve.drain()
                    dve.tensor_scalar(ss[:], ss[:], 1e-24, None, ALU.max).then_inc(ss_ready.sem, 1)

                def divide(it, m):
                    dve.wait_ge(rn_ready.sem, rn_ready.at(it, m + 1))
                    both = every(qk[:, m % 2, :, :])
                    dve.tensor_tensor(both, both, bcast(rnorm[:], [P, 2 * RH, RD]), ALU.mult).then_inc(normed.sem, 1)

                def times_sin(it, gi, m):
                    by = lambda t, i, a, b: t[:, i, :].rearrange("p (h d) -> p h d", d=RD)[:, :, a:b]
                    table = lambda i, a, b: sin[:, i, bass.ds(gi * TPG + m, 1), a:b].to_broadcast([P, RH, b - a])
                    dve.drain()
                    for i in range(2):
                        dve.tensor_tensor(by(rot, i, 0, half), by(qk[:, m % 2], i, half, RD), table(i, 0, half), ALU.mult)
                        dve.tensor_tensor(by(rot, i, half, RD), by(qk[:, m % 2], i, 0, half), table(i, half, RD), ALU.mult)

                def rotate(it, m):
                    dve.drain()
                    dve.wait_ge(turned_a.sem, turned_a.at(it, m + 1))
                    dve.tensor_tensor(rot[:], rot[:], turn_a[:], ALU.add).then_inc(rot_ready.sem, 1)

                def maxima(it, u):
                    dve.wait_ge(scores_ready.sem, scores_ready.at(it, u + 1))
                    dve.wait_ge(turned_ready.sem, turned_ready.at(it, u - 3))
                    dve.sem_inc(masking, 1)
                    for j in range(2):
                        of_head = slice(j * 2 * P, (j + 1) * 2 * P)
                        last = dve.tensor_tensor_reduce(probs[:, u % 4, of_head], score[u % 4][:, of_head],
                                                        mask_now[:, int(u // ST % TPG > 0), :], -1.0, -NEG * 4, ALU.add, ALU.min,
                                                        negmax[:, u % 4, j:j + 1])
                    last.then_inc(max_ready.sem, 1)

                def take_turned(it, u):
                    dve.wait_ge(turned_ready.sem, turned_ready.at(it, u + 1))
                    dve.wait_ge(pv_done.sem, pv_done.at(it, u - 1))
                    dve.tensor_copy(probsT[:, u % 2, :], turned[:]).then_inc(probsT_ready.sem, 1)

                def normalise(it, n):
                    dve.wait_ge(pv_done.sem, pv_done.at(it, (n + 1) * ST))
                    dve.reciprocal(rsum[:], sums[:, n % 2, :])
                    dve.drain()
                    dve.tensor_tensor(attn[:].rearrange("p (h d) -> p h d", d=RD), po[:].rearrange("p (h d) -> p h d", d=RD),
                                      bcast(rsum[:], [P, RH, RD]), ALU.mult).then_inc(attn_ready.sem, 1)

                def take_out(g, n, lin):
                    dve.tensor_tensor(X2[:, g * TPG + (n + 1), :], lin[:, 0:D], XN[:, g * TPG + (n + 1), :], ALU.add)\
                       .then_inc(dve_took.sem, 1)

                dve.tensor_copy(mask_now[:], mask[:, 0:2, :])
                dve.drain()
                start_of_sequence(0)
                for m in range(2):
                    norms(0, m)
                    divide(0, m)
                    if m == 1:
                        dve.wait_ge(lin_ready.sem, prologue.index(("KT", 0)) + 1)
                    times_sin(0, 0, m)
                    if m == 0:
                        rotate(0, 0)
                maxima(0, 0)
                maxima(0, 1)

                def group(it, gi):
                    for u in range(U):
                        n, st = divmod(u, ST)
                        if st == 0:
                            rotate(it, n + 1)
                        maxima(it, u + 2)
                        take_turned(it, u)
                        if st == 0:
                            normalise(it, n - 1)
                        if u == 1:
                            start_of_sequence(it + 1)
                        if st == 1:
                            norms(it, n + 2)
                        if st == 2:
                            divide(it, n + 2)
                        if u == U - 4:
                            dve.tensor_copy(mask_now[:, 0, :], mask[:, bass.ds(it + 1, 1), :])
                            dve.drain()
                        if st == 3:
                            i = order.index(("out", n - 1))
                            dve.wait_ge(lin_ready.sem, lin_ready.at(it, i + 1))
                            take_out(it, n - 1, lin[i % 2])
                            times_sin(it, gi, n + 2)

                with dve.Fori(0, BATCH) as b:
                    with dve.Fori(0, GPB) as gi:
                        group(b * GPB + gi, gi)
                normalise(NG - 1, TPG - 1)
                dve.wait_ge(lin_ready.sem, lin_ready.at(NG, 2))
                take_out(NG - 1, TPG - 1, lin[1])
        s.clear_semaphores()


def combine(nc, io, keep):
    with ExitStack() as ctx:
        s = Space(nc, ctx, "comb")
        x1, s1 = s.sb("x1", [P, NG, TPG, D]), s.sb("s1", [P, NG, TPG, D])
        x_loaded = [s.sem(f"x_loaded{g}") for g in range(NG)]
        gate_ready, result_ready, stored = s.sem("gate_ready"), s.sem("result_ready"), s.sem("stored")
        by_group = lambda name: io[name].rearrange("(g n p) d -> g p n d", p=P, n=TPG)
        tiles = lambda g: keep.XN[:, g * TPG + 1:(g + 1) * TPG + 1, :]
        with nc.Block() as block:
            @block.sync
            def _(sp):
                for g in range(NG):
                    sp.dma_start(x1[:, g, :, :], by_group("x1")[g]).then_inc(x_loaded[g], 16)
                    sp.dma_start(s1[:, g, :, :], by_group("s1")[g]).then_inc(x_loaded[g], 16)
                for g in range(NG):
                    sp.wait_ge(result_ready, g + 1)
                    sp.dma_start(by_group("out")[g], x1[:, g, :, :]).then_inc(stored, 16)
                sp.wait_ge(stored, 16 * NG)

            @block.scalar
            def _(act):
                for g in range(NG):
                    act.activation(tiles(g), tiles(g), ACT.Silu).then_inc(gate_ready, 1)

            @block.vector
            def _(dve):
                for g in range(NG):
                    dve.wait_ge(gate_ready, g + 1)
                    dve.wait_ge(x_loaded[g], 32)
                    dve.tensor_tensor(s1[:, g, :, :], s1[:, g, :, :], tiles(g), ALU.mult)
                    dve.drain()
                    dve.tensor_tensor(x1[:, g, :, :], x1[:, g, :, :], s1[:, g, :, :], ALU.add).then_inc(result_ready, 1)


def build(nc, io):
    rows = [SLOT_TILES * P, D]
    for name, shape in (("rows_in", rows), ("rows_out", rows), ("x1", [NT * P, D]), ("s1", [NT * P, D])):
        io[name] = nc.dram_tensor("scratch_" + name, shape, F32).ap()
    with ExitStack() as ctx:
        keep = Keep(nc, ctx)
        normalise_input(nc, io, keep)
        window_attention(nc, io, keep, 0)
        with ExitStack() as sorted_rows:
            weights = ExpertWeights(nc, sorted_rows)
            route(nc, io, keep, weights)
            experts(nc, io, keep, weights)
            weights.clear_semaphores()
        finish_layer0(nc, io, keep)
        with ExitStack() as last_layers:
            rotary = RotaryWeights(nc, last_layers)
            with ExitStack() as mlp_stages:
                mlp = FeedForwardWeights(nc, mlp_stages, False)
                window_attention(nc, io, keep, 1, mlp)
                feed_forward(nc, io, keep, mlp, rotary, 0)
            ffn = FeedForwardWeights(nc, last_layers, True)
            with nc.Fori(0, 2) as layer:
                rotary_attention(nc, io, keep, rotary, ffn, layer)
                feed_forward(nc, io, keep, ffn, rotary, layer * -1 + 1)
        combine(nc, io, keep)


def layouts(inputs):
    def columns(v):
        c = -(-v.shape[0] // P)
        out = np.zeros((c * P,), v.dtype)
        out[:v.shape[0]] = v
        return out.reshape(c, P).T

    def heads_down(v):
        out = np.zeros((4, 32, v.shape[0] // 64), v.dtype)
        out[:, 0:HD, :] = v.reshape(-1, 4, HD).transpose(1, 2, 0)
        return out.reshape(P, -1)

    def heads_apart(w):
        out = np.zeros((P, KC, w.shape[1] // HD, 32), w.dtype)
        out[:, :, :, 0:HD] = w.reshape(KC, P, -1, HD).transpose(1, 0, 2, 3)
        return out

    x = {name: np.asarray(a) for name, a in inputs.items()}
    a = {"w_router": x["L0_ffn_Wr"].T.reshape(KC, P, EXPERTS).transpose(1, 0, 2),
         "win0_w_rq": heads_apart(x["L0_attn_rq_w"]), "win0_w_rk": heads_apart(x["L0_attn_rkv_w"][:, 0:LAT]),
         "win0_b_rq": heads_down(x["L0_attn_rq_b"]), "win0_b_rk": heads_down(x["L0_attn_rkv_b"][0:LAT]),
         "win0_b_rout": columns(x["L0_attn_rout_b"]),
         "win0_gate_columns": np.stack([np.tile(x[f"L0_attn_{w}"][:, 0], P // HD) for w in ("gl_w", "gr_w")], axis=1),
         "win1_gain": columns(x["L1_attn_ln1_g"]), "win1_offset": columns(x["L1_attn_ln1_b"]),
         "mlp_gain": columns(x["L1_attn_ln2_g"]), "mlp_offset": columns(x["L1_attn_ln2_b"]),
         "mlp_b1": columns(x["L1_attn_b1"])[:, None, :]}
    for layer, b in enumerate(("L0_attn_qkv_b", "L1_attn_b_qkv")):
        a[f"win{layer}_b_qk"] = columns(x[b][0:2 * D]).reshape(P, 2, KC)
    a["ffn_gain"] = np.stack([columns(v) for v in x["L1_ffn_ln_g"]])
    a["ffn_offset"] = np.stack([columns(v) for v in x["L1_ffn_ln_b"]])
    a["ffn_b1"] = np.stack([np.stack([columns(half) for half in np.split(v, 2)], axis=1) for v in x["L1_ffn_b1"]])
    a["ffn_b1"][:, :, 1, -1] = np.roll(a["ffn_b1"][:, :, 1, -1], P // 2, axis=1)
    return {name: np.ascontiguousarray(v) for name, v in a.items()}


def constants():
    bf16 = mybir.dt.np(BF16)
    c = {}
    q, k = np.arange(P)[:, None], np.arange(P)[None, :]
    c["ident"] = np.eye(P, dtype=np.float32)
    c["identb"] = np.eye(P).astype(bf16)
    c["earlier"] = (q < k).astype(bf16)
    first = np.arange(NG + 1) % GPB == 0
    c["going"] = np.broadcast_to(np.where(first, 0.0, 1.0), (P, NG + 1)).astype(np.float32)
    c["iota"] = np.broadcast_to(np.arange(SLOT_TILES), (P, SLOT_TILES)).astype(np.float32)

    def window(prev, cur, closed_at_start):
        m = np.zeros((P, NG + 1, 2 * P))
        for g in range(NG + 1):
            m[:, g, 0:P] = np.where(prev & ~(closed_at_start & first[g]), 0.0, NEG)
            m[:, g, P:] = np.where(cur, 0.0, NEG)
        return m.astype(bf16)

    c["mask0"] = window((k >= q) & (k >= 1), k < q, True)
    own_first = (q < P // 2) == (k < P // 2)
    c["mask1"] = np.where(~own_first | (k <= q), 0.0, NEG).astype(bf16)
    c["mask2"] = window(k >= q, k <= q, True)
    c["same_head"] = (q // HD == k // HD).astype(np.float32)
    c["parity"] = np.stack([(np.arange(P) // HD % 2 == odd).astype(np.float32) for odd in range(2)], axis=1)
    tile = np.arange(NT + 1) % (SEQ // P)
    chunk = tile[None, :, None] * LPT + (np.arange(P) // CHUNK)[:, None, None]
    c["lat_mask"] = np.where((np.arange(LAT) + LPT)[None, None, :] % LAT < chunk, 0.0, NEG).astype(bf16)
    valid = np.ones((P, NG + 1, 2), np.float32)
    valid[0, first, 0] = 0.0
    valid[0:CHUNK, first, 1] = 0.0
    c["valid"] = valid

    f = np.float32
    half = np.arange(0, RD, 2, dtype=f)
    inv_freq = f(1.0) / np.power(f(10000.0), half / f(RD))
    t = np.arange(SEQ, dtype=f)
    freqs = t[:, None] * inv_freq[None, :]
    base = (half + f(0.4 * RD)) / f(1.4 * RD)
    power = (t - f(SEQ // 2)) / f(P // 2)
    scale = np.power(base[None, :], power[:, None])
    cos, sin = np.cos(freqs), np.sin(freqs)
    two = lambda a, b: np.concatenate([a, b], axis=-1)
    tables = {"cos": (two(cos * scale, cos * scale) * f(8.0), two(cos / scale, cos / scale)),
              "sin": (two(-sin * scale, sin * scale) * f(8.0), two(-sin / scale, sin / scale))}
    for name, pair in tables.items():
        a = np.stack([x.reshape(SEQ // P, P, RD) for x in pair]).transpose(2, 0, 1, 3)
        c[name] = np.ascontiguousarray(np.concatenate([a, a[:, :, 0:2]], axis=2)).astype(f)
    return {f"const_{k}": np.ascontiguousarray(v) for k, v in c.items()}


_INS = ["L0_attn_x", "L0_attn_qkv_w", "L0_attn_qkv_b", "L0_attn_rq_w", "L0_attn_rq_b", "L0_attn_rkv_w", "L0_attn_rkv_b",
        "L0_attn_rout_w", "L0_attn_rout_b", "L0_attn_out_w", "L0_attn_out_b", "L0_attn_gl_w", "L0_attn_gr_w", "L0_ffn_Wr",
        "L0_ffn_W1", "L0_ffn_b1", "L0_ffn_Wo", "L0_ffn_bo", "L0_ffn_gamma", "L0_ffn_beta", "L1_attn_ln1_g",
        "L1_attn_ln1_b", "L1_attn_w_qkv", "L1_attn_b_qkv", "L1_attn_w_out", "L1_attn_b_out", "L1_attn_ln2_g",
        "L1_attn_ln2_b", "L1_attn_w1", "L1_attn_b1", "L1_attn_w2", "L1_attn_b2", "L1_ffn_wqkv", "L1_ffn_q_scale",
        "L1_ffn_k_scale", "L1_ffn_wo", "L1_ffn_ln_g", "L1_ffn_ln_b", "L1_ffn_w1", "L1_ffn_b1", "L1_ffn_w2", "L1_ffn_b2"]


def kernel(**inputs):
    import concourse.bacc as bacc
    from concourse.bass_utils import run_bass_kernel_spmd

    nc = bacc.Bacc("TRN2", target_bir_lowering=False, num_devices=1)
    arrays = {name: np.ascontiguousarray(inputs[name]) for name in _INS}
    arrays.update(layouts(inputs))
    arrays.update(constants())
    io = {name: nc.dram_tensor("in_" + name, a.shape, mybir.dt.from_np(a.dtype), kind="ExternalInput").ap()
          for name, a in arrays.items()}
    out = nc.dram_tensor("out", (BATCH, SEQ, D), F32, kind="ExternalOutput").ap()
    io["out"] = out.rearrange("b n d -> (b n) d")
    build(nc, io)
    r = run_bass_kernel_spmd(nc, [{"in_" + name: a for name, a in arrays.items()}], core_ids=[0])
    return r.results[0]["out"]
```
